# Optimizing a Trainium2 kernel written in Bass

```python
import numpy as np
import jax
import jax.numpy as jnp

def _softmax(x, axis=-1):
    return jax.nn.softmax(x, axis=axis)

def _gelu(x):
    return jax.nn.gelu(x, approximate=True)

def _silu(x):
    return jax.nn.silu(x)

def _sigmoid(x):
    return jax.nn.sigmoid(x)

def _layernorm(x, axis=-1, eps=1e-05):
    m = jnp.mean(x, axis=axis, keepdims=True)
    v = jnp.var(x, axis=axis, keepdims=True)
    return (x - m) / jnp.sqrt(v + eps)

def _scatter_add(tgt, idx, src, axis=0):
    return tgt.at[idx].add(src)

def _segment_sum(src, seg, n):
    return jax.ops.segment_sum(src, seg, n)
kernel_name = 'mk_gnn_resnorm_d2_gnn_r64_154571'

def setup_inputs(seed: int=0):
    np.random.seed(seed)
    _w = jnp.asarray

    def _rec_inputs():
        import jax
        import jax.numpy as jnp
        _gk = jax.random.key(seed)
        x = -8.776e-05 + 1 * jax.random.normal(jax.random.fold_in(_gk, 1), (10000, 512), jnp.float32)
        src = jax.random.randint(jax.random.fold_in(_gk, 2), (2500,), 0, 10000, jnp.int32)
        dst = jnp.minimum((10000 * jax.random.uniform(jax.random.fold_in(_gk, 3), (2500,)) ** 2.0).astype(jnp.int32), 9999)
        _o = jnp.argsort(dst, stable=True)
        src = src[_o]
        dst = dst[_o]
        edge_attr_8 = jax.random.uniform(jax.random.fold_in(_gk, 12), (2500, 8), jnp.float32, 0.0, 0.999999)
        edge_weight = jax.random.uniform(jax.random.fold_in(_gk, 14), (2500,), jnp.float32, 0.0, 0.0999999)
        node_vec = jax.random.uniform(jax.random.fold_in(_gk, 15), (10000,), jnp.float32, 0.0, 0.999988)
        return (x, src, dst, edge_attr_8, edge_weight, node_vec)
    x, src, dst, edge_attr_8, edge_weight, node_vec = _rec_inputs()

    def _L0_gnn_setup():
        import jax, jax.numpy as jnp
        import numpy as np
        N, E, D, H = (10000, 2500, 512, 8)
        HD = D // H
        SCALE = HD ** (-0.5)

        def _layernorm(x, g, b):
            mu = jnp.mean(x, axis=-1, keepdims=True)
            var = jnp.mean(jnp.square(x - mu), axis=-1, keepdims=True)
            return (x - mu) * jax.lax.rsqrt(var + 1e-05) * g + b
        key = jax.random.key(seed)
        ks = jax.random.split(key, 12)
        s = D ** (-0.5)
        return {'x': jax.random.normal(ks[0], (N, D), jnp.float32), 'edge_index': jax.random.randint(ks[1], (2, E), 0, N, jnp.int64), 'edge_weights': jax.random.uniform(ks[2], (E, H), jnp.float32), 'ln_g': jnp.ones((D,), jnp.float32), 'ln_b': jnp.zeros((D,), jnp.float32), 'Wq': jax.random.normal(ks[3], (D, D), jnp.float32) * s, 'bq': jnp.zeros((D,), jnp.float32), 'Wk': jax.random.normal(ks[4], (D, D), jnp.float32) * s, 'bk': jnp.zeros((D,), jnp.float32), 'Wv': jax.random.normal(ks[5], (D, D), jnp.float32) * s, 'bv': jnp.zeros((D,), jnp.float32), 'W1': jax.random.normal(ks[6], (D, D), jnp.float32) * s, 'b1': jnp.zeros((D,), jnp.float32), 'W2': jax.random.normal(ks[7], (D, D), jnp.float32) * s, 'b2': jnp.zeros((D,), jnp.float32)}
    _L0_gnn_all = _L0_gnn_setup()
    _L0_gnn_in = {k: v for k, v in _L0_gnn_all.items() if k in ('ln_g', 'ln_b', 'Wq', 'bq', 'Wk', 'bk', 'Wv', 'bv', 'W1', 'b1', 'W2', 'b2')}
    del _L0_gnn_all

    def _L1_gnn_setup():
        import jax, jax.numpy as jnp
        import numpy as np
        N_NODES = 50000
        N_EDGES = 6250
        DIM = 512

        def _graph_conv(x, W0, W1, b, diag, edge_vals, edge_src, edge_dst):
            n = x.shape[0]
            self_term = diag[:, None] * (x @ W0)
            msgs = edge_vals[:, None] * (x @ W1)[edge_src]
            neigh = jax.ops.segment_sum(msgs, edge_dst, num_segments=n)
            return jax.nn.relu(self_term + neigh + b)
        key = jax.random.key(seed)
        ks = jax.random.split(key, 10)
        scale = 1.0 / np.sqrt(DIM)
        return {'x': jax.random.normal(ks[0], (N_NODES, DIM), jnp.float32), 'W0_1': jax.random.normal(ks[1], (DIM, DIM), jnp.float32) * scale, 'W1_1': jax.random.normal(ks[2], (DIM, DIM), jnp.float32) * scale, 'b1': jnp.zeros((DIM,), jnp.float32), 'W0_2': jax.random.normal(ks[3], (DIM, DIM), jnp.float32) * scale, 'W1_2': jax.random.normal(ks[4], (DIM, DIM), jnp.float32) * scale, 'b2': jnp.zeros((DIM,), jnp.float32), 'diag': jax.random.uniform(ks[5], (N_NODES,), jnp.float32), 'edge_vals': jax.random.uniform(ks[6], (N_EDGES,), jnp.float32) * 0.1, 'edge_src': jax.random.randint(ks[7], (N_EDGES,), 0, N_NODES, jnp.int32), 'edge_dst': jax.random.randint(ks[8], (N_EDGES,), 0, N_NODES, jnp.int32)}
    _L1_gnn_all = _L1_gnn_setup()
    _L1_gnn_in = {k: v for k, v in _L1_gnn_all.items() if k in ('W0_1', 'W1_1', 'b1', 'W0_2', 'W1_2', 'b2')}
    del _L1_gnn_all
    return {'x': x, 'src': src, 'dst': dst, 'edge_attr_8': edge_attr_8, 'edge_weight': edge_weight, 'node_vec': node_vec, 'L0_gnn_ln_g': _L0_gnn_in['ln_g'], 'L0_gnn_ln_b': _L0_gnn_in['ln_b'], 'L0_gnn_Wq': _L0_gnn_in['Wq'], 'L0_gnn_bq': _L0_gnn_in['bq'], 'L0_gnn_Wk': _L0_gnn_in['Wk'], 'L0_gnn_bk': _L0_gnn_in['bk'], 'L0_gnn_Wv': _L0_gnn_in['Wv'], 'L0_gnn_bv': _L0_gnn_in['bv'], 'L0_gnn_W1': _L0_gnn_in['W1'], 'L0_gnn_b1': _L0_gnn_in['b1'], 'L0_gnn_W2': _L0_gnn_in['W2'], 'L0_gnn_b2': _L0_gnn_in['b2'], 'L1_gnn_W0_1': _L1_gnn_in['W0_1'], 'L1_gnn_W1_1': _L1_gnn_in['W1_1'], 'L1_gnn_b1': _L1_gnn_in['b1'], 'L1_gnn_W0_2': _L1_gnn_in['W0_2'], 'L1_gnn_W1_2': _L1_gnn_in['W1_2'], 'L1_gnn_b2': _L1_gnn_in['b2']}

def reference(x, src, dst, edge_attr_8, edge_weight, node_vec, L0_gnn_ln_g, L0_gnn_ln_b, L0_gnn_Wq, L0_gnn_bq, L0_gnn_Wk, L0_gnn_bk, L0_gnn_Wv, L0_gnn_bv, L0_gnn_W1, L0_gnn_b1, L0_gnn_W2, L0_gnn_b2, L1_gnn_W0_1, L1_gnn_W1_1, L1_gnn_b1, L1_gnn_W0_2, L1_gnn_W1_2, L1_gnn_b2):
    import jax
    import jax.numpy as jnp

    def _L0_gnn_ref(x, edge_index, edge_weights, ln_g, ln_b, Wq, bq, Wk, bk, Wv, bv, W1, b1, W2, b2):
        import jax, jax.numpy as jnp
        import numpy as np
        N, E, D, H = (10000, 2500, 512, 8)
        HD = D // H
        SCALE = HD ** (-0.5)

        def _layernorm(x, g, b):
            mu = jnp.mean(x, axis=-1, keepdims=True)
            var = jnp.mean(jnp.square(x - mu), axis=-1, keepdims=True)
            return (x - mu) * jax.lax.rsqrt(var + 1e-05) * g + b
        origin, destination = (edge_index[0], edge_index[1])
        x_norm = _layernorm(x, ln_g, ln_b)
        q = (x_norm @ Wq + bq).reshape(N, H, HD)
        k = (x_norm @ Wk + bk).reshape(N, H, HD)
        v = (x_norm @ Wv + bv).reshape(N, H, HD)
        scores = jnp.einsum('ehd,ehd->eh', q[origin], k[destination]) * SCALE
        ws = scores * edge_weights
        seg_max = jax.ops.segment_max(ws, origin, num_segments=N)
        seg_max = jnp.where(jnp.isfinite(seg_max), seg_max, 0.0)
        e = jnp.exp(ws - seg_max[origin])
        denom = jax.ops.segment_sum(e, origin, num_segments=N)
        att = e / (denom[origin] + 1e-16)
        weighted_values = att[:, :, None] * v[destination]
        values = jax.ops.segment_sum(weighted_values, origin, num_segments=N)
        values = values.reshape(N, D)
        values = (values @ W1 + b1) @ W2 + b2
        return x + values

    def _L1_gnn_ref(x, W0_1, W1_1, b1, W0_2, W1_2, b2, diag, edge_vals, edge_src, edge_dst):
        import jax, jax.numpy as jnp
        import numpy as np
        N_NODES = 50000
        N_EDGES = 6250
        DIM = 512

        def _graph_conv(x, W0, W1, b, diag, edge_vals, edge_src, edge_dst):
            n = x.shape[0]
            self_term = diag[:, None] * (x @ W0)
            msgs = edge_vals[:, None] * (x @ W1)[edge_src]
            neigh = jax.ops.segment_sum(msgs, edge_dst, num_segments=n)
            return jax.nn.relu(self_term + neigh + b)
        h = _graph_conv(x, W0_1, W1_1, b1, diag, edge_vals, edge_src, edge_dst)
        h = _graph_conv(h, W0_2, W1_2, b2, diag, edge_vals, edge_src, edge_dst)
        return (h + x) * 0.5
    edge_index = jnp.stack([src, dst])
    x = _layernorm(x + _L0_gnn_ref(x, edge_index, edge_attr_8, L0_gnn_ln_g, L0_gnn_ln_b, L0_gnn_Wq, L0_gnn_bq, L0_gnn_Wk, L0_gnn_bk, L0_gnn_Wv, L0_gnn_bv, L0_gnn_W1, L0_gnn_b1, L0_gnn_W2, L0_gnn_b2), axis=-1)
    x = _layernorm(x + _L1_gnn_ref(x, L1_gnn_W0_1, L1_gnn_W1_1, L1_gnn_b1, L1_gnn_W0_2, L1_gnn_W1_2, L1_gnn_b2, node_vec, edge_weight, src, dst), axis=-1)
    return x

_drawn_inputs = setup_inputs


def setup_inputs(seed=0):
    import zlib

    import numpy as np

    out = dict(_drawn_inputs(seed))
    spreads = {'L0_gnn_ln_g': (1.0, 0.2),
     'L0_gnn_ln_b': (0.0, 0.42),
     'L0_gnn_bq': (0.0, 2.0),
     'L0_gnn_bk': (0.0, 2.0),
     'L0_gnn_bv': (0.0, 0.381),
     'L0_gnn_b1': (0.0, 0.1),
     'L0_gnn_b2': (0.0, 0.1),
     'L1_gnn_b1': (0.0, 0.8),
     'L1_gnn_b2': (0.0, 0.356)}
    factors = {'edge_attr_8': 5.978,
     'edge_weight': 8.0,
     'L0_gnn_Wq': 2.804,
     'L0_gnn_Wk': 2.807,
     'L1_gnn_W1_1': 8.0,
     'L1_gnn_W1_2': 8.0}
    for name, (base, spread) in spreads.items():
        noise = np.random.default_rng([zlib.crc32(name.encode()), seed]).standard_normal(out[name].shape)
        drawn = base * np.exp(spread * noise) if base else spread * noise
        out[name] = jnp.asarray(drawn.astype(out[name].dtype))
    for name, factor in factors.items():
        out[name] = (out[name] * factor).astype(out[name].dtype)
    return out
```

```python
from contextlib import ExitStack

import concourse.bass as bass
from concourse import mybir

ALU = mybir.AluOpType
ACT = mybir.ActivationFunctionType
AX = mybir.AxisListType
F32 = mybir.dt.float32
F32R = mybir.dt.float32r
BF16 = mybir.dt.bfloat16
I32 = mybir.dt.int32

P = 128
D = 512
KC = D // P
H = 8
HD = D // H
T = 125
EPS = 1e-5
FAR = 1000000
GAP = -3.0e38

WS = D
SRC, DST, EW, RANKB, DIAG = WS + H, WS + H + 1, WS + H + 2, WS + H + 3, WS + H + 4
ROW = DIAG + 4
FIELDS = ROW - WS


class Tile:

    def __init__(self, turn, c, unroll, count):
        self.turn, self.c, self.unroll, self.count = turn, c, unroll, count
        self.t = c if turn is None else turn * unroll + c

    def later(self, k):
        return Tile(self.turn, self.c + k, self.unroll, self.count)

    def buf(self, m=2):
        return self.c % m

    def use(self, m=2):
        return self.c // m if self.turn is None else self.turn * (self.unroll // m) + self.c // m

    def early(self, k):
        return self.turn is None and self.c < k

    def exists(self):
        return self.turn is not None or 0 <= self.c < self.count


def tiles(eng, step, count, unroll=2, before=0, after=0):
    for c in range(-before, unroll):
        step(Tile(None, c, unroll, count))
    with eng.Fori(1, count // unroll - 1) as turn:
        for c in range(unroll):
            step(Tile(turn, c, unroll, count))
    for c in range(count - unroll, count + after):
        step(Tile(None, c, unroll, count))


def at(part, a):
    if a.exists():
        part(a)


def alone(eng):
    eng.nop(nofuse=True)


def build(nc, x, src, dst, attr, ew, node_vec, ln_g, ln_b, wq, bq, wk, bk, wv, bv, w1, b1, w2, b2,
          w01, w11, gb1, w02, w12g, gb2, out):
    N = x.shape[0]
    E = src.shape[0]
    NT, ET = N // T, E // T
    SCALE = HD ** -0.5
    CENTRE = N * E // 2

    def dram(name, shape, dt):
        return nc.dram_tensor(name, shape, dt, kind="Internal").ap()

    by_src = dram("by_src", (E, ROW), F32)
    x_by_src = dram("x_by_src", (E, D), F32)
    by_dst = dram("by_dst", (E + 1, 4), F32)
    x_new = dram("x_new", (E, D), F32)
    x1_rows = dram("x1_rows", (E, D), F32)
    h1_rows = dram("h1_rows", (E, D), F32)
    neigh = dram("neigh", (E, 2 * D), F32)
    neigh1 = dram("neigh1", (E, D), F32)
    slot_src = dram("slot_src", (N, 1), I32)
    slot_dst = dram("slot_dst", (N, 1), I32)
    src_col = src.rearrange("(p t) -> p t", p=T)
    dst_col = dst.rearrange("(p t) -> p t", p=T)
    ew_col = ew.rearrange("(p t) -> p t", p=T)
    vec_rows = node_vec.rearrange("(n o) -> n o", o=1)

    whole = ExitStack()

    def holder(stack):
        def sb(name, shape, dt=F32):
            return stack.enter_context(nc.sbuf_tensor(name, shape, dt))

        def ps(name, shape=(P, D)):
            return stack.enter_context(nc.psum_tensor(name, list(shape), F32))
        return sb, ps

    part_sems = []

    def sem(name):
        part_sems.append(nc.alloc_semaphore(name))
        return part_sems[-1]

    def end_part():
        nc.clear_and_free_semaphores(part_sems)
        nc.all_engine_barrier()
        part_sems.clear()

    def sems(name, n=2):
        return [sem(f"{name}_buf{i}") for i in range(n)]

    def weight_rows(w):
        return w.rearrange("(k p) n -> p k n", p=P)

    def columns(v):
        return v.rearrange("(k p) -> p k", p=P)

    def row_for_all(v, n=T):
        return v.rearrange("(o d) -> o d", o=1).to_broadcast([n, v.shape[0]])

    def chunks(a):
        return a.rearrange("p (k c) -> p k c", k=KC)[:, :, 0:T]

    def transpose_tile(bank, rows, ident):
        for k in range(KC):
            last = nc.tensor.transpose(bank[:, P * k:P * k + T], rows[:, P * k:P * (k + 1)], ident[0:T, 0:T])
        return last

    def product(bank, hi, lo, w):
        w_hi, w_lo = w
        n = 0
        for k in range(KC):
            for a, b in ((hi, w_hi), (hi, w_lo), (lo, w_hi)):
                last = nc.tensor.matmul(bank[0:T, :], a[:, k, 0:T], b[:, k, :], start=(n == 0), stop=(n == 3 * KC - 1))
                n += 1
        return last

    whole.enter_context(nc.allow_non_contiguous_dma(reason="small columns"))
    with whole:
        sb, _ = holder(whole)
        ident = sb("ident", [P, P])
        eps = sb("eps", [P, 3])
        conv2_w = [sb(f"w_slot0_{p}", [P, KC, D], F32R) for p in ("hi", "lo")]
        dense2_w = [sb(f"w_slot1_{p}", [P, KC, D], F32R) for p in ("hi", "lo")]
        q_w, k_w = conv2_w, dense2_w
        attn_w = [sb(f"w_attn_{p}", [P, KC, D], F32R) for p in ("hi", "lo")]
        dense1_w = [sb(f"w_dense1_{p}", [P, KC, D], F32R) for p in ("hi", "lo")]
        conv1_w = [sb(f"w_conv1_{p}", [P, KC, D], F32R) for p in ("hi", "lo")]
        half_c = sb("half_c", [T, D])
        neigh_b = sb("neigh_b", [T, 2 * D])

        with ExitStack() as ph:
            sb, ps = holder(ph)
            v_w = [sb(f"w_v_{p}", [P, KC, D], F32R) for p in ("hi", "lo")]
            q_bias, k_bias, v_bias = (sb(f"{n}_bias", [T, D]) for n in "qkv")
            edge_i = sb("edge_i", [T, 2, ET], I32)
            edge_f = sb("edge_f", [T, 3, ET])
            attr_s = sb("attr_s", [T, ET, H])
            key_row = sb("key_row", [T, 2, E])
            key_col = sb("key_col", [T, 2, ET])
            sums = sb("sums", [T, 2, ET])

            with ExitStack() as ph0:
                sb0, ps0 = holder(ph0)
                stage = [sb0(f"stage{i}", [P, KC, D]) for i in range(2)]
                gain = sb0("gain", [P, KC])
                shift = sb0("shift", [P, KC])
                node_row = sb0("node_row", [T, E], I32)
                number = sb0("number", [T, E], I32)
                number_c = sb0("number_c", [T, ET], I32)
                far = sb0("far", [T, NT], I32)
                sentinel = sb0("sentinel", [1, 4])
                bias_ps = [ps0(f"bias_ps{i}") for i in range(2)]
                w_in = sems("w_in")
                small_in, rows_in = sem("small_in"), sem("rows_in")
                bias_in = sem("bias_in")
                made, ident0, ident1 = sem("made"), sem("ident0"), sem("ident1")
                w_high, w_done, bias_mm, bias_done = sem("w_high"), sem("w_done"), sem("bias_mm"), sem("bias_done")
                keys_done, far_out = sem("keys_done"), sem("far_out")
                block = nc.Block()
                block = ph0.enter_context(block)

                @block.sync
                def _(sp):
                    sp.dma_start(gain[:, :], columns(ln_g)).then_inc(small_in, 16)
                    sp.dma_start(shift[:, :], columns(ln_b)).then_inc(small_in, 16)
                    for i, w in enumerate((wq, wk, wv)):
                        if i >= 2:
                            sp.wait_ge(w_done, i - 1)
                            sp.wait_ge(bias_mm, i - 1)
                        sp.dma_start(stage[i % 2][:, :, :], weight_rows(w)).then_inc(w_in[i % 2], 16)
                    sp.wait_ge(made, 4)
                    sp.dma_start(slot_src.rearrange("(p t) o -> p (t o)", p=T), far[:, :]).then_inc(far_out, 16)
                    sp.dma_start(slot_dst.rearrange("(p t) o -> p (t o)", p=T), far[:, :]).then_inc(far_out, 16)
                    sp.dma_start(by_dst[E:E + 1, :], sentinel[:, :]).then_inc(far_out, 16)
                    sp.wait_ge(far_out, 48)

                @block.scalar
                def _(act):
                    act.dma_start(node_row[:, :], row_for_all(src)).then_inc(rows_in, 16)
                    act.dma_start(edge_i[:, 0, :], src_col).then_inc(small_in, 16)
                    act.dma_start(edge_i[:, 1, :], dst_col).then_inc(small_in, 16)
                    act.dma_start(edge_f[:, 2, :], ew_col).then_inc(small_in, 16)
                    act.dma_start(attr_s[:, :, :], attr.rearrange("(p t) h -> p t h", p=T)).then_inc(small_in, 16)
                    for b, v in ((q_bias, bq), (k_bias, bk), (v_bias, bv)):
                        act.dma_start(b[:, :], row_for_all(v)).then_inc(bias_in, 16)
                    act.wait_ge(keys_done, 1)
                    act.dma_start(node_row[:, :], row_for_all(dst)).then_inc(rows_in, 16)
                    act.wait_ge(small_in, 96)
                    for i, w in enumerate((q_w, k_w, v_w)):
                        act.wait_ge(w_in[i % 2], 16 * (i // 2 + 1))
                        for k in range(KC):
                            last = nc.scalar.activation(w[0][:, k, :], stage[i % 2][:, k, :], ACT.Copy, scale=gain[:, k:k + 1])
                        last.then_inc(w_high, 1)

                @block.gpsimd
                def _(pool):
                    nc.gpsimd.memset(ident[:, :], 0.0).then_inc(ident0, 1)
                    nc.gpsimd.iota(number[:, :], [[1, E]], base=-CENTRE, channel_multiplier=0).then_inc(made, 1)
                    nc.gpsimd.iota(number_c[:, :], [[1, ET]], base=-CENTRE, channel_multiplier=ET).then_inc(made, 1)
                    nc.gpsimd.iota(far[:, :], [[0, NT]], base=FAR, channel_multiplier=0).then_inc(made, 1)
                    nc.gpsimd.memset(sentinel[:, :], -1.0).then_inc(made, 1)
                    pool.wait_ge(ident0, 1)
                    nc.gpsimd.affine_select(out=ident[:, :], in_=ident[:, :], compare_op=ALU.not_equal, fill=1.0,
                                            base=0, pattern=[[-1, P]], channel_multiplier=1).then_inc(ident1, 1)

                @block.vector
                def _(dve):
                    for i, v in enumerate((EPS, EPS / 4, EPS / 2.25)):
                        nc.vector.memset(eps[:, i:i + 1], v)
                    dve.wait_ge(made, 3)
                    dve.wait_ge(rows_in, 16)
                    nc.vector.scalar_tensor_tensor(key_row[:, 0, :], node_row[:, :], float(E), number[:, :],
                                                   ALU.mult, ALU.add).then_inc(keys_done, 1)
                    dve.wait_ge(small_in, 96)
                    for j in range(2):
                        nc.vector.scalar_tensor_tensor(key_col[:, j, :], edge_i[:, j, :], float(E), number_c[:, :],
                                                       ALU.mult, ALU.add)
                        nc.vector.tensor_copy(edge_f[:, j, :], edge_i[:, j, :])
                    for i, w in enumerate((q_w, k_w, v_w)):
                        dve.wait_ge(w_high, i + 1)
                        for k in range(KC):
                            last = nc.vector.scalar_tensor_tensor(
                                w[1][:, k, :], stage[i % 2][:, k, :], gain[:, k:k + 1],
                                w[0][:, k, :].bitcast(F32), ALU.mult, ALU.subtract)
                        last.then_inc(w_done, 1)
                        if i == 0:
                            dve.wait_ge(rows_in, 32)
                            nc.vector.scalar_tensor_tensor(key_row[:, 1, :], node_row[:, :], float(E), number[:, :],
                                                           ALU.mult, ALU.add)
                        dve.wait_ge(bias_mm, i + 1)
                        if i == 0:
                            dve.wait_ge(bias_in, 48)
                        b = (q_bias, k_bias, v_bias)[i]
                        nc.vector.tensor_tensor(b[:, :], bias_ps[i % 2][0:T, :], b[:, :], ALU.add).then_inc(bias_done, 1)

                @block.tensor
                def _(pe):
                    pe.wait_ge(small_in, 96)
                    for i in range(3):
                        pe.wait_ge(w_in[i % 2], 16 * (i // 2 + 1))
                        if i >= 2:
                            pe.wait_ge(bias_done, i - 1)
                        for k in range(KC):
                            last = nc.tensor.matmul(bias_ps[i % 2][0:T, :], shift[:, k:k + 1].to_broadcast([P, T]),
                                                    stage[i % 2][:, k, :], start=(k == 0), stop=(k == KC - 1))
                        last.then_inc(bias_mm, 1)

            end_part()
            with ExitStack() as ph1:
                sb1, ps1 = holder(ph1)
                xg = [[sb1(f"xg{j}_{b}", [T, D]) for b in range(2)] for j in range(2)]
                dg = [sb1(f"dg{b}", [T, 1]) for b in range(2)]
                row = [sb1(f"row{b}", [T, ROW]) for b in range(2)]
                idx = [sb1(f"idx{b}", [T, 4], I32) for b in range(2)]
                st = [sb1(f"st{b}", [T, 2, 6]) for b in range(2)]
                mv = [sb1(f"mv{b}", [T, 2, 2]) for b in range(2)]
                rs = [sb1(f"rs{b}", [T, 2, 2]) for b in range(2)]
                xh = [[sb1(f"xh{j}_{b}", [T, D]) for b in range(2)] for j in range(2)]
                hi = [[sb1(f"p_hi{j}_{b}", [P, KC, P], F32R) for b in range(2)] for j in range(2)]
                lo = [[sb1(f"p_lo{j}_{b}", [P, KC, P], F32R) for b in range(2)] for j in range(2)]
                qs, ks, qk = sb1("qs", [T, D]), sb1("ks", [T, D]), sb1("qk", [T, D])
                score = sb1("score", [T, H])
                waste = sb1("waste", [T, 2, E], BF16)
                tp = [ps1(f"p_tp{j}") for j in range(2)]
                qkv = [[ps1(f"p_{n}{b}") for b in range(2)] for n in "qkv"]
                got_x = [sems("got_xs"), sems("got_xd")]
                got_diag, sent_x, sent_row = sems("got_diag"), sems("sent_x"), sems("sent_row")
                p_idx, p_rank_idx = sem("p_idx"), sem("p_rank_idx")
                p_stats, p_aggr, p_dev, p_rec, p_xh = sem("p_stats"), sem("p_aggr"), sem("p_dev"), sem("p_rec"), sem("p_xh")
                p_t, p_hi, p_lo = sem("p_t"), sem("p_hi"), sem("p_lo")
                p_mm = [sem(f"p_mm_{n}") for n in "qkv"]
                p_q, p_k, p_v, p_qk, p_sc, p_row = sem("p_q"), sem("p_k"), sem("p_v"), sem("p_qk"), sem("p_sc"), sem("p_row")
                p_sums, p_rowf = sem("p_sums"), sem("p_rowf")
                block = ph1.enter_context(nc.Block())

                @block.gpsimd
                def _(pool):
                    bound = {"N": pool.to_reg(N - 1), "E": pool.to_reg(E - 1)}
                    def fetch(a):
                        b, n = a.buf(), a.use()
                        if not a.early(2):
                            pool.wait_ge(sent_x[b], 16 * n)
                            pool.wait_ge(p_xh, a.t - 1)
                            pool.wait_ge(got_diag[b], 16 * n)
                            pool.wait_ge(p_rowf, a.t - 1)
                            pool.wait_ge(got_x[0][b], 16 * n)
                            pool.wait_ge(got_x[1][b], 16 * n)
                        nc.gpsimd.tensor_copy(idx[b][:, 0:2], edge_i[:, :, bass.ds(a.t, 1)].rearrange("p j o -> p (j o)"))\
                            .then_inc(p_idx, 1)
                        pool.wait_ge(p_idx, a.t + 1)
                        for j in range(2):
                            alone(pool)
                            pool.indirect_dma_start(xg[j][b][:, :], None, x, bass.IndirectOffsetOnAxis(ap=idx[b][:, j:j + 1], axis=0),
                                                    bounds_check=bound["N"], oob_is_err=False).then_inc(got_x[j][b], 16)
                        alone(pool)
                        pool.indirect_dma_start(dg[b][:, :], None, vec_rows, bass.IndirectOffsetOnAxis(ap=idx[b][:, 0:1], axis=0),
                                                bounds_check=bound["N"], oob_is_err=False).then_inc(got_diag[b], 16)

                    def send(a):
                        b = a.buf()
                        pool.wait_ge(p_rank_idx, a.t + 1)
                        pool.wait_ge(got_x[0][b], 16 * a.use() + 16)
                        alone(pool)
                        pool.indirect_dma_start(x_by_src, bass.IndirectOffsetOnAxis(ap=idx[b][:, 2:3], axis=0), xg[0][b][:, :], None,
                                                bounds_check=bound["E"], oob_is_err=False).then_inc(sent_x[b], 16)
                        pool.wait_ge(p_k, a.t + 1)
                        if not a.early(1):
                            pool.wait_ge(p_sc, a.t)
                        nc.gpsimd.tensor_tensor(qk[:, :], qs[:, :], ks[:, :], ALU.mult).then_inc(p_qk, 1)
                        if a.later(2).exists():
                            fetch(a.later(2))
                        pool.wait_ge(p_row, a.t + 1)
                        alone(pool)
                        pool.indirect_dma_start(by_src, bass.IndirectOffsetOnAxis(ap=idx[b][:, 2:3], axis=0), row[b][:, :], None,
                                                bounds_check=bound["E"], oob_is_err=False).then_inc(sent_row[b], 16)

                    fetch(Tile(None, 0, 2, ET))
                    fetch(Tile(None, 1, 2, ET))

                    def step(a):
                        send(a)
                    tiles(pool, step, ET)
                    for b in range(2):
                        pool.wait_ge(sent_row[b], 16 * (ET // 2))
                        pool.wait_ge(sent_x[b], 16 * (ET // 2))

                @block.scalar
                def _(act):
                    def high(a):
                        b = a.buf()
                        act.wait_ge(p_t, a.t + 1)
                        if not a.early(2):
                            act.wait_ge(p_mm[2], a.t - 1)
                        nc.scalar.activation(hi[0][b][:, :, 0:T], chunks(tp[0][:, :]), ACT.Copy)
                        nc.scalar.activation(hi[1][b][:, :, 0:T], chunks(tp[1][:, :]), ACT.Copy).then_inc(p_hi, 1)

                    def deviation(a):
                        b = a.buf()
                        act.wait_ge(p_aggr, a.t + 1)
                        if not a.early(2):
                            act.wait_ge(p_rec, a.t - 1)
                        nc.scalar.activation(rs[b][:, :, 0:1], mv[b][:, :, 1:2], ACT.Sqrt, bias=eps[0:T, 0:1]).then_inc(p_dev, 1)

                    def rank(a):
                        if not a.early(1):
                            act.wait_ge(p_sums, 2 * a.t)
                        for j in range(2):
                            nc.scalar.activation(waste[:, j, :], key_row[:, j, :], ACT.Sign, scale=-1.0,
                                                 bias=key_col[:, j, bass.ds(a.t, 1)],
                                                 accum_out=sums[:, j, bass.ds(a.t, 1)]).then_inc(p_sums, 1)

                    deviation(Tile(None, 0, 2, ET))
                    deviation(Tile(None, 1, 2, ET))
                    high(Tile(None, 0, 2, ET))

                    def step(a):
                        if a.later(1).exists():
                            high(a.later(1))
                        rank(a)
                        if a.later(2).exists():
                            deviation(a.later(2))
                    tiles(act, step, ET)

                @block.vector
                def _(dve):
                    def norm(a):
                        b, n = a.buf(), a.use()
                        for j in range(2):
                            dve.wait_ge(got_x[j][b], 16 * n + 16)
                            nc.vector.bn_stats(st[b][:, j, :], xg[j][b][:, :]).then_inc(p_stats, 1)
                        for j in range(2):
                            dve.wait_ge(p_stats, 2 * a.t + 1 + j)
                            alone(dve)
                            last = nc.vector.bn_aggr(mv[b][:, j, :], st[b][:, j, :])
                        last.then_inc(p_aggr, 1)
                        dve.wait_ge(p_dev, a.t + 1)
                        nc.vector.reciprocal(rs[b][:, :, 1:2], rs[b][:, :, 0:1]).then_inc(p_rec, 1)
                        dve.wait_ge(p_rec, a.t + 1)
                        if not a.early(2):
                            dve.wait_ge(p_t, a.t - 1)
                        for j in range(2):
                            last = nc.vector.tensor_scalar(xh[j][b][:, :], xg[j][b][:, :], mv[b][:, j, 0:1], rs[b][:, j, 1:2],
                                                           ALU.subtract, ALU.mult)
                        last.then_inc(p_xh, 1)

                    def low(a):
                        b = a.buf()
                        dve.wait_ge(p_hi, a.t + 1)
                        for j in range(2):
                            last = nc.vector.tensor_tensor(lo[j][b][:, :, 0:T], chunks(tp[j][:, :]), hi[j][b][:, :, 0:T].bitcast(F32),
                                                           ALU.subtract)
                        last.then_inc(p_lo, 1)

                    norm(Tile(None, 0, 2, ET))
                    norm(Tile(None, 1, 2, ET))
                    low(Tile(None, 0, 2, ET))

                    def step(a):
                        b, n = a.buf(), a.use()
                        dve.wait_ge(p_sums, 2 * a.t + 2)
                        if not a.early(2):
                            dve.wait_ge(sent_row[b], 16 * n)
                        nc.vector.tensor_scalar(idx[b][:, 2:3], sums[:, 0, bass.ds(a.t, 1)], float(E - 1), 0.5, ALU.add, ALU.mult)\
                            .then_inc(p_rank_idx, 1)
                        if a.later(1).exists():
                            low(a.later(1))
                        if not a.early(1):
                            dve.wait_ge(p_qk, a.t)
                        dve.wait_ge(p_mm[0], a.t + 1)
                        nc.vector.tensor_tensor(qs[:, :], qkv[0][b][0:T, :], q_bias[:, :], ALU.add).then_inc(p_q, 1)
                        dve.wait_ge(p_mm[1], a.t + 1)
                        nc.vector.tensor_tensor(ks[:, :], qkv[1][b][0:T, :], k_bias[:, :], ALU.add).then_inc(p_k, 1)
                        if not a.early(2):
                            dve.wait_ge(sent_row[b], 16 * n)
                        nc.vector.tensor_scalar(row[b][:, RANKB:RANKB + 1], sums[:, 1, bass.ds(a.t, 1)], float(E - 1), 0.5, ALU.add, ALU.mult)
                        nc.vector.tensor_copy(row[b][:, SRC:EW + 1], edge_f[:, :, bass.ds(a.t, 1)].rearrange("p j o -> p (j o)"))
                        nc.vector.memset(row[b][:, DIAG + 1:ROW], 0.0)
                        dve.wait_ge(got_diag[b], 16 * n + 16)
                        nc.vector.tensor_copy(row[b][:, DIAG:DIAG + 1], dg[b][:, :]).then_inc(p_rowf, 1)
                        if a.later(2).exists():
                            norm(a.later(2))
                        dve.wait_ge(p_mm[2], a.t + 1)
                        nc.vector.tensor_tensor(row[b][:, 0:D], qkv[2][b][0:T, :], v_bias[:, :], ALU.add).then_inc(p_v, 1)
                        dve.wait_ge(p_qk, a.t + 1)
                        nc.vector.tensor_reduce(score[:, :], qk[:, :].rearrange("p (h d) -> p h d", h=H), axis=AX.X, op=ALU.add)\
                            .then_inc(p_sc, 1)
                        dve.wait_ge(p_sc, a.t + 1)
                        nc.vector.scalar_tensor_tensor(row[b][:, WS:WS + H], score[:, :], SCALE,
                                                       attr_s[:, bass.ds(a.t, 1), :].rearrange("p o h -> p (o h)"),
                                                       ALU.mult, ALU.mult).then_inc(p_row, 1)
                    tiles(dve, step, ET)

                @block.tensor
                def _(pe):
                    def turn(a):
                        b = a.buf()
                        pe.wait_ge(p_xh, a.t + 1)
                        if not a.early(1):
                            pe.wait_ge(p_lo, a.t)
                        for j in range(2):
                            last = transpose_tile(tp[j], xh[j][b], ident)
                        last.then_inc(p_t, 1)

                    turn(Tile(None, 0, 2, ET))

                    def step(a):
                        b = a.buf()
                        if a.later(1).exists():
                            turn(a.later(1))
                        pe.wait_ge(p_lo, a.t + 1)
                        for n, (side, w, free) in enumerate(((0, q_w, p_q), (1, k_w, p_k), (1, v_w, p_v))):
                            if not a.early(2):
                                pe.wait_ge(free, a.t - 1)
                            product(qkv[n][b], hi[side][b], lo[side][b], w).then_inc(p_mm[n], 1)
                    tiles(pe, step, ET)

        end_part()
        by_dst_s = whole.enter_context(nc.sbuf_tensor("by_dst_s", [T, ET, 4], F32))
        near = whole.enter_context(nc.sbuf_tensor("src_fields", [T, ET, FIELDS], F32))
        place_i = whole.enter_context(nc.sbuf_tensor("place_i", [T, 4, ET], I32))
        PLACE, SLOT, RB, SRCI = range(4)
        rec_den = whole.enter_context(nc.sbuf_tensor("rec_den", [T, ET, H], F32))
        e_col = whole.enter_context(nc.sbuf_tensor("e_col", [T, ET, H], F32))
        prev_key = whole.enter_context(nc.sbuf_tensor("prev_key", [T, ET + 1], F32))
        last_row = whole.enter_context(nc.sbuf_tensor("last_row", [T, 1], F32))
        with ExitStack() as ph:
            sb, ps = holder(ph)
            R = H + 1
            QT = 4
            NB = ET // QT
            key9 = sb("key9", [R, E])
            run = sb("run", [R, E])
            top = sb("top", [R, E])
            same = sb("same", [R, E + 1])
            gap = sb("gap", [R, E + 1])
            place_f = sb("place_f", [T, ET])
            ends = sb("ends", [T, ET])
            stage = [sb(f"stage_b{i}", [P, KC, D]) for i in range(2)]
            w2_parts = [sb(f"w2_{p}", [P, KC, D], F32R) for p in ("hi", "lo")]
            w1t = [sb(f"w1t_{p}", [P, KC, P], F32R) for p in ("hi", "lo")]
            b1_col = sb("b1_col", [P, KC])
            field9 = sb("field9", [T, ET, R])
            banks = ps("wide", (P, NB, D))
            one = ps("one_bank")
            two = ps("two_bank")
            three = ps("three_bank")
            wide = banks[0:R, :, 0:QT * T]
            s_in, s_small, s_bias = sem("s_in"), sem("s_small"), sem("s_bias")
            s_w_in = sems("s_w_in")
            s_pos, s_f9, s_t = sem("s_pos"), sem("s_f9"), sem("s_t")
            s_ev, s_same, s_gap, s_run, s_top, s_d, s_e, s_sum = (sem(f"s_{n}") for n in ("ev", "same", "gap", "run", "top", "d", "e", "sum"))
            s_back, s_got, s_end, s_c = sem("s_back"), sem("s_got"), sem("s_end"), sem("s_c")
            s_hi, s_lo, s_w1t, s_w1h, s_w1l, s_w12, s_w12h, s_w12l, s_cmm, s_cev = (
                sem(f"s_{n}") for n in ("hi", "lo", "w1t", "w1h", "w1l", "w12", "w12h", "w12l", "cmm", "cev"))
            block = ph.enter_context(nc.Block())
            loads = ((w2, w2_parts), (w01, dense1_w), (w11, conv1_w), (w12g, conv2_w), (w02, dense2_w))

            @block.sync
            def _(sp):
                sp.dma_start(near[:, :, :], by_src[:, WS:ROW].rearrange("(t p) f -> p t f", p=T)).then_inc(s_in, 16)
                sp.dma_start(b1_col[:, :], columns(b1)).then_inc(s_small, 16)
                sp.dma_start(half_c[:, :], row_for_all(b2)).then_inc(s_bias, 16)
                sp.dma_start(neigh_b[:, 0:D], row_for_all(gb1)).then_inc(s_bias, 16)
                sp.dma_start(neigh_b[:, D:2 * D], row_for_all(gb2)).then_inc(s_bias, 16)
                sp.dma_start(stage[0][:, :, :], weight_rows(w2)).then_inc(s_w_in[0], 16)
                sp.dma_start(stage[1][:, :, :], weight_rows(w1)).then_inc(s_w_in[1], 16)
                for i in range(1, len(loads)):
                    sp.wait_ge(s_lo, i)
                    if i == 1:
                        sp.wait_ge(s_cmm, 1)
                    sp.dma_start(stage[0][:, :, :], weight_rows(loads[i][0])).then_inc(s_w_in[0], 16)

            @block.gpsimd
            def _(pool):
                nc.gpsimd.iota(place_i[:, PLACE, :], [[T, ET]], base=0, channel_multiplier=1).then_inc(s_pos, 1)
                nc.gpsimd.memset(last_row[:, :], 0.0).then_inc(s_pos, 1)
                pool.wait_ge(s_pos, 2)
                nc.gpsimd.affine_select(out=last_row[:, :], in_=last_row[:, :], compare_op=ALU.not_equal, fill=1.0,
                                        base=-(T - 1), pattern=[[0, 1]], channel_multiplier=1).then_inc(s_pos, 1)
                for i, (_, w) in enumerate(loads):
                    pool.wait_ge(s_hi, i + 1)
                    for k in range(KC):
                        last = nc.gpsimd.tensor_tensor(w[1][:, k, :], stage[0][:, k, :], w[0][:, k, :].bitcast(F32), ALU.subtract)
                    last.then_inc(s_lo, 1)

            @block.scalar
            def _(act):
                def high(i):
                    act.wait_ge(s_w_in[0], 16 * (i + 1))
                    for k in range(KC):
                        last = nc.scalar.activation(loads[i][1][0][:, k, :], stage[0][:, k, :], ACT.Copy)
                    last.then_inc(s_hi, 1)

                high(0)
                act.wait_ge(s_d, 1)
                nc.scalar.activation(run[0:H, :], top[0:H, :], ACT.Exp).then_inc(s_e, 1)
                for m in range(KC):
                    act.wait_ge(s_w1t, m + 1)
                    if m:
                        act.wait_ge(s_w12, m)
                    nc.scalar.activation(w1t[0][:, :, :], one[:, :].rearrange("p (k c) -> p k c", k=KC), ACT.Copy).then_inc(s_w1h, 1)
                    act.wait_ge(s_w12, m + 1)
                    nc.scalar.activation(attn_w[0][:, m, :], two[:, :], ACT.Copy).then_inc(s_w12h, 1)
                for i in range(1, len(loads)):
                    high(i)

            @block.vector
            def _(dve):
                dve.wait_ge(s_pos, 3)
                dve.wait_ge(s_in, 16)
                nc.vector.tensor_copy(place_f[:, :], place_i[:, PLACE, :]).then_inc(s_f9, 1)
                nc.vector.tensor_copy(field9[:, :, 0:H], near[:, :, 0:H]).then_inc(s_f9, 1)
                dve.wait_ge(s_f9, 1)
                nc.vector.tensor_copy(field9[:, :, H], place_f[:, :]).then_inc(s_f9, 1)
                dve.wait_ge(s_t, 1)
                nc.vector.tensor_copy(key9[:, :].rearrange("r (b c) -> r b c", b=NB), wide).then_inc(s_ev, 1)
                nc.vector.memset(same[:, 0:1], 0.0)
                nc.vector.memset(same[:, E:E + 1], 0.0)
                dve.wait_ge(s_ev, 1)
                nc.vector.tensor_tensor(same[:, 1:E], key9[:, 1:E], key9[:, 0:E - 1], ALU.is_equal).then_inc(s_same, 1)
                dve.wait_ge(s_same, 1)
                nc.vector.tensor_scalar(gap[:, :], same[:, :], 1.0, -GAP, ALU.subtract, ALU.mult).then_inc(s_gap, 1)
                dve.wait_ge(s_t, 2)
                nc.vector.tensor_copy(key9[:, :].rearrange("r (b c) -> r b c", b=NB), wide).then_inc(s_ev, 1)
                dve.wait_ge(s_ev, 2)
                dve.wait_ge(s_gap, 1)
                nc.vector.tensor_tensor_scan(run[:, :], gap[:, 0:E], key9[:, :], 0.0, ALU.add, ALU.max).then_inc(s_run, 1)
                dve.wait_ge(s_run, 1)
                nc.vector.tensor_tensor_scan(top[:, ::-1], gap[:, E:0:-1], run[:, ::-1], 0.0, ALU.add, ALU.max).then_inc(s_top, 1)
                dve.wait_ge(s_back, 1)
                nc.vector.tensor_copy(ends[:, :], three[0:T, 0:ET * R].rearrange("p (t r) -> p t r", r=R)[:, :, H]).then_inc(s_end, 1)
                nc.vector.tensor_tensor(top[0:H, :], key9[0:H, :], top[0:H, :], ALU.subtract).then_inc(s_d, 1)
                dve.wait_ge(s_e, 1)
                nc.vector.tensor_tensor_scan(key9[0:H, :], same[0:H, 0:E], run[0:H, :], 0.0, ALU.mult, ALU.add).then_inc(s_sum, 1)
                dve.wait_ge(s_end, 1)
                nc.vector.tensor_tensor(place_f[:, :], place_f[:, :], ends[:, :], ALU.not_equal).then_inc(s_end, 1)
                dve.wait_ge(s_end, 2)
                nc.vector.scalar_tensor_tensor(place_i[:, SLOT, :], place_f[:, :], float(FAR), near[:, :, SRC - WS], ALU.mult, ALU.add)
                nc.vector.tensor_copy(place_i[:, RB, :], near[:, :, RANKB - WS])
                nc.vector.tensor_copy(place_i[:, SRCI, :], near[:, :, SRC - WS])
                nc.vector.tensor_copy(by_dst_s[:, :, 0:2], near[:, :, DST - WS:EW - WS + 1])
                nc.vector.tensor_copy(by_dst_s[:, :, 2], ends[:, :])
                nc.vector.tensor_copy(by_dst_s[:, :, 3], ends[:, :])
                nc.vector.tensor_scalar(prev_key[:, 1:ET + 1], near[:, :, SRC - WS], 1.0, last_row[:, 0:1], ALU.add, ALU.mult).then_inc(s_c, 1)
                nc.vector.memset(prev_key[:, 0:1], 0.0).then_inc(s_c, 1)
                dve.wait_ge(s_c, 2)
                nc.vector.tensor_scalar(prev_key[:, :], prev_key[:, :], 1.0, None, ALU.subtract)
                dve.wait_ge(s_bias, 48)
                dve.wait_ge(s_cmm, 1)
                nc.vector.tensor_tensor(half_c[:, :], two[0:T, :], half_c[:, :], ALU.add).then_inc(s_cev, 1)
                dve.wait_ge(s_cev, 1)
                nc.vector.tensor_scalar(half_c[:, :], half_c[:, :], 0.5, None, ALU.mult)
                nc.vector.tensor_scalar(neigh_b[:, D:2 * D], neigh_b[:, D:2 * D], 1.0 / 3.0, None, ALU.mult)
                dve.wait_ge(s_back, 2)
                nc.vector.tensor_copy(e_col[:, :, :], three[0:T, 0:ET * H].rearrange("p (t h) -> p t h", h=H)).then_inc(s_got, 1)
                nc.vector.tensor_scalar(rec_den[:, :, :], three[0:T, ET * H:2 * ET * H].rearrange("p (t h) -> p t h", h=H),
                                        1e-16, None, ALU.add).then_inc(s_got, 1)
                dve.wait_ge(s_got, 2)
                nc.vector.reciprocal(rec_den[:, :, :], rec_den[:, :, :])
                for m in range(KC):
                    dve.wait_ge(s_w1h, m + 1)
                    nc.vector.tensor_tensor(w1t[1][:, :, :], one[:, :].rearrange("p (k c) -> p k c", k=KC),
                                            w1t[0][:, :, :].bitcast(F32), ALU.subtract).then_inc(s_w1l, 1)
                    dve.wait_ge(s_w12h, m + 1)
                    nc.vector.tensor_tensor(attn_w[1][:, m, :], two[:, :], attn_w[0][:, m, :].bitcast(F32), ALU.subtract).then_inc(s_w12l, 1)

            @block.tensor
            def _(pe):
                def wide_at(t):
                    return banks[0:R, t // QT, (t % QT) * T:(t % QT + 1) * T]

                pe.wait_ge(s_in, 16)
                for t in range(ET):
                    last = nc.tensor.transpose(wide_at(t), near[:, t, SRC - WS:SRC - WS + 1].to_broadcast([T, R]), ident[0:T, 0:T])
                last.then_inc(s_t, 1)
                pe.wait_ge(s_f9, 3)
                pe.wait_ge(s_ev, 1)
                for t in range(ET):
                    last = nc.tensor.transpose(wide_at(t), field9[:, t, :], ident[0:T, 0:T])
                last.then_inc(s_t, 1)
                pe.wait_ge(s_small, 16)
                pe.wait_ge(s_w_in[0], 16)
                for k in range(KC):
                    last = nc.tensor.matmul(two[0:T, :], b1_col[:, k:k + 1].to_broadcast([P, T]), stage[0][:, k, :],
                                            start=(k == 0), stop=(k == KC - 1))
                last.then_inc(s_cmm, 1)
                pe.wait_ge(s_top, 1)
                for t in range(ET):
                    last = nc.tensor.transpose(three[0:T, t * R:(t + 1) * R], top[:, t * T:(t + 1) * T], ident[0:R, 0:R])
                last.then_inc(s_back, 1)
                pe.wait_ge(s_end, 1)
                pe.wait_ge(s_sum, 1)
                for t in range(ET):
                    nc.tensor.transpose(three[0:T, t * H:(t + 1) * H], run[0:H, t * T:(t + 1) * T], ident[0:H, 0:H])
                    last = nc.tensor.transpose(three[0:T, (ET + t) * H:(ET + t + 1) * H], key9[0:H, t * T:(t + 1) * T], ident[0:H, 0:H])
                last.then_inc(s_back, 1)
                pe.wait_ge(s_w_in[1], 16)
                pe.wait_ge(s_lo, 1)
                pe.wait_ge(s_cev, 1)
                for m in range(KC):
                    if m:
                        pe.wait_ge(s_w1l, m)
                    for k in range(KC):
                        last = nc.tensor.transpose(one[:, P * k:P * (k + 1)], stage[1][:, m, P * k:P * (k + 1)], ident[:, :])
                    last.then_inc(s_w1t, 1)
                    pe.wait_ge(s_w1l, m + 1)
                    if m:
                        pe.wait_ge(s_w12l, m)
                    n = 0
                    for k in range(KC):
                        for a, b in ((0, 0), (0, 1), (1, 0)):
                            last = nc.tensor.matmul(two[:, :], w1t[a][:, k, :], w2_parts[b][:, k, :], start=(n == 0), stop=(n == 3 * KC - 1))
                            n += 1
                    last.then_inc(s_w12, 1)

        end_part()
        with ExitStack() as ph:
            sb, ps = holder(ph)
            vx = [sb(f"vx{b}", [T, 2, D]) for b in range(2)]
            wvs = [sb(f"wvs{b}", [T, D]) for b in range(2)]
            match = [sb(f"match{b}", [T, 2, T]) for b in range(2)]
            key_now = [sb(f"key_now{b}", [T, 1]) for b in range(2)]
            total = [sb(f"total{b}", [T, D]) for b in range(2)]
            vals = [sb(f"vals{b}", [T, D]) for b in range(2)]
            hi = [sb(f"a_hi{b}", [P, KC, P], F32R) for b in range(2)]
            lo = [sb(f"a_lo{b}", [P, KC, P], F32R) for b in range(2)]
            u = [sb(f"u{b}", [T, D]) for b in range(2)]
            y = [sb(f"y{b}", [T, D]) for b in range(2)]
            x1 = [sb(f"x1_{b}", [T, D]) for b in range(2)]
            st, mv, rs = sb("a_st", [T, 6]), sb("a_mv", [T, 2]), sb("a_rs", [T, 2])
            pidx = [sb(f"pidx{b}", [T, 4], I32) for b in range(2)]
            brow = [sb(f"brow{b}", [T, 4]) for b in range(2)]
            keys_ps = [ps(f"a_keys{b}") for b in range(2)]
            sum_ps = [ps(f"a_sum{b}") for b in range(2)]
            tp = [ps(f"a_tp{b}") for b in range(2)]
            out_ps = [ps(f"a_out{b}") for b in range(2)]
            a_v, a_x, a_u_out, a_x1_out = sems("a_v"), sems("a_x"), sems("a_u_out"), sems("a_x1_out")
            a_slot, a_brow = sems("a_slot"), sems("a_brow")
            a_key, a_m, a_wv, a_sum, a_tot, a_val, a_t, a_hi, a_lo, a_mm, a_u, a_y, a_st, a_ag, a_dev, a_rec, a_x1, a_idx, a_zero = (
                sem(f"a_{n}") for n in ("key", "m", "wv", "sum", "tot", "val", "t", "hi", "lo", "mm", "u", "y", "st", "ag", "dev", "rec", "x1", "idx", "zero"))
            a_now = sem("a_now")
            block = ph.enter_context(nc.Block())

            @block.sync
            def _(sp):
                def load(a):
                    b = a.buf()
                    if not a.early(2):
                        sp.wait_ge(a_wv, a.t - 1)
                        sp.wait_ge(a_u, a.t - 1)
                    sp.dma_start(vx[b][:, 0, :], by_src[bass.ds(a.t * T, T), 0:D]).then_inc(a_v[b], 16)
                    sp.dma_start(vx[b][:, 1, :], x_by_src[bass.ds(a.t * T, T), :]).then_inc(a_x[b], 16)

                def store(a):
                    b = a.buf()
                    sp.wait_ge(a_u, a.t + 1)
                    sp.dma_start(x_new[bass.ds(a.t * T, T), :], u[b][:, :]).then_inc(a_u_out[b], 16)
                    sp.wait_ge(a_x1, a.t + 1)
                    sp.dma_start(x1_rows[bass.ds(a.t * T, T), :], x1[b][:, :]).then_inc(a_x1_out[b], 16)

                load(Tile(None, 0, 2, ET))
                load(Tile(None, 1, 2, ET))

                def step(a):
                    store(a)
                    if a.later(2).exists():
                        load(a.later(2))
                tiles(sp, step, ET)
                for b in range(2):
                    sp.wait_ge(a_u_out[b], 16 * (ET // 2))
                    sp.wait_ge(a_x1_out[b], 16 * (ET // 2))

            @block.gpsimd
            def _(pool):
                bound = {"N": pool.to_reg(N - 1), "E": pool.to_reg(E - 1)}
                def step(a):
                    b, n = a.buf(), a.use()
                    if not a.early(2):
                        pool.wait_ge(a_slot[b], 16 * n)
                        pool.wait_ge(a_brow[b], 16 * n)
                    nc.gpsimd.tensor_copy(pidx[b][:, 0:3], place_i[:, 0:3, bass.ds(a.t, 1)].rearrange("p j o -> p (j o)"))
                    nc.gpsimd.tensor_copy(brow[b][:, :], by_dst_s[:, bass.ds(a.t, 1), :].rearrange("p o f -> p (o f)")).then_inc(a_idx, 1)
                    pool.wait_ge(a_idx, a.t + 1)
                    alone(pool)
                    pool.indirect_dma_start(by_dst, bass.IndirectOffsetOnAxis(ap=pidx[b][:, RB:RB + 1], axis=0), brow[b][:, :], None,
                                            bounds_check=bound["E"], oob_is_err=False).then_inc(a_brow[b], 16)
                    alone(pool)
                    pool.indirect_dma_start(slot_src, bass.IndirectOffsetOnAxis(ap=pidx[b][:, SLOT:SLOT + 1], axis=0),
                                            pidx[b][:, PLACE:PLACE + 1], None,
                                            bounds_check=bound["N"], oob_is_err=False).then_inc(a_slot[b], 16)
                tiles(pool, step, ET)
                for b in range(2):
                    pool.wait_ge(a_slot[b], 16 * (ET // 2))
                    pool.wait_ge(a_brow[b], 16 * (ET // 2))

            @block.scalar
            def _(act):
                def now(a):
                    if not a.early(2):
                        act.wait_ge(a_key, a.t - 1)
                    nc.scalar.copy(key_now[a.buf()][:, :], near[:, bass.ds(a.t, 1), SRC - WS:SRC - WS + 1].rearrange("p o f -> p (o f)"))\
                        .then_inc(a_now, 1)

                now(Tile(None, 0, 2, ET))
                now(Tile(None, 1, 2, ET))

                def step(a):
                    b = a.buf()
                    if a.later(2).exists():
                        now(a.later(2))
                    act.wait_ge(a_sum, a.t + 1)
                    if not a.early(2):
                        act.wait_ge(a_val, a.t - 1)
                        act.wait_ge(a_sum, a.t)
                    nc.scalar.activation(total[b][:, :], sum_ps[b][0:T, :], ACT.Copy).then_inc(a_tot, 1)
                    act.wait_ge(a_t, a.t + 1)
                    if not a.early(2):
                        act.wait_ge(a_mm, a.t - 1)
                    nc.scalar.activation(hi[b][:, :, 0:T], chunks(tp[b][:, :]), ACT.Copy).then_inc(a_hi, 1)
                    act.wait_ge(a_ag, a.t + 1)
                    nc.scalar.activation(rs[:, 0:1], mv[:, 1:2], ACT.Sqrt, bias=eps[0:T, 1:2]).then_inc(a_dev, 1)
                tiles(act, step, ET)

            @block.vector
            def _(dve):
                nc.vector.memset(total[1][:, :], 0.0).then_inc(a_zero, 1)

                def prepare(a):
                    b, n = a.buf(), a.use()
                    dve.wait_ge(a_key, a.t + 1)
                    if not a.early(2):
                        dve.wait_ge(a_sum, a.t - 1)
                    nc.vector.tensor_scalar(match[b][:, 0, :], keys_ps[b][0:T, 0:T],
                                            near[:, bass.ds(a.t, 1), SRC - WS:SRC - WS + 1].rearrange("p o f -> p (o f)"), None, ALU.is_equal)
                    nc.vector.tensor_scalar(match[b][:, 1, :], keys_ps[b][0:T, 0:T], prev_key[:, bass.ds(a.t, 1)], None, ALU.is_equal).then_inc(a_m, 1)
                    dve.wait_ge(a_v[b], 16 * n + 16)
                    nc.vector.tensor_tensor(wvs[b][:, :].rearrange("p (h d) -> p h d", h=H), vx[b][:, 0, :].rearrange("p (h d) -> p h d", h=H),
                                            e_col[:, bass.ds(a.t, 1), :].rearrange("p o h -> p h o").to_broadcast([T, H, HD]),
                                            ALU.mult).then_inc(a_wv, 1)

                prepare(Tile(None, 0, 2, ET))

                def step(a):
                    b, n = a.buf(), a.use()
                    if a.later(1).exists():
                        prepare(a.later(1))
                    dve.wait_ge(a_tot, a.t + 1)
                    if not a.early(2):
                        dve.wait_ge(a_t, a.t - 1)
                    nc.vector.tensor_tensor(vals[b][:, :].rearrange("p (h d) -> p h d", h=H), total[b][:, :].rearrange("p (h d) -> p h d", h=H),
                                            rec_den[:, bass.ds(a.t, 1), :].rearrange("p o h -> p h o").to_broadcast([T, H, HD]),
                                            ALU.mult).then_inc(a_val, 1)
                    dve.wait_ge(a_hi, a.t + 1)
                    nc.vector.tensor_tensor(lo[b][:, :, 0:T], chunks(tp[b][:, :]), hi[b][:, :, 0:T].bitcast(F32), ALU.subtract).then_inc(a_lo, 1)
                    dve.wait_ge(a_mm, a.t + 1)
                    dve.wait_ge(a_x[b], 16 * n + 16)
                    if not a.early(2):
                        dve.wait_ge(a_u_out[b], 16 * n)
                        dve.wait_ge(a_x1_out[b], 16 * n)
                    nc.vector.scalar_tensor_tensor(u[b][:, :], out_ps[b][0:T, :], 0.5, vx[b][:, 1, :], ALU.mult, ALU.add).then_inc(a_u, 1)
                    dve.wait_ge(a_u, a.t + 1)
                    nc.vector.tensor_tensor(y[b][:, :], u[b][:, :], half_c[:, :], ALU.add).then_inc(a_y, 1)
                    dve.wait_ge(a_y, a.t + 1)
                    nc.vector.bn_stats(st[:, :], y[b][:, :]).then_inc(a_st, 1)
                    dve.wait_ge(a_st, a.t + 1)
                    alone(dve)
                    nc.vector.bn_aggr(mv[:, :], st[:, :]).then_inc(a_ag, 1)
                    dve.wait_ge(a_dev, a.t + 1)
                    nc.vector.reciprocal(rs[:, 1:2], rs[:, 0:1]).then_inc(a_rec, 1)
                    dve.wait_ge(a_rec, a.t + 1)
                    nc.vector.tensor_scalar(x1[b][:, :], y[b][:, :], mv[:, 0:1], rs[:, 1:2], ALU.subtract, ALU.mult).then_inc(a_x1, 1)
                tiles(dve, step, ET)

            @block.tensor
            def _(pe):
                def keys(a):
                    b = a.buf()
                    if not a.early(2):
                        pe.wait_ge(a_m, a.t - 1)
                    pe.wait_ge(a_now, a.t + 1)
                    nc.tensor.transpose(keys_ps[b][0:T, 0:T], key_now[b][:, :].to_broadcast([T, T]), ident[0:T, 0:T]).then_inc(a_key, 1)

                def sums_of(a):
                    b = a.buf()
                    pe.wait_ge(a_m, a.t + 1)
                    pe.wait_ge(a_wv, a.t + 1)
                    if not a.early(2):
                        pe.wait_ge(a_tot, a.t - 1)
                    nc.tensor.matmul(sum_ps[b][0:T, :], match[b][:, 0, :], wvs[b][:, :], start=True, stop=False)
                    if a.early(1):
                        pe.wait_ge(a_zero, 1)
                    else:
                        pe.wait_ge(a_tot, a.t)
                    nc.tensor.matmul(sum_ps[b][0:T, :], match[b][:, 1, :], total[1 - b][:, :], start=False, stop=True).then_inc(a_sum, 1)

                keys(Tile(None, 0, 2, ET))
                keys(Tile(None, 1, 2, ET))
                sums_of(Tile(None, 0, 2, ET))

                def step(a):
                    b = a.buf()
                    pe.wait_ge(a_val, a.t + 1)
                    if not a.early(2):
                        pe.wait_ge(a_lo, a.t - 1)
                    transpose_tile(tp[b], vals[b], ident).then_inc(a_t, 1)
                    if a.later(2).exists():
                        keys(a.later(2))
                    if a.later(1).exists():
                        sums_of(a.later(1))
                    pe.wait_ge(a_lo, a.t + 1)
                    if not a.early(2):
                        pe.wait_ge(a_u, a.t - 1)
                    product(out_ps[b], hi[b], lo[b], attn_w).then_inc(a_mm, 1)
                tiles(pe, step, ET)

        end_part()
        dfield = whole.enter_context(nc.sbuf_tensor("dfield", [T, ET, 4], F32))
        dprev = whole.enter_context(nc.sbuf_tensor("dprev", [T, ET + 1], F32))
        dnext = whole.enter_context(nc.sbuf_tensor("dnext", [T, ET], F32))
        dplace = whole.enter_context(nc.sbuf_tensor("dplace", [T, 2, ET], I32))

        def convolve(first):
            table = x1_rows if first else h1_rows
            w = conv1_w if first else conv2_w
            c0 = 0 if first else D
            nm = "c1" if first else "c2"
            stores = 32 if first else 16
            with ExitStack() as ph:
                sb, ps = holder(ph)
                g = [sb(f"{nm}_g{b}", [T, D]) for b in range(2)]
                key_now = [sb(f"{nm}_key_now{b}", [T, 1]) for b in range(2)]
                match = [sb(f"{nm}_match{b}", [T, 2, T]) for b in range(2)]
                total = [sb(f"{nm}_total{b}", [T, D]) for b in range(2)]
                hi = [sb(f"{nm}_hi{b}", [P, KC, P], F32R) for b in range(2)]
                lo = [sb(f"{nm}_lo{b}", [P, KC, P], F32R) for b in range(2)]
                res = [sb(f"{nm}_res{b}", [T, D]) for b in range(2)]
                pidx = [sb(f"{nm}_idx{b}", [T, 3], I32) for b in range(2)]
                keys_ps = [ps(f"{nm}_keys{b}") for b in range(2)]
                sum_ps = [ps(f"{nm}_sum{b}") for b in range(2)]
                tp = [ps(f"{nm}_tp{b}") for b in range(2)]
                out_ps = [ps(f"{nm}_out{b}") for b in range(2)]
                s_g, s_out, s_slot = sems(f"{nm}_g"), sems(f"{nm}_out"), sems(f"{nm}_slot")
                s_key, s_m, s_sum, s_tot, s_t, s_hi, s_lo, s_mm, s_res, s_idx, s_zero, s_field, s_prep = (
                    sem(f"{nm}_{n}") for n in ("key", "m", "sum", "tot", "t", "hi", "lo", "mm", "res", "idx", "zero", "field", "prep"))
                s_now = sem(f"{nm}_now")
                block = ph.enter_context(nc.Block())

                @block.sync
                def _(sp):
                    if first:
                        sp.dma_start(dfield[:, :, :], by_dst[0:E, :].rearrange("(t p) f -> p t f", p=T)).then_inc(s_field, 16)
                        sp.dma_start(dnext[:, :], by_dst[1:E + 1, 0:1].rearrange("(t p) f -> p (t f)", p=T)).then_inc(s_field, 16)

                    def step(a):
                        b = a.buf()
                        sp.wait_ge(s_res, a.t + 1)
                        sp.dma_start(neigh[bass.ds(a.t * T, T), c0:c0 + D], res[b][:, :]).then_inc(s_out[b], 16)
                        if first:
                            sp.dma_start(neigh1[bass.ds(a.t * T, T), :], res[b][:, :]).then_inc(s_out[b], 16)
                    tiles(sp, step, ET)
                    for b in range(2):
                        sp.wait_ge(s_out[b], stores * (ET // 2))

                @block.gpsimd
                def _(pool):
                    bound = {"N": pool.to_reg(N - 1), "E": pool.to_reg(E - 1)}
                    if first:
                        pool.wait_ge(s_prep, 4)

                    def step(a):
                        b, n = a.buf(), a.use()
                        if not a.early(2):
                            pool.wait_ge(s_sum, a.t - 1)
                            pool.wait_ge(s_g[b], 16 * n)
                            if first:
                                pool.wait_ge(s_slot[b], 16 * n)
                        nc.gpsimd.tensor_copy(pidx[b][:, 0:2], dplace[:, :, bass.ds(a.t, 1)].rearrange("p j o -> p (j o)"))
                        nc.gpsimd.tensor_copy(pidx[b][:, 2:3], place_i[:, PLACE, bass.ds(a.t, 1)]).then_inc(s_idx, 1)
                        pool.wait_ge(s_idx, a.t + 1)
                        alone(pool)
                        pool.indirect_dma_start(g[b][:, :], None, table, bass.IndirectOffsetOnAxis(ap=pidx[b][:, 0:1], axis=0),
                                                bounds_check=bound["E"], oob_is_err=False).then_inc(s_g[b], 16)
                        if first:
                            alone(pool)
                            pool.indirect_dma_start(slot_dst, bass.IndirectOffsetOnAxis(ap=pidx[b][:, 1:2], axis=0), pidx[b][:, 2:3], None,
                                                    bounds_check=bound["N"], oob_is_err=False).then_inc(s_slot[b], 16)
                    tiles(pool, step, ET)
                    if first:
                        for b in range(2):
                            pool.wait_ge(s_slot[b], 16 * (ET // 2))

                @block.scalar
                def _(act):
                    def now(a):
                        if not a.early(2):
                            act.wait_ge(s_key, a.t - 1)
                        nc.scalar.copy(key_now[a.buf()][:, :], dfield[:, bass.ds(a.t, 1), 0:1].rearrange("p o f -> p (o f)")).then_inc(s_now, 1)

                    if first:
                        act.wait_ge(s_field, 32)
                    now(Tile(None, 0, 2, ET))
                    now(Tile(None, 1, 2, ET))

                    def step(a):
                        b = a.buf()
                        if a.later(2).exists():
                            now(a.later(2))
                        act.wait_ge(s_sum, a.t + 1)
                        if not a.early(2):
                            act.wait_ge(s_t, a.t - 1)
                        nc.scalar.activation(total[b][:, :], sum_ps[b][0:T, :], ACT.Copy).then_inc(s_tot, 1)
                        act.wait_ge(s_t, a.t + 1)
                        if not a.early(2):
                            act.wait_ge(s_mm, a.t - 1)
                        nc.scalar.activation(hi[b][:, :, 0:T], chunks(tp[b][:, :]), ACT.Copy).then_inc(s_hi, 1)
                    tiles(act, step, ET)

                @block.vector
                def _(dve):
                    nc.vector.memset(total[1][:, :], 0.0).then_inc(s_zero, 1)
                    if first:
                        dve.wait_ge(s_field, 32)
                        nc.vector.tensor_tensor(dnext[:, :], dnext[:, :], dfield[:, :, 0], ALU.is_equal).then_inc(s_prep, 1)
                        nc.vector.tensor_scalar(dprev[:, 1:ET + 1], dfield[:, :, 0], 1.0, last_row[:, 0:1], ALU.add, ALU.mult).then_inc(s_prep, 1)
                        nc.vector.memset(dprev[:, 0:1], 0.0).then_inc(s_prep, 1)
                        dve.wait_ge(s_prep, 3)
                        nc.vector.tensor_scalar(dprev[:, :], dprev[:, :], 1.0, None, ALU.subtract)
                        nc.vector.tensor_copy(dplace[:, 0, :], dfield[:, :, 2])
                        nc.vector.scalar_tensor_tensor(dplace[:, 1, :], dnext[:, :], float(FAR), dfield[:, :, 0], ALU.mult, ALU.add).then_inc(s_prep, 1)
                        dve.wait_ge(s_prep, 4)

                    def prepare(a):
                        b = a.buf()
                        dve.wait_ge(s_key, a.t + 1)
                        if not a.early(2):
                            dve.wait_ge(s_sum, a.t - 1)
                        nc.vector.tensor_scalar(match[b][:, 0, :], keys_ps[b][0:T, 0:T],
                                                dfield[:, bass.ds(a.t, 1), 0:1].rearrange("p o f -> p (o f)"),
                                                dfield[:, bass.ds(a.t, 1), 1:2].rearrange("p o f -> p (o f)"), ALU.is_equal, ALU.mult)
                        nc.vector.tensor_scalar(match[b][:, 1, :], keys_ps[b][0:T, 0:T],
                                                dprev[:, bass.ds(a.t, 1)], None, ALU.is_equal).then_inc(s_m, 1)

                    prepare(Tile(None, 0, 2, ET))

                    def step(a):
                        b, n = a.buf(), a.use()
                        if a.later(1).exists():
                            prepare(a.later(1))
                        dve.wait_ge(s_hi, a.t + 1)
                        nc.vector.tensor_tensor(lo[b][:, :, 0:T], chunks(tp[b][:, :]), hi[b][:, :, 0:T].bitcast(F32), ALU.subtract).then_inc(s_lo, 1)
                        dve.wait_ge(s_mm, a.t + 1)
                        if not a.early(2):
                            dve.wait_ge(s_out[b], stores * n)
                        nc.vector.scalar_tensor_tensor(res[b][:, :], out_ps[b][0:T, :], 1.0 if first else 1.0 / 3.0, neigh_b[:, c0:c0 + D],
                                                       ALU.mult, ALU.add).then_inc(s_res, 1)
                    tiles(dve, step, ET)

                @block.tensor
                def _(pe):
                    def keys(a):
                        b = a.buf()
                        if not a.early(2):
                            pe.wait_ge(s_m, a.t - 1)
                        pe.wait_ge(s_now, a.t + 1)
                        nc.tensor.transpose(keys_ps[b][0:T, 0:T], key_now[b][:, :].to_broadcast([T, T]), ident[0:T, 0:T]).then_inc(s_key, 1)

                    def sums_of(a):
                        b, n = a.buf(), a.use()
                        pe.wait_ge(s_m, a.t + 1)
                        pe.wait_ge(s_g[b], 16 * n + 16)
                        if not a.early(2):
                            pe.wait_ge(s_tot, a.t - 1)
                        nc.tensor.matmul(sum_ps[b][0:T, :], match[b][:, 0, :], g[b][:, :],
                                         start=True, stop=False)
                        if a.early(1):
                            pe.wait_ge(s_zero, 1)
                        else:
                            pe.wait_ge(s_tot, a.t)
                        nc.tensor.matmul(sum_ps[b][0:T, :], match[b][:, 1, :], total[1 - b][:, :],
                                         start=False, stop=True).then_inc(s_sum, 1)

                    keys(Tile(None, 0, 2, ET))
                    keys(Tile(None, 1, 2, ET))
                    sums_of(Tile(None, 0, 2, ET))

                    def step(a):
                        b = a.buf()
                        pe.wait_ge(s_tot, a.t + 1)
                        if not a.early(2):
                            pe.wait_ge(s_lo, a.t - 1)
                        transpose_tile(tp[b], total[b], ident).then_inc(s_t, 1)
                        if a.later(2).exists():
                            keys(a.later(2))
                        if a.later(1).exists():
                            sums_of(a.later(1))
                        pe.wait_ge(s_lo, a.t + 1)
                        if not a.early(2):
                            pe.wait_ge(s_res, a.t - 1)
                        product(out_ps[b], hi[b], lo[b], w).then_inc(s_mm, 1)
                    tiles(pe, step, ET)

        convolve(True)
        end_part()

        with ExitStack() as ph:
            sb, ps = holder(ph)
            x1 = [sb(f"h_x1_{b}", [T, D]) for b in range(2)]
            hi = [sb(f"h_hi{b}", [P, KC, P], F32R) for b in range(2)]
            lo = [sb(f"h_lo{b}", [P, KC, P], F32R) for b in range(2)]
            nb = [sb(f"h_nb{b}", [T, D]) for b in range(2)]
            pre = [sb(f"h_pre{b}", [T, D]) for b in range(2)]
            h1 = [sb(f"h_h1{b}", [T, D]) for b in range(2)]
            pidx = [sb(f"h_idx{b}", [T, 2], I32) for b in range(2)]
            tp = [ps(f"h_tp{b}") for b in range(2)]
            out_ps = [ps(f"h_out{b}") for b in range(2)]
            h_in, h_sl, h_nb, h_store = sems("h_in"), sems("h_sl"), sems("h_nb"), sems("h_store")
            h_idx, h_t, h_hi, h_lo, h_mm, h_pre, h_out = (sem(f"h_{n}") for n in ("idx", "t", "hi", "lo", "mm", "pre", "out"))
            block = ph.enter_context(nc.Block())

            @block.sync
            def _(sp):
                def load(a):
                    b = a.buf()
                    if not a.early(2):
                        sp.wait_ge(h_t, a.t - 1)
                    sp.dma_start(x1[b][:, :], x1_rows[bass.ds(a.t * T, T), :]).then_inc(h_in[b], 16)

                load(Tile(None, 0, 2, ET))
                load(Tile(None, 1, 2, ET))

                def step(a):
                    b = a.buf()
                    if a.later(2).exists():
                        load(a.later(2))
                    sp.wait_ge(h_out, a.t + 1)
                    sp.dma_start(h1_rows[bass.ds(a.t * T, T), :], h1[b][:, :]).then_inc(h_store[b], 16)
                tiles(sp, step, ET)
                for b in range(2):
                    sp.wait_ge(h_store[b], 16 * (ET // 2))

            @block.gpsimd
            def _(pool):
                bound = {"N": pool.to_reg(N - 1), "E": pool.to_reg(E - 1)}
                def look(a):
                    b, n = a.buf(), a.use()
                    if not a.early(2):
                        pool.wait_ge(h_nb[b], 16 * n)
                        pool.wait_ge(h_pre, a.t - 1)
                    nc.gpsimd.tensor_copy(pidx[b][:, 0:1], place_i[:, SRCI, bass.ds(a.t, 1)]).then_inc(h_idx, 1)
                    nc.gpsimd.tensor_copy(nb[b][:, :], neigh_b[:, 0:D]).then_inc(h_idx, 1)
                    pool.wait_ge(h_idx, 2 * a.t + 2)
                    alone(pool)
                    pool.indirect_dma_start(pidx[b][:, 1:2], None, slot_dst, bass.IndirectOffsetOnAxis(ap=pidx[b][:, 0:1], axis=0),
                                            bounds_check=bound["N"], oob_is_err=False).then_inc(h_sl[b], 16)

                def fetch(a):
                    b, n = a.buf(), a.use()
                    pool.wait_ge(h_sl[b], 16 * n + 16)
                    alone(pool)
                    pool.indirect_dma_start(nb[b][:, :], None, neigh1, bass.IndirectOffsetOnAxis(ap=pidx[b][:, 1:2], axis=0),
                                            bounds_check=bound["E"], oob_is_err=False).then_inc(h_nb[b], 16)

                look(Tile(None, 0, 2, ET))

                def step(a):
                    if a.later(1).exists():
                        look(a.later(1))
                    fetch(a)
                tiles(pool, step, ET)

            @block.scalar
            def _(act):
                def step(a):
                    b, n = a.buf(), a.use()
                    act.wait_ge(h_t, a.t + 1)
                    if not a.early(2):
                        act.wait_ge(h_mm, a.t - 1)
                    nc.scalar.activation(hi[b][:, :, 0:T], chunks(tp[b][:, :]), ACT.Copy).then_inc(h_hi, 1)
                    act.wait_ge(h_pre, a.t + 1)
                    if not a.early(2):
                        act.wait_ge(h_store[b], 16 * n)
                    nc.scalar.activation(h1[b][:, :], pre[b][:, :], ACT.Relu).then_inc(h_out, 1)
                tiles(act, step, ET)

            @block.vector
            def _(dve):
                def low(a):
                    b = a.buf()
                    dve.wait_ge(h_hi, a.t + 1)
                    nc.vector.tensor_tensor(lo[b][:, :, 0:T], chunks(tp[b][:, :]), hi[b][:, :, 0:T].bitcast(F32), ALU.subtract).then_inc(h_lo, 1)

                def step(a):
                    b, n = a.buf(), a.use()
                    low(a)
                    dve.wait_ge(h_mm, a.t + 1)
                    dve.wait_ge(h_nb[b], 16 * n + 16)
                    if not a.early(2):
                        dve.wait_ge(h_out, a.t - 1)
                    nc.vector.scalar_tensor_tensor(pre[b][:, :], out_ps[b][0:T, :],
                                                   near[:, bass.ds(a.t, 1), DIAG - WS:DIAG - WS + 1].rearrange("p o f -> p (o f)"),
                                                   nb[b][:, :], ALU.mult, ALU.add).then_inc(h_pre, 1)
                tiles(dve, step, ET)

            @block.tensor
            def _(pe):
                def turn(a):
                    b, n = a.buf(), a.use()
                    pe.wait_ge(h_in[b], 16 * n + 16)
                    if not a.early(2):
                        pe.wait_ge(h_lo, a.t - 1)
                    transpose_tile(tp[b], x1[b], ident).then_inc(h_t, 1)

                turn(Tile(None, 0, 2, ET))

                def step(a):
                    b = a.buf()
                    if a.later(1).exists():
                        turn(a.later(1))
                    pe.wait_ge(h_lo, a.t + 1)
                    if not a.early(2):
                        pe.wait_ge(h_pre, a.t - 1)
                    product(out_ps[b], hi[b], lo[b], dense1_w).then_inc(h_mm, 1)
                tiles(pe, step, ET)

        end_part()
        convolve(False)

        end_part()
        with ExitStack() as ph:
            sb, ps = holder(ph)
            slots = sb("slots", [T, 2, NT], I32)
            diag = sb("diag", [T, 2, NT])
            xb = [sb(f"xb{b}", [T, D]) for b in range(4)]
            nb = [sb(f"nb{b}", [T, 2 * D]) for b in range(4)]
            pidx = [sb(f"n_idx{b}", [T, 2], I32) for b in range(4)]
            y = [sb(f"n_y{b}", [T, D]) for b in range(2)]
            x1 = [sb(f"n_x1_{b}", [T, D]) for b in range(4)]
            st, mv, rs = ([[sb(f"n_{n}{j}_{b}", [T, s]) for b in range(2)] for j in range(2)]
                          for n, s in (("st", 6), ("mv", 2), ("rs", 3)))
            hi1, lo1, hi2, lo2 = ([sb(f"n_{n}_{b}", [P, KC, P], F32R) for b in range(2)] for n in ("hi1", "lo1", "hi2", "lo2"))
            h1 = [sb(f"n_h1_{b}", [T, D]) for b in range(2)]
            h2 = [sb(f"n_h2_{b}", [T, D]) for b in range(2)]
            s2 = [sb(f"n_s{b}", [T, D]) for b in range(2)]
            res = [sb(f"n_res{b}", [T, D]) for b in range(2)]
            tp1, tp2, mm1, mm2 = ([ps(f"n_{n}_{b}") for b in range(2)] for n in ("tp1", "tp2", "mm1", "mm2"))
            n_in, n_u, n_nb = sems("n_in", 4), sems("n_u", 4), sems("n_nb", 4)
            n_store = sems("n_store")
            n_small, n_third, n_fill, n_idx = sem("n_small"), sem("n_third"), sem("n_fill"), sem("n_idx")
            (n_y, n_st1, n_ag1, n_dev1, n_rec1, n_off1, n_x1, n_t1, n_hi1, n_lo1, n_mm1, n_h1, n_t2, n_hi2, n_lo2, n_mm2,
             n_h2, n_s, n_st2, n_ag2, n_dev2, n_rec2, n_off2, n_res) = (
                sem(f"n_{n}") for n in ("y", "st1", "ag1", "dev1", "rec1", "off1", "x1", "t1", "hi1", "lo1", "mm1", "h1", "t2", "hi2",
                                        "lo2", "mm2", "h2", "s", "st2", "ag2", "dev2", "rec2", "off2", "res"))
            block = ph.enter_context(nc.Block())
            UN = 4

            def tile_rows(table, a):
                return table.rearrange("(p t) d -> p t d", p=T)[:, bass.ds(a.t, 1), :].rearrange("p o d -> p (o d)")

            @block.sync
            def _(sp):
                def load(a):
                    b4 = a.buf(4)
                    if not a.early(4):
                        sp.wait_ge(n_y, a.t - 3)
                    sp.dma_start(xb[b4][:, :], tile_rows(x, a)).then_inc(n_in[b4], 16)

                def store(a):
                    b = a.buf()
                    sp.wait_ge(n_res, a.t + 1)
                    sp.dma_start(tile_rows(out, a), res[b][:, :]).then_inc(n_store[b], 16)

                sp.dma_start(slots[:, 0, :], slot_src.rearrange("(p t) o -> p (t o)", p=T)).then_inc(n_small, 16)
                sp.dma_start(slots[:, 1, :], slot_dst.rearrange("(p t) o -> p (t o)", p=T)).then_inc(n_small, 16)
                sp.dma_start(diag[:, 0, :], node_vec.rearrange("(p t) -> p t", p=T)).then_inc(n_small, 16)

                def step(a):
                    at(load, a.later(4))
                    at(store, a.later(-4))
                tiles(sp, step, NT, UN, before=4, after=4)
                for b in range(2):
                    sp.wait_ge(n_store[b], 16 * (NT // 2))

            @block.gpsimd
            def _(pool):
                bound = {"N": pool.to_reg(N - 1), "E": pool.to_reg(E - 1)}
                pool.wait_ge(n_small, 48)

                def fetch_x(a):
                    n, b4 = a.use(4), a.buf(4)
                    if not a.early(4):
                        pool.wait_ge(n_u[b4], 16 * n)
                        pool.wait_ge(n_nb[b4], 16 * n)
                    nc.gpsimd.tensor_copy(pidx[b4][:, :], slots[:, :, bass.ds(a.t, 1)].rearrange("p j o -> p (j o)")).then_inc(n_idx, 1)
                    pool.wait_ge(n_idx, a.t + 1)
                    pool.wait_ge(n_in[b4], 16 * n + 16)
                    alone(pool)
                    pool.indirect_dma_start(xb[b4][:, :], None, x_new, bass.IndirectOffsetOnAxis(ap=pidx[b4][:, 0:1], axis=0),
                                            bounds_check=bound["E"], oob_is_err=False).then_inc(n_u[b4], 16)

                def fetch_nb(a):
                    b4 = a.buf(4)
                    pool.wait_ge(n_fill, a.t + 1)
                    alone(pool)
                    pool.indirect_dma_start(nb[b4][:, :], None, neigh, bass.IndirectOffsetOnAxis(ap=pidx[b4][:, 1:2], axis=0),
                                            bounds_check=bound["E"], oob_is_err=False).then_inc(n_nb[b4], 16)

                def add(a):
                    b, n, b4 = a.buf(), a.use(4), a.buf(4)
                    pool.wait_ge(n_u[b4], 16 * n + 16)
                    if not a.early(2):
                        pool.wait_ge(n_x1, a.t - 1)
                    nc.gpsimd.tensor_tensor(y[b][:, :], xb[b4][:, :], half_c[:, :], ALU.add).then_inc(n_y, 1)

                def step(a):
                    at(fetch_x, a.later(1))
                    at(add, a)
                    at(fetch_nb, a.later(-1))
                tiles(pool, step, NT, UN, before=1, after=1)

            @block.scalar
            def _(act):
                def dev1(a):
                    b = a.buf()
                    act.wait_ge(n_ag1, a.t + 1)
                    if not a.early(2):
                        act.wait_ge(n_rec1, a.t - 1)
                    nc.scalar.activation(rs[0][b][:, 0:1], mv[0][b][:, 1:2], ACT.Sqrt, bias=eps[0:T, 1:2]).then_inc(n_dev1, 1)

                def norm1(a):
                    b, b4 = a.buf(), a.buf(4)
                    act.wait_ge(n_off1, a.t + 1)
                    if not a.early(4):
                        act.wait_ge(n_s, a.t - 3)
                    nc.scalar.activation(x1[b4][:, :], y[b][:, :], ACT.Identity, scale=rs[0][b][:, 1:2], bias=rs[0][b][:, 2:3])\
                        .then_inc(n_x1, 1)

                def fill(a):
                    b4 = a.buf(4)
                    if not a.early(4):
                        act.wait_ge(n_h2, a.t - 3)
                    nc.scalar.activation(nb[b4][:, :], neigh_b[:, :], ACT.Copy).then_inc(n_fill, 1)

                def high1(a):
                    b = a.buf()
                    act.wait_ge(n_t1, a.t + 1)
                    if not a.early(2):
                        act.wait_ge(n_mm1, a.t - 1)
                    nc.scalar.activation(hi1[b][:, :, 0:T], chunks(tp1[b][:, :]), ACT.Copy).then_inc(n_hi1, 1)

                def high2(a):
                    b = a.buf()
                    act.wait_ge(n_t2, a.t + 1)
                    if not a.early(2):
                        act.wait_ge(n_mm2, a.t - 1)
                    nc.scalar.activation(hi2[b][:, :, 0:T], chunks(tp2[b][:, :]), ACT.Relu).then_inc(n_hi2, 1)

                def dev2(a):
                    b = a.buf()
                    act.wait_ge(n_ag2, a.t + 1)
                    if not a.early(2):
                        act.wait_ge(n_rec2, a.t - 1)
                    nc.scalar.activation(rs[1][b][:, 0:1], mv[1][b][:, 1:2], ACT.Sqrt, bias=eps[0:T, 2:3]).then_inc(n_dev2, 1)

                def finish(a):
                    b, n = a.buf(), a.use()
                    act.wait_ge(n_off2, a.t + 1)
                    if not a.early(2):
                        act.wait_ge(n_store[b], 16 * n)
                    nc.scalar.activation(res[b][:, :], s2[b][:, :], ACT.Identity, scale=rs[1][b][:, 1:2], bias=rs[1][b][:, 2:3])\
                        .then_inc(n_res, 1)

                def step(a):
                    at(high2, a.later(-1))
                    at(dev2, a.later(-2))
                    at(dev1, a.later(2))
                    at(fill, a.later(2))
                    at(high1, a.later(1))
                    at(finish, a.later(-2))
                    at(norm1, a.later(2))
                tiles(act, step, NT, UN, before=2, after=2)

            @block.vector
            def _(dve):
                dve.wait_ge(n_small, 48)
                nc.vector.tensor_scalar(diag[:, 1, :], diag[:, 0, :], 1.0 / 3.0, None, ALU.mult).then_inc(n_third, 1)
                dve.wait_ge(n_third, 1)

                def stats1(a):
                    b = a.buf()
                    dve.wait_ge(n_y, a.t + 1)
                    nc.vector.bn_stats(st[0][b][:, :], y[b][:, :]).then_inc(n_st1, 1)
                    dve.wait_ge(n_st1, a.t + 1)
                    if not a.early(2):
                        dve.wait_ge(n_x1, a.t - 1)
                    alone(dve)
                    nc.vector.bn_aggr(mv[0][b][:, :], st[0][b][:, :]).then_inc(n_ag1, 1)

                def scale1(a):
                    b = a.buf()
                    dve.wait_ge(n_dev1, a.t + 1)
                    if not a.early(2):
                        dve.wait_ge(n_x1, a.t - 1)
                    nc.vector.reciprocal(rs[0][b][:, 1:2], rs[0][b][:, 0:1]).then_inc(n_rec1, 1)
                    dve.wait_ge(n_rec1, a.t + 1)
                    nc.vector.tensor_scalar(rs[0][b][:, 2:3], mv[0][b][:, 0:1], rs[0][b][:, 1:2], -1.0, ALU.mult, ALU.mult)\
                        .then_inc(n_off1, 1)

                def low1(a):
                    b = a.buf()
                    dve.wait_ge(n_hi1, a.t + 1)
                    nc.vector.tensor_tensor(lo1[b][:, :, 0:T], chunks(tp1[b][:, :]), hi1[b][:, :, 0:T].bitcast(F32), ALU.subtract)\
                        .then_inc(n_lo1, 1)

                def hidden(a):
                    b, b4 = a.buf(), a.buf(4)
                    dve.wait_ge(n_mm1, a.t + 1)
                    dve.wait_ge(n_nb[b4], 16 * a.use(4) + 16)
                    if not a.early(2):
                        dve.wait_ge(n_t2, a.t - 1)
                    nc.vector.scalar_tensor_tensor(h1[b][:, :], mm1[b][0:T, :], diag[:, 0, bass.ds(a.t, 1)], nb[b4][:, 0:D],
                                                   ALU.mult, ALU.add).then_inc(n_h1, 1)

                def low2(a):
                    b = a.buf()
                    dve.wait_ge(n_hi2, a.t + 1)
                    nc.vector.scalar_tensor_tensor(lo2[b][:, :, 0:T], chunks(tp2[b][:, :]), 0.0, hi2[b][:, :, 0:T].bitcast(F32),
                                                   ALU.max, ALU.subtract).then_inc(n_lo2, 1)

                def sum2(a):
                    b, b4 = a.buf(), a.buf(4)
                    dve.wait_ge(n_mm2, a.t + 1)
                    nc.vector.scalar_tensor_tensor(h2[b][:, :], mm2[b][0:T, :], diag[:, 1, bass.ds(a.t, 1)], nb[b4][:, D:2 * D],
                                                   ALU.mult, ALU.add).then_inc(n_h2, 1)
                    dve.wait_ge(n_h2, a.t + 1)
                    if not a.early(2):
                        dve.wait_ge(n_res, a.t - 1)
                    nc.vector.scalar_tensor_tensor(s2[b][:, :], h2[b][:, :], 0.0, x1[b4][:, :], ALU.max, ALU.add).then_inc(n_s, 1)
                    dve.wait_ge(n_s, a.t + 1)
                    nc.vector.bn_stats(st[1][b][:, :], s2[b][:, :]).then_inc(n_st2, 1)
                    dve.wait_ge(n_st2, a.t + 1)
                    alone(dve)
                    nc.vector.bn_aggr(mv[1][b][:, :], st[1][b][:, :]).then_inc(n_ag2, 1)

                def scale2(a):
                    b = a.buf()
                    dve.wait_ge(n_dev2, a.t + 1)
                    if not a.early(2):
                        dve.wait_ge(n_res, a.t - 1)
                    nc.vector.reciprocal(rs[1][b][:, 1:2], rs[1][b][:, 0:1]).then_inc(n_rec2, 1)
                    dve.wait_ge(n_rec2, a.t + 1)
                    nc.vector.tensor_scalar(rs[1][b][:, 2:3], mv[1][b][:, 0:1], rs[1][b][:, 1:2], -1.0, ALU.mult, ALU.mult)\
                        .then_inc(n_off2, 1)

                def step(a):
                    at(low2, a.later(-1))
                    at(sum2, a.later(-2))
                    at(stats1, a.later(2))
                    at(hidden, a)
                    at(scale2, a.later(-2))
                    at(scale1, a.later(2))
                    at(low1, a.later(1))
                tiles(dve, step, NT, UN, before=2, after=2)

            @block.tensor
            def _(pe):
                def turn1(a):
                    b = a.buf()
                    pe.wait_ge(n_x1, a.t + 1)
                    if not a.early(2):
                        pe.wait_ge(n_lo1, a.t - 1)
                    transpose_tile(tp1[b], x1[a.buf(4)], ident).then_inc(n_t1, 1)

                def dense1(a):
                    b = a.buf()
                    pe.wait_ge(n_lo1, a.t + 1)
                    if not a.early(2):
                        pe.wait_ge(n_h1, a.t - 1)
                    product(mm1[b], hi1[b], lo1[b], dense1_w).then_inc(n_mm1, 1)

                def turn2(a):
                    b = a.buf()
                    pe.wait_ge(n_h1, a.t + 1)
                    if not a.early(2):
                        pe.wait_ge(n_lo2, a.t - 1)
                    transpose_tile(tp2[b], h1[b], ident).then_inc(n_t2, 1)

                def dense2(a):
                    b = a.buf()
                    pe.wait_ge(n_lo2, a.t + 1)
                    if not a.early(2):
                        pe.wait_ge(n_h2, a.t - 1)
                    product(mm2[b], hi2[b], lo2[b], dense2_w).then_inc(n_mm2, 1)

                def step(a):
                    at(dense1, a)
                    at(turn1, a.later(1))
                    at(dense2, a.later(-1))
                    at(turn2, a)
                tiles(pe, step, NT, UN, before=1, after=1)


_INS = ['x', 'src', 'dst', 'edge_attr_8', 'edge_weight', 'node_vec',
        'L0_gnn_ln_g', 'L0_gnn_ln_b', 'L0_gnn_Wq', 'L0_gnn_bq', 'L0_gnn_Wk', 'L0_gnn_bk', 'L0_gnn_Wv', 'L0_gnn_bv',
        'L0_gnn_W1', 'L0_gnn_b1', 'L0_gnn_W2', 'L0_gnn_b2',
        'L1_gnn_W0_1', 'L1_gnn_W1_1', 'L1_gnn_b1', 'L1_gnn_W0_2', 'L1_gnn_W1_2', 'L1_gnn_b2']


def kernel(**inputs):
    import numpy as _np
    import concourse.bacc as _bacc
    from concourse import mybir as _mybir
    from concourse.bass_utils import run_bass_kernel_spmd as _run

    nc = _bacc.Bacc("TRN2", target_bir_lowering=False, num_devices=1)
    arrays, args = {}, []
    for name in _INS:
        a = _np.ascontiguousarray(inputs[name])
        arrays[f"in_{name}"] = a
        args.append(nc.dram_tensor(f"in_{name}", a.shape, _mybir.dt.from_np(a.dtype), kind="ExternalInput").ap())
    shape = inputs['x'].shape
    args.append(nc.dram_tensor("out_0", shape, _mybir.dt.float32, kind="ExternalOutput").ap())
    build(nc, *args)
    r = _run(nc, [arrays], core_ids=[0])
    return r.results[0]["out_0"]
```

```python
from contextlib import ExitStack

import concourse.bass as bass
from concourse import mybir

ALU = mybir.AluOpType
ACT = mybir.ActivationFunctionType
AX = mybir.AxisListType
F32 = mybir.dt.float32
F32R = mybir.dt.float32r
BF16 = mybir.dt.bfloat16
I32 = mybir.dt.int32

P = 128
D = 512
KC = D // P
H = 8
HD = D // H
T = 125
EPS = 1e-5
FAR = 1000000
GAP = -3.0e38

WS = D
SRC, DST, EW, RANKB, DIAG = WS + H, WS + H + 1, WS + H + 2, WS + H + 3, WS + H + 4
ROW = DIAG + 4
FIELDS = ROW - WS


class Tile:

    def __init__(self, turn, c, unroll, count):
        self.turn, self.c, self.unroll, self.count = turn, c, unroll, count
        self.t = c if turn is None else turn * unroll + c

    def later(self, k):
        return Tile(self.turn, self.c + k, self.unroll, self.count)

    def buf(self, m=2):
        return self.c % m

    def use(self, m=2):
        return self.c // m if self.turn is None else self.turn * (self.unroll // m) + self.c // m

    def early(self, k):
        return self.turn is None and self.c < k

    def exists(self):
        return self.turn is not None or 0 <= self.c < self.count


def tiles(eng, step, count, unroll=2, before=0, after=0):
    for c in range(-before, unroll):
        step(Tile(None, c, unroll, count))
    with eng.Fori(1, count // unroll - 1) as turn:
        for c in range(unroll):
            step(Tile(turn, c, unroll, count))
    for c in range(count - unroll, count + after):
        step(Tile(None, c, unroll, count))


def at(part, a):
    if a.exists():
        part(a)


def alone(eng):
    eng.nop(nofuse=True)


def build(nc, x, src, dst, attr, ew, node_vec, ln_g, ln_b, wq, bq, wk, bk, wv, bv, w1, b1, w2, b2,
          w01, w11, gb1, w02, w12g, gb2, out):
    N = x.shape[0]
    E = src.shape[0]
    NT, ET = N // T, E // T
    SCALE = HD ** -0.5
    CENTRE = N * E // 2

    def dram(name, shape, dt):
        return nc.dram_tensor(name, shape, dt, kind="Internal").ap()

    by_src = dram("by_src", (E, ROW), F32)
    x_by_src = dram("x_by_src", (E, D), F32)
    by_dst = dram("by_dst", (E + 1, 4), F32)
    x_new = dram("x_new", (E, D), F32)
    z_rows = dram("z_rows", (E, D), F32)
    z2_rows = dram("z2_rows", (E, D), F32)
    neigh = dram("neigh", (E, 2 * D), F32)
    neigh1 = dram("neigh1", (E, D), F32)
    slot_src = dram("slot_src", (N, 1), I32)
    slot_dst = dram("slot_dst", (N, 1), I32)
    src_col = src.rearrange("(p t) -> p t", p=T)
    dst_col = dst.rearrange("(p t) -> p t", p=T)
    ew_col = ew.rearrange("(p t) -> p t", p=T)
    vec_rows = node_vec.rearrange("(n o) -> n o", o=1)

    whole = ExitStack()

    def holder(stack):
        def sb(name, shape, dt=F32):
            return stack.enter_context(nc.sbuf_tensor(name, shape, dt))

        def ps(name, shape=(P, D)):
            return stack.enter_context(nc.psum_tensor(name, list(shape), F32))
        return sb, ps

    part_sems = []

    def sem(name):
        part_sems.append(nc.alloc_semaphore(name))
        return part_sems[-1]

    def end_part():
        nc.clear_and_free_semaphores(part_sems)
        nc.all_engine_barrier()
        part_sems.clear()

    def sems(name, n=2):
        return [sem(f"{name}_buf{i}") for i in range(n)]

    def weight_rows(w):
        return w.rearrange("(k p) n -> p k n", p=P)

    def columns(v):
        return v.rearrange("(k p) -> p k", p=P)

    def row_for_all(v, n=T):
        return v.rearrange("(o d) -> o d", o=1).to_broadcast([n, v.shape[0]])

    def chunks(a):
        return a.rearrange("p (k c) -> p k c", k=KC)[:, :, 0:T]

    def transpose_tile(bank, rows, ident):
        for k in range(KC):
            last = nc.tensor.transpose(bank[:, P * k:P * k + T], rows[:, P * k:P * (k + 1)], ident[0:T, 0:T])
        return last

    def product(bank, hi, lo, w):
        w_hi, w_lo = w
        n = 0
        for k in range(KC):
            for a, b in ((hi, w_hi), (hi, w_lo), (lo, w_hi)):
                last = nc.tensor.matmul(bank[0:T, :], a[:, k, 0:T], b[:, k, :], start=(n == 0), stop=(n == 3 * KC - 1))
                n += 1
        return last

    whole.enter_context(nc.allow_non_contiguous_dma(reason="small columns"))
    with whole:
        sb, _ = holder(whole)
        ident = sb("ident", [P, P])
        eps = sb("eps", [P, 3])
        conv2_w = [sb(f"w_slot0_{p}", [P, KC, D], F32R) for p in ("hi", "lo")]
        dense2_w = [sb(f"w_slot1_{p}", [P, KC, D], F32R) for p in ("hi", "lo")]
        q_w, k_w = conv2_w, dense2_w
        attn_w = [sb(f"w_attn_{p}", [P, KC, D], F32R) for p in ("hi", "lo")]
        dense1_w = [sb(f"w_dense1_{p}", [P, KC, D], F32R) for p in ("hi", "lo")]
        conv1_w = [sb(f"w_conv1_{p}", [P, KC, D], F32R) for p in ("hi", "lo")]
        half_c = sb("half_c", [T, D])
        neigh_b = sb("neigh_b", [T, 2 * D])

        with ExitStack() as ph:
            sb, ps = holder(ph)
            v_w = [sb(f"w_v_{p}", [P, KC, D], F32R) for p in ("hi", "lo")]
            q_bias, k_bias, v_bias = (sb(f"{n}_bias", [T, D]) for n in "qkv")
            edge_i = sb("edge_i", [T, 2, ET], I32)
            edge_f = sb("edge_f", [T, 3, ET])
            attr_s = sb("attr_s", [T, ET, H])
            key_row = sb("key_row", [T, 2, E])
            key_col = sb("key_col", [T, 2, ET])
            sums = sb("sums", [T, 2, ET])

            with ExitStack() as ph0:
                sb0, ps0 = holder(ph0)
                stage = [sb0(f"stage{i}", [P, KC, D]) for i in range(2)]
                gain = sb0("gain", [P, KC])
                shift = sb0("shift", [P, KC])
                node_row = sb0("node_row", [T, E], I32)
                number = sb0("number", [T, E], I32)
                number_c = sb0("number_c", [T, ET], I32)
                far = sb0("far", [T, NT], I32)
                sentinel = sb0("sentinel", [1, 4])
                bias_ps = [ps0(f"bias_ps{i}") for i in range(2)]
                w_in = sems("w_in")
                small_in, rows_in = sem("small_in"), sem("rows_in")
                bias_in = sem("bias_in")
                made, ident0, ident1 = sem("made"), sem("ident0"), sem("ident1")
                w_high, w_done, bias_mm, bias_done = sem("w_high"), sem("w_done"), sem("bias_mm"), sem("bias_done")
                keys_done, far_out = sem("keys_done"), sem("far_out")
                block = nc.Block()
                block = ph0.enter_context(block)

                @block.sync
                def _(sp):
                    sp.dma_start(gain[:, :], columns(ln_g)).then_inc(small_in, 16)
                    sp.dma_start(shift[:, :], columns(ln_b)).then_inc(small_in, 16)
                    for i, w in enumerate((wq, wk, wv)):
                        if i >= 2:
                            sp.wait_ge(w_done, i - 1)
                            sp.wait_ge(bias_mm, i - 1)
                        sp.dma_start(stage[i % 2][:, :, :], weight_rows(w)).then_inc(w_in[i % 2], 16)
                    sp.wait_ge(made, 4)
                    sp.dma_start(slot_src.rearrange("(p t) o -> p (t o)", p=T), far[:, :]).then_inc(far_out, 16)
                    sp.dma_start(slot_dst.rearrange("(p t) o -> p (t o)", p=T), far[:, :]).then_inc(far_out, 16)
                    sp.dma_start(by_dst[E:E + 1, :], sentinel[:, :]).then_inc(far_out, 16)
                    sp.wait_ge(far_out, 48)

                @block.scalar
                def _(act):
                    act.dma_start(node_row[:, :], row_for_all(src)).then_inc(rows_in, 16)
                    act.dma_start(edge_i[:, 0, :], src_col).then_inc(small_in, 16)
                    act.dma_start(edge_i[:, 1, :], dst_col).then_inc(small_in, 16)
                    act.dma_start(edge_f[:, 2, :], ew_col).then_inc(small_in, 16)
                    act.dma_start(attr_s[:, :, :], attr.rearrange("(p t) h -> p t h", p=T)).then_inc(small_in, 16)
                    for b, v in ((q_bias, bq), (k_bias, bk), (v_bias, bv)):
                        act.dma_start(b[:, :], row_for_all(v)).then_inc(bias_in, 16)
                    act.wait_ge(keys_done, 1)
                    act.dma_start(node_row[:, :], row_for_all(dst)).then_inc(rows_in, 16)
                    act.wait_ge(small_in, 96)
                    for i, w in enumerate((q_w, k_w, v_w)):
                        act.wait_ge(w_in[i % 2], 16 * (i // 2 + 1))
                        for k in range(KC):
                            last = nc.scalar.activation(w[0][:, k, :], stage[i % 2][:, k, :], ACT.Copy, scale=gain[:, k:k + 1])
                        last.then_inc(w_high, 1)

                @block.gpsimd
                def _(pool):
                    nc.gpsimd.memset(ident[:, :], 0.0).then_inc(ident0, 1)
                    nc.gpsimd.iota(number[:, :], [[1, E]], base=-CENTRE, channel_multiplier=0).then_inc(made, 1)
                    nc.gpsimd.iota(number_c[:, :], [[1, ET]], base=-CENTRE, channel_multiplier=ET).then_inc(made, 1)
                    nc.gpsimd.iota(far[:, :], [[0, NT]], base=FAR, channel_multiplier=0).then_inc(made, 1)
                    nc.gpsimd.memset(sentinel[:, :], -1.0).then_inc(made, 1)
                    pool.wait_ge(ident0, 1)
                    nc.gpsimd.affine_select(out=ident[:, :], in_=ident[:, :], compare_op=ALU.not_equal, fill=1.0,
                                            base=0, pattern=[[-1, P]], channel_multiplier=1).then_inc(ident1, 1)

                @block.vector
                def _(dve):
                    for i, v in enumerate((EPS, EPS / 4, EPS / 2.25)):
                        nc.vector.memset(eps[:, i:i + 1], v)
                    dve.wait_ge(made, 3)
                    dve.wait_ge(rows_in, 16)
                    nc.vector.scalar_tensor_tensor(key_row[:, 0, :], node_row[:, :], float(E), number[:, :],
                                                   ALU.mult, ALU.add).then_inc(keys_done, 1)
                    dve.wait_ge(small_in, 96)
                    for j in range(2):
                        nc.vector.scalar_tensor_tensor(key_col[:, j, :], edge_i[:, j, :], float(E), number_c[:, :],
                                                       ALU.mult, ALU.add)
                        nc.vector.tensor_copy(edge_f[:, j, :], edge_i[:, j, :])
                    for i, w in enumerate((q_w, k_w, v_w)):
                        dve.wait_ge(w_high, i + 1)
                        for k in range(KC):
                            last = nc.vector.scalar_tensor_tensor(
                                w[1][:, k, :], stage[i % 2][:, k, :], gain[:, k:k + 1],
                                w[0][:, k, :].bitcast(F32), ALU.mult, ALU.subtract)
                        last.then_inc(w_done, 1)
                        if i == 0:
                            dve.wait_ge(rows_in, 32)
                            nc.vector.scalar_tensor_tensor(key_row[:, 1, :], node_row[:, :], float(E), number[:, :],
                                                           ALU.mult, ALU.add)
                        dve.wait_ge(bias_mm, i + 1)
                        if i == 0:
                            dve.wait_ge(bias_in, 48)
                        b = (q_bias, k_bias, v_bias)[i]
                        nc.vector.tensor_tensor(b[:, :], bias_ps[i % 2][0:T, :], b[:, :], ALU.add).then_inc(bias_done, 1)

                @block.tensor
                def _(pe):
                    pe.wait_ge(small_in, 96)
                    for i in range(3):
                        pe.wait_ge(w_in[i % 2], 16 * (i // 2 + 1))
                        if i >= 2:
                            pe.wait_ge(bias_done, i - 1)
                        for k in range(KC):
                            last = nc.tensor.matmul(bias_ps[i % 2][0:T, :], shift[:, k:k + 1].to_broadcast([P, T]),
                                                    stage[i % 2][:, k, :], start=(k == 0), stop=(k == KC - 1))
                        last.then_inc(bias_mm, 1)

            end_part()
            with ExitStack() as ph1:
                sb1, ps1 = holder(ph1)
                xg = [[sb1(f"xg{j}_{b}", [T, D]) for b in range(4)] for j in range(2)]
                dg = [sb1(f"dg{b}", [T, 1]) for b in range(4)]
                diag_col = sb1("diag_col", [T, ET])
                row = [sb1(f"row{b}", [T, ROW]) for b in range(2)]
                idx = [sb1(f"idx{b}", [T, 2], I32) for b in range(4)]
                rank_i = [sb1(f"rank_i{b}", [T, 1], I32) for b in range(4)]
                st = [sb1(f"st{b}", [T, 2, 6]) for b in range(2)]
                mv = [sb1(f"mv{b}", [T, 2, 2]) for b in range(2)]
                rs = [sb1(f"rs{b}", [T, 2, 2]) for b in range(2)]
                xh = [[sb1(f"xh{j}_{b}", [T, D]) for b in range(2)] for j in range(2)]
                hi = [[sb1(f"p_hi{j}_{b}", [P, KC, P], F32R) for b in range(2)] for j in range(2)]
                lo = [[sb1(f"p_lo{j}_{b}", [P, KC, P], F32R) for b in range(2)] for j in range(2)]
                qs, ks, qk = ([sb1(f"{n}{b}", [T, D]) for b in range(2)] for n in ("qs", "ks", "qk"))
                score = [sb1(f"score{b}", [T, H]) for b in range(2)]
                waste = sb1("waste", [T, 2, E], BF16)
                tp = [ps1(f"p_tp{j}") for j in range(2)]
                qkv = [[ps1(f"p_{n}{b}") for b in range(2)] for n in "qkv"]
                got_x = [sems("got_xs", 4), sems("got_xd", 4)]
                got_diag, sent_x, sent_row = sems("got_diag", 4), sems("sent_x", 4), sems("sent_row", 4)
                p_idx, p_place, p_dg = sem("p_idx"), sem("p_place"), sem("p_dg")
                p_stats, p_aggr, p_dev, p_rec, p_xh = sem("p_stats"), sem("p_aggr"), sem("p_dev"), sem("p_rec"), sem("p_xh")
                p_t, p_hi, p_lo = sem("p_t"), sem("p_hi"), sem("p_lo")
                p_mm = [sem(f"p_mm_{n}") for n in "qkv"]
                p_q, p_k, p_v, p_qk, p_sc, p_row = sem("p_q"), sem("p_k"), sem("p_v"), sem("p_qk"), sem("p_sc"), sem("p_row")
                p_rank = [sem("p_rank_src"), sem("p_rank_dst")]
                UN = 4
                block = ph1.enter_context(nc.Block())

                @block.gpsimd
                def _(pool):
                    bound = {"N": pool.to_reg(N - 1), "E": pool.to_reg(E - 1)}

                    def fetch(a):
                        b4, n = a.buf(4), a.use(4)
                        if not a.early(4):
                            pool.wait_ge(sent_x[b4], 16 * n)
                            pool.wait_ge(p_xh, a.t - 3)
                            pool.wait_ge(p_dg, a.t - 3)
                            pool.wait_ge(got_diag[b4], 16 * n)
                            pool.wait_ge(got_x[0][b4], 16 * n)
                            pool.wait_ge(got_x[1][b4], 16 * n)
                        nc.gpsimd.tensor_copy(idx[b4][:, :], edge_i[:, :, bass.ds(a.t, 1)].rearrange("p j o -> p (j o)"))\
                            .then_inc(p_idx, 1)
                        pool.wait_ge(p_idx, a.t + 1)
                        for j in range(2):
                            alone(pool)
                            pool.indirect_dma_start(xg[j][b4][:, :], None, x,
                                                    bass.IndirectOffsetOnAxis(ap=idx[b4][:, j:j + 1], axis=0),
                                                    bounds_check=bound["N"], oob_is_err=False).then_inc(got_x[j][b4], 16)
                        alone(pool)
                        pool.indirect_dma_start(dg[b4][:, :], None, vec_rows, bass.IndirectOffsetOnAxis(ap=idx[b4][:, 0:1], axis=0),
                                                bounds_check=bound["N"], oob_is_err=False).then_inc(got_diag[b4], 16)

                    def send_x(a):
                        b4 = a.buf(4)
                        pool.wait_ge(p_place, a.t + 1)
                        pool.wait_ge(got_x[0][b4], 16 * a.use(4) + 16)
                        alone(pool)
                        pool.indirect_dma_start(x_by_src, bass.IndirectOffsetOnAxis(ap=rank_i[b4][:, :], axis=0), xg[0][b4][:, :], None,
                                                bounds_check=bound["E"], oob_is_err=False).then_inc(sent_x[b4], 16)

                    def multiply(a):
                        b = a.buf()
                        pool.wait_ge(p_k, a.t + 1)
                        if not a.early(2):
                            pool.wait_ge(p_sc, a.t - 1)
                        nc.gpsimd.tensor_tensor(qk[b][:, :], qs[b][:, :], ks[b][:, :], ALU.mult).then_inc(p_qk, 1)

                    def send_row(a):
                        b, b4 = a.buf(), a.buf(4)
                        pool.wait_ge(p_row, a.t + 1)
                        alone(pool)
                        pool.indirect_dma_start(by_src, bass.IndirectOffsetOnAxis(ap=rank_i[b4][:, :], axis=0), row[b][:, :], None,
                                                bounds_check=bound["E"], oob_is_err=False).then_inc(sent_row[b4], 16)

                    def step(a):
                        at(multiply, a.later(-1))
                        at(fetch, a.later(4))
                        at(send_x, a.later(2))
                        at(send_row, a.later(-1))
                    tiles(pool, step, ET, UN, before=4, after=1)
                    for b4 in range(4):
                        pool.wait_ge(sent_row[b4], 16 * (ET // 4))
                        pool.wait_ge(sent_x[b4], 16 * (ET // 4))

                @block.scalar
                def _(act):
                    def high(a):
                        b = a.buf()
                        act.wait_ge(p_t, a.t + 1)
                        if not a.early(2):
                            act.wait_ge(p_mm[2], a.t - 1)
                        nc.scalar.activation(hi[0][b][:, :, 0:T], chunks(tp[0][:, :]), ACT.Copy)
                        nc.scalar.activation(hi[1][b][:, :, 0:T], chunks(tp[1][:, :]), ACT.Copy).then_inc(p_hi, 1)

                    def deviation(a):
                        b = a.buf()
                        act.wait_ge(p_aggr, a.t + 1)
                        if not a.early(2):
                            act.wait_ge(p_rec, a.t - 1)
                        nc.scalar.activation(rs[b][:, :, 0:1], mv[b][:, :, 1:2], ACT.Sqrt, bias=eps[0:T, 0:1]).then_inc(p_dev, 1)

                    def rank(a, j):
                        if not a.early(1):
                            act.wait_ge(p_rank[j], a.t)
                        nc.scalar.activation(waste[:, j, :], key_row[:, j, :], ACT.Sign, scale=-1.0,
                                             bias=key_col[:, j, bass.ds(a.t, 1)],
                                             accum_out=sums[:, j, bass.ds(a.t, 1)]).then_inc(p_rank[j], 1)

                    def rank_src(a):
                        rank(a, 0)

                    def rank_dst(a):
                        rank(a, 1)

                    def step(a):
                        at(deviation, a.later(3))
                        at(rank_src, a.later(2))
                        at(high, a.later(1))
                        at(rank_dst, a.later(2))
                    tiles(act, step, ET, UN, before=3)

                @block.vector
                def _(dve):
                    def stats(a):
                        b, b4, n = a.buf(), a.buf(4), a.use(4)
                        for j in range(2):
                            dve.wait_ge(got_x[j][b4], 16 * n + 16)
                            nc.vector.bn_stats(st[b][:, j, :], xg[j][b4][:, :]).then_inc(p_stats, 1)

                    def moments(a):
                        b = a.buf()
                        for j in range(2):
                            dve.wait_ge(p_stats, 2 * a.t + 1 + j)
                            alone(dve)
                            last = nc.vector.bn_aggr(mv[b][:, j, :], st[b][:, j, :])
                        last.then_inc(p_aggr, 1)

                    def keep_diag(a):
                        b4, n = a.buf(4), a.use(4)
                        dve.wait_ge(got_diag[b4], 16 * n + 16)
                        nc.vector.tensor_copy(diag_col[:, bass.ds(a.t, 1)], dg[b4][:, :]).then_inc(p_dg, 1)

                    def reciprocal(a):
                        b = a.buf()
                        dve.wait_ge(p_dev, a.t + 1)
                        nc.vector.reciprocal(rs[b][:, :, 1:2], rs[b][:, :, 0:1]).then_inc(p_rec, 1)

                    def norm(a):
                        b, b4 = a.buf(), a.buf(4)
                        dve.wait_ge(p_rec, a.t + 1)
                        if not a.early(2):
                            dve.wait_ge(p_t, a.t - 1)
                        for j in range(2):
                            last = nc.vector.tensor_scalar(xh[j][b][:, :], xg[j][b4][:, :], mv[b][:, j, 0:1], rs[b][:, j, 1:2],
                                                           ALU.subtract, ALU.mult)
                        last.then_inc(p_xh, 1)

                    def low(a):
                        b = a.buf()
                        dve.wait_ge(p_hi, a.t + 1)
                        for j in range(2):
                            last = nc.vector.tensor_tensor(lo[j][b][:, :, 0:T], chunks(tp[j][:, :]), hi[j][b][:, :, 0:T].bitcast(F32),
                                                           ALU.subtract)
                        last.then_inc(p_lo, 1)

                    def place(a):
                        b4, n = a.buf(4), a.use(4)
                        dve.wait_ge(p_rank[0], a.t + 1)
                        if not a.early(4):
                            dve.wait_ge(sent_row[b4], 16 * n)
                            dve.wait_ge(sent_x[b4], 16 * n)
                        nc.vector.tensor_scalar(rank_i[b4][:, :], sums[:, 0, bass.ds(a.t, 1)], float(E - 1), 0.5, ALU.add, ALU.mult)\
                            .then_inc(p_place, 1)

                    def q_rows(a):
                        b = a.buf()
                        dve.wait_ge(p_mm[0], a.t + 1)
                        if not a.early(2):
                            dve.wait_ge(p_qk, a.t - 1)
                        nc.vector.tensor_tensor(qs[b][:, :], qkv[0][b][0:T, :], q_bias[:, :], ALU.add).then_inc(p_q, 1)

                    def k_rows(a):
                        b = a.buf()
                        dve.wait_ge(p_mm[1], a.t + 1)
                        nc.vector.tensor_tensor(ks[b][:, :], qkv[1][b][0:T, :], k_bias[:, :], ALU.add).then_inc(p_k, 1)

                    def v_rows(a):
                        b = a.buf()
                        dve.wait_ge(p_mm[2], a.t + 1)
                        if not a.early(2):
                            o = a.later(-2)
                            dve.wait_ge(sent_row[o.buf(4)], 16 * o.use(4) + 16)
                        nc.vector.tensor_tensor(row[b][:, 0:D], qkv[2][b][0:T, :], v_bias[:, :], ALU.add).then_inc(p_v, 1)
                        dve.wait_ge(p_rank[1], a.t + 1)
                        nc.vector.tensor_scalar(row[b][:, RANKB:RANKB + 1], sums[:, 1, bass.ds(a.t, 1)], float(E - 1), 0.5, ALU.add, ALU.mult)
                        nc.vector.tensor_copy(row[b][:, SRC:EW + 1], edge_f[:, :, bass.ds(a.t, 1)].rearrange("p j o -> p (j o)"))
                        nc.vector.tensor_copy(row[b][:, DIAG:DIAG + 1], diag_col[:, bass.ds(a.t, 1)])
                        nc.vector.memset(row[b][:, DIAG + 1:ROW], 0.0)

                    def scores(a):
                        b = a.buf()
                        dve.wait_ge(p_qk, a.t + 1)
                        nc.vector.tensor_reduce(score[b][:, :], qk[b][:, :].rearrange("p (h d) -> p h d", h=H), axis=AX.X, op=ALU.add)\
                            .then_inc(p_sc, 1)

                    def weigh(a):
                        b = a.buf()
                        dve.wait_ge(p_sc, a.t + 1)
                        nc.vector.scalar_tensor_tensor(row[b][:, WS:WS + H], score[b][:, :], SCALE,
                                                       attr_s[:, bass.ds(a.t, 1), :].rearrange("p o h -> p (o h)"),
                                                       ALU.mult, ALU.mult).then_inc(p_row, 1)

                    def step(a):
                        at(v_rows, a.later(-1))
                        at(stats, a.later(3))
                        at(scores, a.later(-1))
                        at(moments, a.later(3))
                        at(norm, a.later(2))
                        at(weigh, a.later(-1))
                        at(q_rows, a)
                        at(keep_diag, a.later(3))
                        at(reciprocal, a.later(3))
                        at(place, a.later(2))
                        at(low, a.later(1))
                        at(k_rows, a)
                    tiles(dve, step, ET, UN, before=3, after=1)

                @block.tensor
                def _(pe):
                    def turn(a):
                        b = a.buf()
                        pe.wait_ge(p_xh, a.t + 1)
                        if not a.early(1):
                            pe.wait_ge(p_lo, a.t)
                        for j in range(2):
                            last = transpose_tile(tp[j], xh[j][b], ident)
                        last.then_inc(p_t, 1)

                    def project(a, n):
                        b = a.buf()
                        side, w, free = ((0, q_w, p_q), (1, k_w, p_k), (1, v_w, p_v))[n]
                        pe.wait_ge(p_lo, a.t + 1)
                        if not a.early(2):
                            pe.wait_ge(free, a.t - 1)
                        product(qkv[n][b], hi[side][b], lo[side][b], w).then_inc(p_mm[n], 1)

                    def step(a):
                        if a.exists():
                            project(a, 0)
                        at(turn, a.later(1))
                        if a.exists():
                            project(a, 1)
                            project(a, 2)
                    tiles(pe, step, ET, UN, before=1)

        end_part()
        by_dst_s = whole.enter_context(nc.sbuf_tensor("by_dst_s", [T, ET, 4], F32))
        near = whole.enter_context(nc.sbuf_tensor("src_fields", [T, ET, FIELDS], F32))
        place_i = whole.enter_context(nc.sbuf_tensor("place_i", [T, 4, ET], I32))
        PLACE, SLOT, RB, SRCI = range(4)
        rec_den = whole.enter_context(nc.sbuf_tensor("rec_den", [T, ET, H], F32))
        e_col = whole.enter_context(nc.sbuf_tensor("e_col", [T, ET, H], F32))
        prev_key = whole.enter_context(nc.sbuf_tensor("prev_key", [T, ET + 1], F32))
        last_row = whole.enter_context(nc.sbuf_tensor("last_row", [T, 1], F32))
        with ExitStack() as ph:
            sb, ps = holder(ph)
            R = H + 1
            QT = 4
            NB = ET // QT
            key9 = sb("key9", [R, E])
            run = sb("run", [R, E])
            top = sb("top", [R, E])
            same = sb("same", [R, E + 1])
            gap = sb("gap", [R, E + 1])
            place_f = sb("place_f", [T, ET])
            ends = sb("ends", [T, ET])
            stage = [sb(f"stage_b{i}", [P, KC, D]) for i in range(4)]
            w1_rows = sb("w1_rows", [P, KC, D])
            w2_parts = [sb(f"w2_{p}", [P, KC, D], F32R) for p in ("hi", "lo")]
            w1t = [sb(f"w1t_{p}", [P, KC, P], F32R) for p in ("hi", "lo")]
            b1_col = sb("b1_col", [P, KC])
            field9 = sb("field9", [T, ET, R])
            banks = ps("wide", (P, NB, D))
            one = ps("one_bank")
            two = ps("two_bank")
            three = ps("three_bank")
            wide = banks[0:R, :, 0:QT * T]
            s_in, s_small, s_bias = sem("s_in"), sem("s_small"), sem("s_bias")
            s_w_in, s_w1_in = sems("s_w_in", 4), sem("s_w1_in")
            s_pos, s_f9, s_t = sem("s_pos"), sem("s_f9"), sem("s_t")
            s_ev, s_same, s_gap, s_run, s_top, s_d, s_e, s_sum = (sem(f"s_{n}") for n in ("ev", "same", "gap", "run", "top", "d", "e", "sum"))
            s_back, s_got, s_end, s_c = sem("s_back"), sem("s_got"), sem("s_end"), sem("s_c")
            s_hi, s_lo, s_w1t, s_w1h, s_w1l, s_w12, s_w12h, s_w12l, s_cmm, s_cev = (
                sem(f"s_{n}") for n in ("hi", "lo", "w1t", "w1h", "w1l", "w12", "w12h", "w12l", "cmm", "cev"))
            block = ph.enter_context(nc.Block())
            loads = ((w2, w2_parts), (w01, dense1_w), (w11, conv1_w), (w12g, conv2_w), (w02, dense2_w))

            @block.sync
            def _(sp):
                sp.dma_start(near[:, :, :], by_src[:, WS:ROW].rearrange("(t p) f -> p t f", p=T)).then_inc(s_in, 16)
                sp.dma_start(b1_col[:, :], columns(b1)).then_inc(s_small, 16)
                sp.dma_start(stage[0][:, :, :], weight_rows(w2)).then_inc(s_w_in[0], 16)
                sp.dma_start(half_c[:, :], row_for_all(b2)).then_inc(s_bias, 16)
                sp.dma_start(neigh_b[:, 0:D], row_for_all(gb1)).then_inc(s_bias, 16)
                sp.dma_start(neigh_b[:, D:2 * D], row_for_all(gb2)).then_inc(s_bias, 16)
                sp.dma_start(w1_rows[:, :, :], weight_rows(w1)).then_inc(s_w1_in, 16)
                for i in range(1, len(loads)):
                    if i >= 4:
                        sp.wait_ge(s_lo, i - 3)
                        sp.wait_ge(s_cmm, 1)
                    sp.dma_start(stage[i % 4][:, :, :], weight_rows(loads[i][0])).then_inc(s_w_in[i % 4], 16)

            @block.gpsimd
            def _(pool):
                nc.gpsimd.iota(place_i[:, PLACE, :], [[T, ET]], base=0, channel_multiplier=1).then_inc(s_pos, 1)
                nc.gpsimd.memset(last_row[:, :], 0.0).then_inc(s_pos, 1)
                pool.wait_ge(s_pos, 2)
                nc.gpsimd.affine_select(out=last_row[:, :], in_=last_row[:, :], compare_op=ALU.not_equal, fill=1.0,
                                        base=-(T - 1), pattern=[[0, 1]], channel_multiplier=1).then_inc(s_pos, 1)
                for i, (_, w) in enumerate(loads):
                    pool.wait_ge(s_hi, i + 1)
                    for k in range(KC):
                        last = nc.gpsimd.tensor_tensor(w[1][:, k, :], stage[i % 4][:, k, :], w[0][:, k, :].bitcast(F32), ALU.subtract)
                    last.then_inc(s_lo, 1)

            @block.scalar
            def _(act):
                def high(i):
                    act.wait_ge(s_w_in[i % 4], 16 * (i // 4 + 1))
                    for k in range(KC):
                        last = nc.scalar.activation(loads[i][1][0][:, k, :], stage[i % 4][:, k, :], ACT.Copy)
                    last.then_inc(s_hi, 1)

                def high_w1(m):
                    act.wait_ge(s_w1t, m + 1)
                    if m:
                        act.wait_ge(s_w12, m)
                    nc.scalar.activation(w1t[0][:, :, :], one[:, :].rearrange("p (k c) -> p k c", k=KC), ACT.Copy).then_inc(s_w1h, 1)

                def high_w12(m):
                    act.wait_ge(s_w12, m + 1)
                    nc.scalar.activation(attn_w[0][:, m, :], two[:, :], ACT.Copy).then_inc(s_w12h, 1)

                high(0)
                high_w1(0)
                high(1)
                high_w12(0)
                high_w1(1)
                high(2)
                high_w12(1)
                high_w1(2)
                act.wait_ge(s_d, 1)
                nc.scalar.activation(run[0:H, :], top[0:H, :], ACT.Exp).then_inc(s_e, 1)
                high_w12(2)
                high_w1(3)
                high(3)
                high_w12(3)
                high(4)

            @block.vector
            def _(dve):
                def low_w1(m):
                    dve.wait_ge(s_w1h, m + 1)
                    nc.vector.tensor_tensor(w1t[1][:, :, :], one[:, :].rearrange("p (k c) -> p k c", k=KC),
                                            w1t[0][:, :, :].bitcast(F32), ALU.subtract).then_inc(s_w1l, 1)

                def low_w12(m):
                    dve.wait_ge(s_w12h, m + 1)
                    nc.vector.tensor_tensor(attn_w[1][:, m, :], two[:, :], attn_w[0][:, m, :].bitcast(F32), ALU.subtract).then_inc(s_w12l, 1)

                dve.wait_ge(s_pos, 3)
                dve.wait_ge(s_in, 16)
                nc.vector.tensor_copy(place_f[:, :], place_i[:, PLACE, :]).then_inc(s_f9, 1)
                nc.vector.tensor_copy(field9[:, :, 0:H], near[:, :, 0:H]).then_inc(s_f9, 1)
                dve.wait_ge(s_f9, 1)
                nc.vector.tensor_copy(field9[:, :, H], place_f[:, :]).then_inc(s_f9, 1)
                dve.wait_ge(s_t, 1)
                nc.vector.tensor_copy(key9[:, :].rearrange("r (b c) -> r b c", b=NB), wide).then_inc(s_ev, 1)
                nc.vector.memset(same[:, 0:1], 0.0)
                nc.vector.memset(same[:, E:E + 1], 0.0)
                dve.wait_ge(s_ev, 1)
                nc.vector.tensor_tensor(same[:, 1:E], key9[:, 1:E], key9[:, 0:E - 1], ALU.is_equal).then_inc(s_same, 1)
                dve.wait_ge(s_bias, 48)
                dve.wait_ge(s_cmm, 1)
                nc.vector.tensor_tensor(half_c[:, :], two[0:T, :], half_c[:, :], ALU.add).then_inc(s_cev, 1)
                dve.wait_ge(s_cev, 1)
                nc.vector.tensor_scalar(half_c[:, :], half_c[:, :], 0.5, None, ALU.mult)
                nc.vector.tensor_scalar(neigh_b[:, D:2 * D], neigh_b[:, D:2 * D], 1.0 / 3.0, None, ALU.mult)
                dve.wait_ge(s_same, 1)
                nc.vector.tensor_scalar(gap[:, :], same[:, :], 1.0, -GAP, ALU.subtract, ALU.mult).then_inc(s_gap, 1)
                dve.wait_ge(s_t, 2)
                nc.vector.tensor_copy(key9[:, :].rearrange("r (b c) -> r b c", b=NB), wide).then_inc(s_ev, 1)
                dve.wait_ge(s_ev, 2)
                dve.wait_ge(s_gap, 1)
                nc.vector.tensor_tensor_scan(run[:, :], gap[:, 0:E], key9[:, :], 0.0, ALU.add, ALU.max).then_inc(s_run, 1)
                low_w1(0)
                dve.wait_ge(s_run, 1)
                nc.vector.tensor_tensor_scan(top[:, ::-1], gap[:, E:0:-1], run[:, ::-1], 0.0, ALU.add, ALU.max).then_inc(s_top, 1)
                low_w12(0)
                low_w1(1)
                dve.wait_ge(s_back, 1)
                nc.vector.tensor_copy(ends[:, :], three[0:T, 0:ET * R].rearrange("p (t r) -> p t r", r=R)[:, :, H]).then_inc(s_end, 1)
                nc.vector.tensor_tensor(top[0:H, :], key9[0:H, :], top[0:H, :], ALU.subtract).then_inc(s_d, 1)
                low_w12(1)
                low_w1(2)
                dve.wait_ge(s_e, 1)
                nc.vector.tensor_tensor_scan(key9[0:H, :], same[0:H, 0:E], run[0:H, :], 0.0, ALU.mult, ALU.add).then_inc(s_sum, 1)
                low_w12(2)
                low_w1(3)
                dve.wait_ge(s_end, 1)
                nc.vector.tensor_tensor(place_f[:, :], place_f[:, :], ends[:, :], ALU.not_equal).then_inc(s_end, 1)
                dve.wait_ge(s_end, 2)
                nc.vector.scalar_tensor_tensor(place_i[:, SLOT, :], place_f[:, :], float(FAR), near[:, :, SRC - WS], ALU.mult, ALU.add)
                nc.vector.tensor_copy(place_i[:, RB, :], near[:, :, RANKB - WS])
                nc.vector.tensor_copy(place_i[:, SRCI, :], near[:, :, SRC - WS])
                nc.vector.tensor_copy(by_dst_s[:, :, 0:2], near[:, :, DST - WS:EW - WS + 1])
                nc.vector.tensor_copy(by_dst_s[:, :, 2], ends[:, :])
                nc.vector.tensor_copy(by_dst_s[:, :, 3], ends[:, :])
                nc.vector.tensor_scalar(prev_key[:, 1:ET + 1], near[:, :, SRC - WS], 1.0, last_row[:, 0:1], ALU.add, ALU.mult).then_inc(s_c, 1)
                nc.vector.memset(prev_key[:, 0:1], 0.0).then_inc(s_c, 1)
                dve.wait_ge(s_c, 2)
                nc.vector.tensor_scalar(prev_key[:, :], prev_key[:, :], 1.0, None, ALU.subtract)
                low_w12(3)
                dve.wait_ge(s_back, 2)
                nc.vector.tensor_copy(e_col[:, :, :], three[0:T, 0:ET * H].rearrange("p (t h) -> p t h", h=H)).then_inc(s_got, 1)
                nc.vector.tensor_scalar(rec_den[:, :, :], three[0:T, ET * H:2 * ET * H].rearrange("p (t h) -> p t h", h=H),
                                        1e-16, None, ALU.add).then_inc(s_got, 1)
                dve.wait_ge(s_got, 2)
                nc.vector.reciprocal(rec_den[:, :, :], rec_den[:, :, :])

            @block.tensor
            def _(pe):
                def wide_at(t):
                    return banks[0:R, t // QT, (t % QT) * T:(t % QT + 1) * T]

                pe.wait_ge(s_in, 16)
                for t in range(ET):
                    last = nc.tensor.transpose(wide_at(t), near[:, t, SRC - WS:SRC - WS + 1].to_broadcast([T, R]), ident[0:T, 0:T])
                last.then_inc(s_t, 1)
                pe.wait_ge(s_f9, 3)
                pe.wait_ge(s_ev, 1)
                for t in range(ET):
                    last = nc.tensor.transpose(wide_at(t), field9[:, t, :], ident[0:T, 0:T])
                last.then_inc(s_t, 1)
                pe.wait_ge(s_small, 16)
                pe.wait_ge(s_w_in[0], 16)
                for k in range(KC):
                    last = nc.tensor.matmul(two[0:T, :], b1_col[:, k:k + 1].to_broadcast([P, T]), stage[0][:, k, :],
                                            start=(k == 0), stop=(k == KC - 1))
                last.then_inc(s_cmm, 1)
                def turn_w1(m):
                    if m:
                        pe.wait_ge(s_w1l, m)
                    else:
                        pe.wait_ge(s_w1_in, 16)
                    for k in range(KC):
                        last = nc.tensor.transpose(one[:, P * k:P * (k + 1)], w1_rows[:, m, P * k:P * (k + 1)], ident[:, :])
                    last.then_inc(s_w1t, 1)

                def product_w12(m):
                    pe.wait_ge(s_w1l, m + 1)
                    if m:
                        pe.wait_ge(s_w12l, m)
                    else:
                        pe.wait_ge(s_cev, 1)
                        pe.wait_ge(s_lo, 1)
                    n = 0
                    for k in range(KC):
                        for a, b in ((0, 0), (0, 1), (1, 0)):
                            last = nc.tensor.matmul(two[:, :], w1t[a][:, k, :], w2_parts[b][:, k, :], start=(n == 0), stop=(n == 3 * KC - 1))
                            n += 1
                    last.then_inc(s_w12, 1)

                turn_w1(0)
                product_w12(0)
                turn_w1(1)
                pe.wait_ge(s_top, 1)
                for t in range(ET):
                    last = nc.tensor.transpose(three[0:T, t * R:(t + 1) * R], top[:, t * T:(t + 1) * T], ident[0:R, 0:R])
                last.then_inc(s_back, 1)
                product_w12(1)
                turn_w1(2)
                product_w12(2)
                turn_w1(3)
                pe.wait_ge(s_end, 1)
                pe.wait_ge(s_sum, 1)
                for t in range(ET):
                    nc.tensor.transpose(three[0:T, t * H:(t + 1) * H], run[0:H, t * T:(t + 1) * T], ident[0:H, 0:H])
                    last = nc.tensor.transpose(three[0:T, (ET + t) * H:(ET + t + 1) * H], key9[0:H, t * T:(t + 1) * T], ident[0:H, 0:H])
                last.then_inc(s_back, 1)
                product_w12(3)

        end_part()
        edges = ExitStack()
        m_all = edges.enter_context(nc.sbuf_tensor("m_all", [T, ET, D], F32))
        dfield = edges.enter_context(nc.sbuf_tensor("dfield", [T, ET, 4], F32))
        dprev = edges.enter_context(nc.sbuf_tensor("dprev", [T, ET + 1], F32))
        dnext = edges.enter_context(nc.sbuf_tensor("dnext", [T, ET], F32))
        dplace = edges.enter_context(nc.sbuf_tensor("dplace", [T, 3, ET], I32))
        in_place = edges.enter_context(nc.sbuf_tensor("in_place", [T, ET], I32))
        with ExitStack() as ph:
            sb, ps = holder(ph)
            vrow = [sb(f"vrow{b}", [T, D]) for b in range(2)]
            xrow = [sb(f"xrow{b}", [T, D]) for b in range(2)]
            wvs = [sb(f"wvs{b}", [T, D]) for b in range(2)]
            match = [sb(f"match{b}", [T, 2, T]) for b in range(2)]
            key_now = [sb(f"key_now{b}", [T, 1]) for b in range(2)]
            total = [sb(f"total{b}", [T, D]) for b in range(2)]
            vals = [sb(f"vals{b}", [T, D]) for b in range(2)]
            hi_v, lo_v, hi_x, lo_x = ([sb(f"a_{n}{b}", [P, KC, P], F32R) for b in range(2)] for n in ("hi_v", "lo_v", "hi_x", "lo_x"))
            u = [sb(f"u{b}", [T, D]) for b in range(2)]
            y = [sb(f"y{b}", [T, D]) for b in range(2)]
            x1 = [sb(f"x1_{b}", [T, D]) for b in range(2)]
            z = [sb(f"z{b}", [T, D]) for b in range(2)]
            st, mv, rs = ([sb(f"a_{n}{b}", [T, s]) for b in range(2)] for n, s in (("st", 6), ("mv", 2), ("rs", 3)))
            pidx = [sb(f"pidx{b}", [T, 4], I32) for b in range(2)]
            brow = [sb(f"brow{b}", [T, 4]) for b in range(2)]
            didx = [sb(f"didx{b}", [T, 2], I32) for b in range(4)]
            sidx = [sb(f"sidx{b}", [T, 2], I32) for b in range(4)]
            keys_ps = ps("a_keys")
            sum_ps = [ps(f"a_sum{b}") for b in range(2)]
            tp_v, tp_x, attn_ps, m_ps, z_ps = (ps(f"a_{n}") for n in ("tp_v", "tp_x", "attn_ps", "m_ps", "z_ps"))
            a_v, a_x, a_u_out, a_z_out = sems("a_v"), sems("a_x"), sems("a_u_out"), sems("a_z_out")
            a_slot, a_brow = sems("a_slot"), sems("a_brow")
            a_dslot, a_look = sems("a_dslot", 4), sems("a_look", 4)
            a_field, a_prep, a_didx, a_sidx, a_got = sem("a_field"), sem("a_prep"), sem("a_didx"), sem("a_sidx"), sem("a_got")
            (a_now, a_key, a_m, a_wv, a_sum, a_tot, a_val, a_tv, a_hv, a_lv, a_attn, a_u, a_y, a_st, a_ag, a_dev, a_rec, a_off,
             a_x1, a_tx, a_hx, a_lx, a_mmm, a_mcp, a_zmm, a_zcp, a_idx, a_zero) = (
                sem(f"a_{n}") for n in ("now", "key", "m", "wv", "sum", "tot", "val", "tv", "hv", "lv", "attn", "u", "y", "st", "ag",
                                        "dev", "rec", "off", "x1", "tx", "hx", "lx", "mmm", "mcp", "zmm", "zcp", "idx", "zero"))
            UN = 4
            block = ph.enter_context(nc.Block())

            @block.sync
            def _(sp):
                def load_v(a):
                    b = a.buf()
                    if not a.early(2):
                        sp.wait_ge(a_wv, a.t - 1)
                    sp.dma_start(vrow[b][:, :], by_src[bass.ds(a.t * T, T), 0:D]).then_inc(a_v[b], 16)

                def load_x(a):
                    b = a.buf()
                    if not a.early(2):
                        sp.wait_ge(a_u, a.t - 1)
                    sp.dma_start(xrow[b][:, :], x_by_src[bass.ds(a.t * T, T), :]).then_inc(a_x[b], 16)

                def store_u(a):
                    b = a.buf()
                    sp.wait_ge(a_u, a.t + 1)
                    sp.dma_start(x_new[bass.ds(a.t * T, T), :], u[b][:, :]).then_inc(a_u_out[b], 16)

                def store_z(a):
                    b = a.buf()
                    sp.wait_ge(a_zcp, a.t + 1)
                    sp.dma_start(z_rows[bass.ds(a.t * T, T), :], z[b][:, :]).then_inc(a_z_out[b], 16)

                def step(a):
                    at(load_v, a.later(4))
                    at(store_z, a.later(-3))
                    at(load_x, a.later(1))
                    at(store_u, a.later(-1))
                tiles(sp, step, ET, UN, before=4, after=3)
                for b in range(2):
                    sp.wait_ge(a_u_out[b], 16 * (ET // 2))
                    sp.wait_ge(a_z_out[b], 16 * (ET // 2))

            @block.gpsimd
            def _(pool):
                bound = {"N": pool.to_reg(N - 1), "E": pool.to_reg(E - 1)}
                def step(a):
                    b, n = a.buf(), a.use()
                    if not a.early(2):
                        pool.wait_ge(a_slot[b], 16 * n)
                        pool.wait_ge(a_brow[b], 16 * n)
                    nc.gpsimd.tensor_copy(pidx[b][:, 0:3], place_i[:, 0:3, bass.ds(a.t, 1)].rearrange("p j o -> p (j o)"))
                    nc.gpsimd.tensor_copy(brow[b][:, :], by_dst_s[:, bass.ds(a.t, 1), :].rearrange("p o f -> p (o f)")).then_inc(a_idx, 1)
                    pool.wait_ge(a_idx, a.t + 1)
                    alone(pool)
                    pool.indirect_dma_start(by_dst, bass.IndirectOffsetOnAxis(ap=pidx[b][:, RB:RB + 1], axis=0), brow[b][:, :], None,
                                            bounds_check=bound["E"], oob_is_err=False).then_inc(a_brow[b], 16)
                    alone(pool)
                    pool.indirect_dma_start(slot_src, bass.IndirectOffsetOnAxis(ap=pidx[b][:, SLOT:SLOT + 1], axis=0),
                                            pidx[b][:, PLACE:PLACE + 1], None,
                                            bounds_check=bound["N"], oob_is_err=False).then_inc(a_slot[b], 16)
                tiles(pool, step, ET)
                for b in range(2):
                    pool.wait_ge(a_slot[b], 16 * (ET // 2))
                    pool.wait_ge(a_brow[b], 16 * (ET // 2))

                pool.dma_start(dfield[:, :, :], by_dst[0:E, :].rearrange("(t p) f -> p t f", p=T)).then_inc(a_field, 16)
                pool.dma_start(dnext[:, :], by_dst[1:E + 1, 0:1].rearrange("(t p) f -> p (t f)", p=T)).then_inc(a_field, 16)
                nc.gpsimd.memset(dprev[:, 0:1], 0.0)
                pool.wait_ge(a_field, 32)
                nc.gpsimd.tensor_tensor(dnext[:, :], dnext[:, :], dfield[:, :, 0], ALU.subtract).then_inc(a_prep, 1)
                nc.gpsimd.tensor_scalar(dprev[:, 1:ET + 1], dfield[:, :, 0], 1.0, last_row[:, 0:1], ALU.add, ALU.mult).then_inc(a_prep, 1)
                pool.wait_ge(a_prep, 2)
                nc.gpsimd.tensor_scalar(dnext[:, :], dnext[:, :], 0.0, float(FAR), ALU.is_equal, ALU.mult).then_inc(a_prep, 1)
                nc.gpsimd.tensor_scalar(dprev[:, :], dprev[:, :], 1.0, None, ALU.subtract)
                pool.wait_ge(a_prep, 3)
                nc.gpsimd.tensor_tensor(dnext[:, :], dnext[:, :], dfield[:, :, 0], ALU.add).then_inc(a_prep, 1)
                pool.wait_ge(a_prep, 4)
                nc.gpsimd.tensor_copy(dplace[:, 0, :], dnext[:, :])
                nc.gpsimd.tensor_copy(dplace[:, 1, :], place_i[:, PLACE, :])
                nc.gpsimd.tensor_copy(dplace[:, 2, :], dfield[:, :, 2]).then_inc(a_prep, 1)
                pool.wait_ge(a_prep, 5)

                def send_slot(a):
                    b4, n = a.buf(4), a.use(4)
                    if not a.early(4):
                        pool.wait_ge(a_dslot[b4], 16 * n)
                    nc.gpsimd.tensor_copy(didx[b4][:, :], dplace[:, 0:2, bass.ds(a.t, 1)].rearrange("p j o -> p (j o)")).then_inc(a_didx, 1)
                    pool.wait_ge(a_didx, a.t + 1)
                    alone(pool)
                    pool.indirect_dma_start(slot_dst, bass.IndirectOffsetOnAxis(ap=didx[b4][:, 0:1], axis=0), didx[b4][:, 1:2], None,
                                            bounds_check=bound["N"], oob_is_err=False).then_inc(a_dslot[b4], 16)
                tiles(pool, send_slot, ET, UN)
                for b4 in range(4):
                    pool.wait_ge(a_dslot[b4], 16 * (ET // 4))

                def look(a):
                    b4 = a.buf(4)
                    if not a.early(4):
                        pool.wait_ge(a_got, a.t - 3)
                    nc.gpsimd.tensor_copy(sidx[b4][:, 0:1], place_i[:, SRCI, bass.ds(a.t, 1)]).then_inc(a_sidx, 1)
                    pool.wait_ge(a_sidx, a.t + 1)
                    alone(pool)
                    pool.indirect_dma_start(sidx[b4][:, 1:2], None, slot_dst, bass.IndirectOffsetOnAxis(ap=sidx[b4][:, 0:1], axis=0),
                                            bounds_check=bound["N"], oob_is_err=False).then_inc(a_look[b4], 16)

                def keep(a):
                    b4, n = a.buf(4), a.use(4)
                    pool.wait_ge(a_look[b4], 16 * n + 16)
                    nc.gpsimd.tensor_copy(in_place[:, bass.ds(a.t, 1)], sidx[b4][:, 1:2]).then_inc(a_got, 1)

                def look_and_keep(a):
                    at(look, a)
                    at(keep, a.later(-3))
                tiles(pool, look_and_keep, ET, UN, after=3)

            @block.scalar
            def _(act):
                def now(a):
                    if not a.early(2):
                        act.wait_ge(a_key, a.t - 1)
                    nc.scalar.copy(key_now[a.buf()][:, :], near[:, bass.ds(a.t, 1), SRC - WS:SRC - WS + 1].rearrange("p o f -> p (o f)"))\
                        .then_inc(a_now, 1)

                def keep_total(a):
                    b = a.buf()
                    act.wait_ge(a_sum, a.t + 1)
                    if not a.early(2):
                        act.wait_ge(a_val, a.t - 1)
                    nc.scalar.activation(total[b][:, :], sum_ps[b][0:T, :], ACT.Copy).then_inc(a_tot, 1)

                def high_v(a):
                    b = a.buf()
                    act.wait_ge(a_tv, a.t + 1)
                    if not a.early(2):
                        act.wait_ge(a_attn, a.t - 1)
                    nc.scalar.activation(hi_v[b][:, :, 0:T], chunks(tp_v[:, :]), ACT.Copy).then_inc(a_hv, 1)

                def deviation(a):
                    b = a.buf()
                    act.wait_ge(a_ag, a.t + 1)
                    if not a.early(2):
                        act.wait_ge(a_rec, a.t - 1)
                    nc.scalar.activation(rs[b][:, 0:1], mv[b][:, 1:2], ACT.Sqrt, bias=eps[0:T, 1:2]).then_inc(a_dev, 1)

                def norm(a):
                    b = a.buf()
                    act.wait_ge(a_off, a.t + 1)
                    if not a.early(2):
                        act.wait_ge(a_tx, a.t - 1)
                    nc.scalar.activation(x1[b][:, :], y[b][:, :], ACT.Identity, scale=rs[b][:, 1:2], bias=rs[b][:, 2:3]).then_inc(a_x1, 1)

                def high_x(a):
                    b = a.buf()
                    act.wait_ge(a_tx, a.t + 1)
                    if not a.early(2):
                        act.wait_ge(a_zmm, a.t - 1)
                    nc.scalar.activation(hi_x[b][:, :, 0:T], chunks(tp_x[:, :]), ACT.Copy).then_inc(a_hx, 1)

                def keep_m(a):
                    act.wait_ge(a_mmm, a.t + 1)
                    nc.scalar.activation(m_all[:, bass.ds(a.t, 1), :].rearrange("p o d -> p (o d)"), m_ps[0:T, :], ACT.Copy,
                                         scale=near[:, bass.ds(a.t, 1), DIAG - WS:DIAG - WS + 1].rearrange("p o f -> p (o f)"))\
                        .then_inc(a_mcp, 1)

                def keep_z(a):
                    b = a.buf()
                    act.wait_ge(a_zmm, a.t + 1)
                    if not a.early(2):
                        act.wait_ge(a_z_out[b], 16 * a.use())
                    nc.scalar.activation(z[b][:, :], z_ps[0:T, :], ACT.Copy).then_inc(a_zcp, 1)

                def step(a):
                    at(high_x, a.later(-1))
                    at(keep_z, a.later(-2))
                    at(now, a.later(4))
                    at(keep_total, a.later(2))
                    at(high_v, a.later(1))
                    at(deviation, a)
                    at(norm, a)
                    at(keep_m, a.later(-1))
                tiles(act, step, ET, UN, before=4, after=2)

            @block.vector
            def _(dve):
                nc.vector.memset(total[1][:, :], 0.0).then_inc(a_zero, 1)

                def prepare(a):
                    b, n = a.buf(), a.use()
                    dve.wait_ge(a_key, a.t + 1)
                    if not a.early(2):
                        dve.wait_ge(a_sum, a.t - 1)
                    keys = keys_ps[0:T, 0:T]
                    nc.vector.tensor_scalar(match[b][:, 0, :], keys,
                                            near[:, bass.ds(a.t, 1), SRC - WS:SRC - WS + 1].rearrange("p o f -> p (o f)"), None, ALU.is_equal)
                    nc.vector.tensor_scalar(match[b][:, 1, :], keys, prev_key[:, bass.ds(a.t, 1)], None, ALU.is_equal).then_inc(a_m, 1)
                    dve.wait_ge(a_v[b], 16 * n + 16)
                    nc.vector.tensor_tensor(wvs[b][:, :].rearrange("p (h d) -> p h d", h=H), vrow[b][:, :].rearrange("p (h d) -> p h d", h=H),
                                            e_col[:, bass.ds(a.t, 1), :].rearrange("p o h -> p h o").to_broadcast([T, H, HD]),
                                            ALU.mult).then_inc(a_wv, 1)

                def values(a):
                    b = a.buf()
                    dve.wait_ge(a_tot, a.t + 1)
                    if not a.early(2):
                        dve.wait_ge(a_tv, a.t - 1)
                    nc.vector.tensor_tensor(vals[b][:, :].rearrange("p (h d) -> p h d", h=H), total[b][:, :].rearrange("p (h d) -> p h d", h=H),
                                            rec_den[:, bass.ds(a.t, 1), :].rearrange("p o h -> p h o").to_broadcast([T, H, HD]),
                                            ALU.mult).then_inc(a_val, 1)

                def low_v(a):
                    b = a.buf()
                    dve.wait_ge(a_hv, a.t + 1)
                    nc.vector.tensor_tensor(lo_v[b][:, :, 0:T], chunks(tp_v[:, :]), hi_v[b][:, :, 0:T].bitcast(F32), ALU.subtract)\
                        .then_inc(a_lv, 1)

                def add(a):
                    b, n = a.buf(), a.use()
                    dve.wait_ge(a_attn, a.t + 1)
                    dve.wait_ge(a_x[b], 16 * n + 16)
                    if not a.early(2):
                        dve.wait_ge(a_u_out[b], 16 * n)
                        dve.wait_ge(a_x1, a.t - 1)
                    nc.vector.scalar_tensor_tensor(u[b][:, :], attn_ps[0:T, :], 0.5, xrow[b][:, :], ALU.mult, ALU.add).then_inc(a_u, 1)
                    dve.wait_ge(a_u, a.t + 1)
                    nc.vector.tensor_tensor(y[b][:, :], u[b][:, :], half_c[:, :], ALU.add).then_inc(a_y, 1)
                    dve.wait_ge(a_y, a.t + 1)
                    nc.vector.bn_stats(st[b][:, :], y[b][:, :]).then_inc(a_st, 1)
                    dve.wait_ge(a_st, a.t + 1)
                    alone(dve)
                    nc.vector.bn_aggr(mv[b][:, :], st[b][:, :]).then_inc(a_ag, 1)

                def scale(a):
                    b = a.buf()
                    dve.wait_ge(a_dev, a.t + 1)
                    nc.vector.reciprocal(rs[b][:, 1:2], rs[b][:, 0:1]).then_inc(a_rec, 1)
                    dve.wait_ge(a_rec, a.t + 1)
                    nc.vector.tensor_scalar(rs[b][:, 2:3], mv[b][:, 0:1], rs[b][:, 1:2], -1.0, ALU.mult, ALU.mult).then_inc(a_off, 1)

                def low_x(a):
                    b = a.buf()
                    dve.wait_ge(a_hx, a.t + 1)
                    nc.vector.tensor_tensor(lo_x[b][:, :, 0:T], chunks(tp_x[:, :]), hi_x[b][:, :, 0:T].bitcast(F32), ALU.subtract)\
                        .then_inc(a_lx, 1)

                def step(a):
                    at(low_x, a.later(-1))
                    at(values, a.later(1))
                    at(prepare, a.later(3))
                    at(add, a)
                    at(low_v, a.later(1))
                    at(scale, a)
                tiles(dve, step, ET, UN, before=3, after=1)

            @block.tensor
            def _(pe):
                def keys(a):
                    b = a.buf()
                    if not a.early(1):
                        pe.wait_ge(a_m, a.t)
                    pe.wait_ge(a_now, a.t + 1)
                    nc.tensor.transpose(keys_ps[0:T, 0:T], key_now[b][:, :].to_broadcast([T, T]), ident[0:T, 0:T])\
                        .then_inc(a_key, 1)

                def sums_of(a):
                    b = a.buf()
                    pe.wait_ge(a_m, a.t + 1)
                    pe.wait_ge(a_wv, a.t + 1)
                    if not a.early(2):
                        pe.wait_ge(a_tot, a.t - 1)
                    nc.tensor.matmul(sum_ps[b][0:T, :], match[b][:, 0, :], wvs[b][:, :], start=True, stop=False)
                    if a.early(1):
                        pe.wait_ge(a_zero, 1)
                    else:
                        pe.wait_ge(a_tot, a.t)
                    nc.tensor.matmul(sum_ps[b][0:T, :], match[b][:, 1, :], total[1 - b][:, :], start=False, stop=True).then_inc(a_sum, 1)

                def attend(a):
                    b = a.buf()
                    pe.wait_ge(a_lv, a.t + 1)
                    if not a.early(1):
                        pe.wait_ge(a_u, a.t)
                    product(attn_ps, hi_v[b], lo_v[b], attn_w).then_inc(a_attn, 1)

                def turn_v(a):
                    b = a.buf()
                    pe.wait_ge(a_val, a.t + 1)
                    if not a.early(1):
                        pe.wait_ge(a_lv, a.t)
                    transpose_tile(tp_v, vals[b], ident).then_inc(a_tv, 1)

                def turn_x(a):
                    b = a.buf()
                    pe.wait_ge(a_x1, a.t + 1)
                    if not a.early(1):
                        pe.wait_ge(a_lx, a.t)
                    transpose_tile(tp_x, x1[b], ident).then_inc(a_tx, 1)

                def convolve_rows(a):
                    b = a.buf()
                    pe.wait_ge(a_lx, a.t + 1)
                    if not a.early(1):
                        pe.wait_ge(a_mcp, a.t)
                    product(m_ps, hi_x[b], lo_x[b], dense1_w).then_inc(a_mmm, 1)
                    if not a.early(1):
                        pe.wait_ge(a_zcp, a.t)
                    product(z_ps, hi_x[b], lo_x[b], conv1_w).then_inc(a_zmm, 1)

                def step(a):
                    at(keys, a.later(3))
                    at(sums_of, a.later(2))
                    at(attend, a)
                    at(turn_v, a.later(1))
                    at(convolve_rows, a.later(-1))
                    at(turn_x, a)
                tiles(pe, step, ET, UN, before=3, after=1)

        end_part()
        def sum_by_dst(first):
            c0 = 0 if first else D
            nm = "c1" if first else "c2"
            stores = 32 if first else 16
            with ExitStack() as ph:
                sb, ps = holder(ph)
                g = [sb(f"{nm}_g{b}", [T, D]) for b in range(4)]
                key_now = [sb(f"{nm}_key_now{b}", [T, 1]) for b in range(2)]
                match = [sb(f"{nm}_match{b}", [T, 2, T]) for b in range(4)]
                total = [sb(f"{nm}_total{b}", [T, D]) for b in range(2)]
                res = [sb(f"{nm}_res{b}", [T, D]) for b in range(4)]
                pidx = [sb(f"{nm}_idx{b}", [T, 1], I32) for b in range(4)]
                keys_ps = [ps(f"{nm}_keys{b}") for b in range(2)]
                sum_ps = [ps(f"{nm}_sum{b}") for b in range(4)]
                s_g, s_out = sems(f"{nm}_g", 4), sems(f"{nm}_out", 4)
                s_key, s_m, s_sum, s_tot, s_res, s_idx, s_zero, s_now = (
                    sem(f"{nm}_{n}") for n in ("key", "m", "sum", "tot", "res", "idx", "zero", "now"))
                UN = 4
                block = ph.enter_context(nc.Block())

                @block.sync
                def _(sp):
                    def step(a):
                        b4 = a.buf(4)
                        sp.wait_ge(s_res, a.t + 1)
                        sp.dma_start(neigh[bass.ds(a.t * T, T), c0:c0 + D], res[b4][:, :]).then_inc(s_out[b4], 16)
                        if first:
                            sp.dma_start(neigh1[bass.ds(a.t * T, T), :], res[b4][:, :]).then_inc(s_out[b4], 16)
                    tiles(sp, step, ET, UN)
                    for b4 in range(4):
                        sp.wait_ge(s_out[b4], stores * (ET // 4))

                @block.gpsimd
                def _(pool):
                    bound = {"N": pool.to_reg(N - 1), "E": pool.to_reg(E - 1)}
                    def step(a):
                        b4, n = a.buf(4), a.use(4)
                        if not a.early(4):
                            pool.wait_ge(s_sum, a.t - 3)
                            pool.wait_ge(s_g[b4], 16 * n)
                        nc.gpsimd.tensor_copy(pidx[b4][:, :], dplace[:, 2, bass.ds(a.t, 1)]).then_inc(s_idx, 1)
                        pool.wait_ge(s_idx, a.t + 1)
                        alone(pool)
                        pool.indirect_dma_start(g[b4][:, :], None, z_rows if first else z2_rows,
                                                bass.IndirectOffsetOnAxis(ap=pidx[b4][:, 0:1], axis=0),
                                                bounds_check=bound["E"], oob_is_err=False).then_inc(s_g[b4], 16)
                    tiles(pool, step, ET, UN)

                @block.scalar
                def _(act):
                    def now(a):
                        if not a.early(2):
                            act.wait_ge(s_key, a.t - 1)
                        nc.scalar.copy(key_now[a.buf()][:, :], dfield[:, bass.ds(a.t, 1), 0:1].rearrange("p o f -> p (o f)")).then_inc(s_now, 1)

                    def keep_total(a):
                        b, b4 = a.buf(), a.buf(4)
                        act.wait_ge(s_sum, a.t + 1)
                        nc.scalar.activation(total[b][:, :], sum_ps[b4][0:T, :], ACT.Copy).then_inc(s_tot, 1)

                    def step(a):
                        at(keep_total, a)
                        at(now, a.later(4))
                    tiles(act, step, ET, UN, before=4)

                @block.vector
                def _(dve):
                    nc.vector.memset(total[1][:, :], 0.0).then_inc(s_zero, 1)

                    def prepare(a):
                        b, b4 = a.buf(), a.buf(4)
                        dve.wait_ge(s_key, a.t + 1)
                        if not a.early(4):
                            dve.wait_ge(s_sum, a.t - 3)
                        nc.vector.tensor_scalar(match[b4][:, 0, :], keys_ps[b][0:T, 0:T],
                                                dfield[:, bass.ds(a.t, 1), 0:1].rearrange("p o f -> p (o f)"),
                                                dfield[:, bass.ds(a.t, 1), 1:2].rearrange("p o f -> p (o f)"), ALU.is_equal, ALU.mult)
                        nc.vector.tensor_scalar(match[b4][:, 1, :], keys_ps[b][0:T, 0:T],
                                                dprev[:, bass.ds(a.t, 1)], None, ALU.is_equal).then_inc(s_m, 1)

                    def add_bias(a):
                        b4, n = a.buf(4), a.use(4)
                        dve.wait_ge(s_tot, a.t + 1)
                        if not a.early(4):
                            dve.wait_ge(s_out[b4], stores * n)
                        nc.vector.scalar_tensor_tensor(res[b4][:, :], sum_ps[b4][0:T, :], 1.0 if first else 1.0 / 3.0, neigh_b[:, c0:c0 + D],
                                                       ALU.mult, ALU.add).then_inc(s_res, 1)

                    def step(a):
                        at(prepare, a.later(3))
                        at(add_bias, a)
                    tiles(dve, step, ET, UN, before=3)

                @block.tensor
                def _(pe):
                    def keys(a):
                        b = a.buf()
                        if not a.early(2):
                            pe.wait_ge(s_m, a.t - 1)
                        pe.wait_ge(s_now, a.t + 1)
                        nc.tensor.transpose(keys_ps[b][0:T, 0:T], key_now[b][:, :].to_broadcast([T, T]), ident[0:T, 0:T]).then_inc(s_key, 1)

                    def own_sums(a):
                        b4, n = a.buf(4), a.use(4)
                        pe.wait_ge(s_m, a.t + 1)
                        pe.wait_ge(s_g[b4], 16 * n + 16)
                        if not a.early(4):
                            pe.wait_ge(s_res, a.t - 3)
                        nc.tensor.matmul(sum_ps[b4][0:T, :], match[b4][:, 0, :], g[b4][:, :], start=True, stop=False)

                    def carried(a):
                        b, b4 = a.buf(), a.buf(4)
                        if a.early(1):
                            pe.wait_ge(s_zero, 1)
                        else:
                            pe.wait_ge(s_tot, a.t)
                        nc.tensor.matmul(sum_ps[b4][0:T, :], match[b4][:, 1, :], total[1 - b][:, :],
                                         start=False, stop=True).then_inc(s_sum, 1)

                    def step(a):
                        at(carried, a)
                        at(own_sums, a.later(2))
                        at(keys, a.later(4))
                    tiles(pe, step, ET, UN, before=4)

        sum_by_dst(True)
        end_part()

        with ExitStack() as ph:
            sb, ps = holder(ph)
            hi = [sb(f"h_hi{b}", [P, KC, P], F32R) for b in range(2)]
            lo = [sb(f"h_lo{b}", [P, KC, P], F32R) for b in range(2)]
            nb = [sb(f"h_nb{b}", [T, D]) for b in range(4)]
            pre = [sb(f"h_pre{b}", [T, D]) for b in range(2)]
            z = [sb(f"h_z{b}", [T, D]) for b in range(2)]
            pidx = [sb(f"h_idx{b}", [T, 1], I32) for b in range(4)]
            tp = [ps(f"h_tp{b}") for b in range(2)]
            out_ps = [ps(f"h_out{b}") for b in range(2)]
            h_nb, h_store = sems("h_nb", 4), sems("h_store")
            h_idx, h_fill, h_t, h_hi, h_lo, h_mm, h_pre, h_z = (sem(f"h_{n}") for n in ("idx", "fill", "t", "hi", "lo", "mm", "pre", "z"))
            UN = 4
            block = ph.enter_context(nc.Block())

            @block.sync
            def _(sp):
                def step(a):
                    b = a.buf()
                    sp.wait_ge(h_z, a.t + 1)
                    sp.dma_start(z2_rows[bass.ds(a.t * T, T), :], z[b][:, :]).then_inc(h_store[b], 16)
                tiles(sp, step, ET)
                for b in range(2):
                    sp.wait_ge(h_store[b], 16 * (ET // 2))

            @block.gpsimd
            def _(pool):
                bound = {"N": pool.to_reg(N - 1), "E": pool.to_reg(E - 1)}

                def fetch(a):
                    b4, n = a.buf(4), a.use(4)
                    if not a.early(4):
                        pool.wait_ge(h_nb[b4], 16 * n)
                    nc.gpsimd.tensor_copy(pidx[b4][:, :], in_place[:, bass.ds(a.t, 1)]).then_inc(h_idx, 1)
                    pool.wait_ge(h_idx, a.t + 1)
                    pool.wait_ge(h_fill, a.t + 1)
                    alone(pool)
                    pool.indirect_dma_start(nb[b4][:, :], None, neigh1, bass.IndirectOffsetOnAxis(ap=pidx[b4][:, 0:1], axis=0),
                                            bounds_check=bound["E"], oob_is_err=False).then_inc(h_nb[b4], 16)
                tiles(pool, fetch, ET, UN)

            @block.scalar
            def _(act):
                def fill(a):
                    b4 = a.buf(4)
                    if not a.early(4):
                        act.wait_ge(h_pre, a.t - 3)
                    nc.scalar.activation(nb[b4][:, :], neigh_b[:, 0:D], ACT.Copy).then_inc(h_fill, 1)

                def high(a):
                    b = a.buf()
                    act.wait_ge(h_t, a.t + 1)
                    if not a.early(2):
                        act.wait_ge(h_mm, a.t - 1)
                    nc.scalar.activation(hi[b][:, :, 0:T], chunks(tp[b][:, :]), ACT.Relu).then_inc(h_hi, 1)

                def keep(a):
                    b, n = a.buf(), a.use()
                    act.wait_ge(h_mm, a.t + 1)
                    if not a.early(2):
                        act.wait_ge(h_store[b], 16 * n)
                    nc.scalar.activation(z[b][:, :], out_ps[b][0:T, :], ACT.Copy).then_inc(h_z, 1)

                def step(a):
                    at(fill, a.later(3))
                    at(high, a)
                    at(keep, a.later(-1))
                tiles(act, step, ET, UN, before=3, after=1)

            @block.vector
            def _(dve):
                def add(a):
                    b, b4, n = a.buf(), a.buf(4), a.use(4)
                    dve.wait_ge(h_nb[b4], 16 * n + 16)
                    if not a.early(2):
                        dve.wait_ge(h_t, a.t - 1)
                    nc.vector.tensor_tensor(pre[b][:, :], m_all[:, bass.ds(a.t, 1), :].rearrange("p o d -> p (o d)"), nb[b4][:, :], ALU.add)\
                        .then_inc(h_pre, 1)

                def low(a):
                    b = a.buf()
                    dve.wait_ge(h_hi, a.t + 1)
                    nc.vector.scalar_tensor_tensor(lo[b][:, :, 0:T], chunks(tp[b][:, :]), 0.0, hi[b][:, :, 0:T].bitcast(F32),
                                                   ALU.max, ALU.subtract).then_inc(h_lo, 1)

                def step(a):
                    at(add, a.later(1))
                    at(low, a)
                tiles(dve, step, ET, UN, before=1)

            @block.tensor
            def _(pe):
                def turn(a):
                    b = a.buf()
                    pe.wait_ge(h_pre, a.t + 1)
                    if not a.early(2):
                        pe.wait_ge(h_lo, a.t - 1)
                    transpose_tile(tp[b], pre[b], ident).then_inc(h_t, 1)

                def project(a):
                    b = a.buf()
                    pe.wait_ge(h_lo, a.t + 1)
                    if not a.early(2):
                        pe.wait_ge(h_z, a.t - 1)
                    product(out_ps[b], hi[b], lo[b], conv2_w).then_inc(h_mm, 1)

                def step(a):
                    at(turn, a)
                    at(project, a.later(-1))
                tiles(pe, step, ET, UN, after=1)

        end_part()
        sum_by_dst(False)
        end_part()
        edges.close()
        with ExitStack() as ph:
            sb, ps = holder(ph)
            slots = sb("slots", [T, 2, NT], I32)
            diag = sb("diag", [T, 2, NT])
            xb = [sb(f"xb{b}", [T, D]) for b in range(4)]
            nb = [sb(f"nb{b}", [T, 2 * D]) for b in range(4)]
            pidx = [sb(f"n_idx{b}", [T, 2], I32) for b in range(8)]
            y = [sb(f"n_y{b}", [T, D]) for b in range(2)]
            x1 = [sb(f"n_x1_{b}", [T, D]) for b in range(8)]
            st, mv, rs = ([[sb(f"n_{n}{j}_{b}", [T, s]) for b in range(2)] for j in range(2)]
                          for n, s in (("st", 6), ("mv", 2), ("rs", 3)))
            hi1, lo1, hi2, lo2 = ([sb(f"n_{n}_{b}", [P, KC, P], F32R) for b in range(2)] for n in ("hi1", "lo1", "hi2", "lo2"))
            h1 = [sb(f"n_h1_{b}", [T, D]) for b in range(2)]
            h2 = [sb(f"n_h2_{b}", [T, D]) for b in range(2)]
            s2 = [sb(f"n_s{b}", [T, D]) for b in range(2)]
            res = [sb(f"n_res{b}", [T, D]) for b in range(2)]
            tp1, tp2, mm1, mm2 = ([ps(f"n_{n}_{b}") for b in range(2)] for n in ("tp1", "tp2", "mm1", "mm2"))
            n_in, n_u, n_nb = sems("n_in", 4), sems("n_u", 4), sems("n_nb", 4)
            n_store = sems("n_store")
            n_small, n_third, n_fill, n_idx = sem("n_small"), sem("n_third"), sem("n_fill"), sem("n_idx")
            (n_y, n_st1, n_ag1, n_dev1, n_rec1, n_off1, n_x1, n_t1, n_hi1, n_lo1, n_mm1, n_h1, n_t2, n_hi2, n_lo2, n_mm2,
             n_h2, n_s, n_st2, n_ag2, n_dev2, n_rec2, n_off2, n_res) = (
                sem(f"n_{n}") for n in ("y", "st1", "ag1", "dev1", "rec1", "off1", "x1", "t1", "hi1", "lo1", "mm1", "h1", "t2", "hi2",
                                        "lo2", "mm2", "h2", "s", "st2", "ag2", "dev2", "rec2", "off2", "res"))
            block = ph.enter_context(nc.Block())
            UN = 8

            def tile_rows(table, a):
                return table.rearrange("(p t) d -> p t d", p=T)[:, bass.ds(a.t, 1), :].rearrange("p o d -> p (o d)")

            @block.sync
            def _(sp):
                def load(a):
                    b4 = a.buf(4)
                    if not a.early(4):
                        sp.wait_ge(n_y, a.t - 3)
                    sp.dma_start(xb[b4][:, :], tile_rows(x, a)).then_inc(n_in[b4], 16)

                def store(a):
                    b = a.buf()
                    sp.wait_ge(n_res, a.t + 1)
                    sp.dma_start(tile_rows(out, a), res[b][:, :]).then_inc(n_store[b], 16)

                sp.dma_start(slots[:, 0, :], slot_src.rearrange("(p t) o -> p (t o)", p=T)).then_inc(n_small, 16)
                sp.dma_start(slots[:, 1, :], slot_dst.rearrange("(p t) o -> p (t o)", p=T)).then_inc(n_small, 16)
                sp.dma_start(diag[:, 0, :], node_vec.rearrange("(p t) -> p t", p=T)).then_inc(n_small, 16)

                def step(a):
                    at(load, a.later(6))
                    at(store, a.later(-3))
                tiles(sp, step, NT, UN, before=6, after=3)
                for b in range(2):
                    sp.wait_ge(n_store[b], 16 * (NT // 2))

            @block.gpsimd
            def _(pool):
                bound = {"N": pool.to_reg(N - 1), "E": pool.to_reg(E - 1)}
                pool.wait_ge(n_small, 48)

                def fetch_x(a):
                    n, b4, b8 = a.use(4), a.buf(4), a.buf(8)
                    if not a.early(8):
                        pool.wait_ge(n_u[b4], 16 * n - 16)
                        pool.wait_ge(n_nb[b4], 16 * n - 16)
                    nc.gpsimd.tensor_copy(pidx[b8][:, :], slots[:, :, bass.ds(a.t, 1)].rearrange("p j o -> p (j o)")).then_inc(n_idx, 1)
                    pool.wait_ge(n_idx, a.t + 1)
                    pool.wait_ge(n_in[b4], 16 * n + 16)
                    alone(pool)
                    pool.indirect_dma_start(xb[b4][:, :], None, x_new, bass.IndirectOffsetOnAxis(ap=pidx[b8][:, 0:1], axis=0),
                                            bounds_check=bound["E"], oob_is_err=False).then_inc(n_u[b4], 16)

                def fetch_nb(a):
                    b4, b8 = a.buf(4), a.buf(8)
                    pool.wait_ge(n_fill, a.t + 1)
                    alone(pool)
                    pool.indirect_dma_start(nb[b4][:, :], None, neigh, bass.IndirectOffsetOnAxis(ap=pidx[b8][:, 1:2], axis=0),
                                            bounds_check=bound["E"], oob_is_err=False).then_inc(n_nb[b4], 16)

                def add(a):
                    b, n, b4 = a.buf(), a.use(4), a.buf(4)
                    pool.wait_ge(n_u[b4], 16 * n + 16)
                    if not a.early(2):
                        pool.wait_ge(n_x1, a.t - 1)
                    nc.gpsimd.tensor_tensor(y[b][:, :], xb[b4][:, :], half_c[:, :], ALU.add).then_inc(n_y, 1)

                def step(a):
                    at(fetch_x, a.later(5))
                    at(add, a.later(4))
                    at(fetch_nb, a.later(1))
                tiles(pool, step, NT, UN, before=5)

            @block.scalar
            def _(act):
                def dev1(a):
                    b = a.buf()
                    act.wait_ge(n_ag1, a.t + 1)
                    if not a.early(2):
                        act.wait_ge(n_rec1, a.t - 1)
                    nc.scalar.activation(rs[0][b][:, 0:1], mv[0][b][:, 1:2], ACT.Sqrt, bias=eps[0:T, 1:2]).then_inc(n_dev1, 1)

                def norm1(a):
                    b, b8 = a.buf(), a.buf(8)
                    act.wait_ge(n_off1, a.t + 1)
                    if not a.early(8):
                        act.wait_ge(n_s, a.t - 7)
                    nc.scalar.activation(x1[b8][:, :], y[b][:, :], ACT.Identity, scale=rs[0][b][:, 1:2], bias=rs[0][b][:, 2:3])\
                        .then_inc(n_x1, 1)

                def fill(a):
                    b4 = a.buf(4)
                    if not a.early(4):
                        act.wait_ge(n_h2, a.t - 3)
                    nc.scalar.activation(nb[b4][:, :], neigh_b[:, :], ACT.Copy).then_inc(n_fill, 1)

                def high1(a):
                    b = a.buf()
                    act.wait_ge(n_t1, a.t + 1)
                    if not a.early(2):
                        act.wait_ge(n_mm1, a.t - 1)
                    nc.scalar.activation(hi1[b][:, :, 0:T], chunks(tp1[b][:, :]), ACT.Copy).then_inc(n_hi1, 1)

                def high2(a):
                    b = a.buf()
                    act.wait_ge(n_t2, a.t + 1)
                    if not a.early(2):
                        act.wait_ge(n_mm2, a.t - 1)
                    nc.scalar.activation(hi2[b][:, :, 0:T], chunks(tp2[b][:, :]), ACT.Relu).then_inc(n_hi2, 1)

                def dev2(a):
                    b = a.buf()
                    act.wait_ge(n_ag2, a.t + 1)
                    if not a.early(2):
                        act.wait_ge(n_rec2, a.t - 1)
                    nc.scalar.activation(rs[1][b][:, 0:1], mv[1][b][:, 1:2], ACT.Sqrt, bias=eps[0:T, 2:3]).then_inc(n_dev2, 1)

                def finish(a):
                    b, n = a.buf(), a.use()
                    act.wait_ge(n_off2, a.t + 1)
                    if not a.early(2):
                        act.wait_ge(n_store[b], 16 * n)
                    nc.scalar.activation(res[b][:, :], s2[b][:, :], ACT.Identity, scale=rs[1][b][:, 1:2], bias=rs[1][b][:, 2:3])\
                        .then_inc(n_res, 1)

                def step(a):
                    at(fill, a.later(1))
                    at(dev1, a.later(3))
                    at(dev2, a.later(-3))
                    at(high1, a.later(2))
                    at(high2, a.later(-1))
                    at(norm1, a.later(3))
                    at(finish, a.later(-3))
                tiles(act, step, NT, UN, before=3, after=3)

            @block.vector
            def _(dve):
                dve.wait_ge(n_small, 48)
                nc.vector.tensor_scalar(diag[:, 1, :], diag[:, 0, :], 1.0 / 3.0, None, ALU.mult).then_inc(n_third, 1)
                dve.wait_ge(n_third, 1)

                def stats1(a):
                    b = a.buf()
                    dve.wait_ge(n_y, a.t + 1)
                    nc.vector.bn_stats(st[0][b][:, :], y[b][:, :]).then_inc(n_st1, 1)

                def moments1(a):
                    b = a.buf()
                    dve.wait_ge(n_st1, a.t + 1)
                    alone(dve)
                    nc.vector.bn_aggr(mv[0][b][:, :], st[0][b][:, :]).then_inc(n_ag1, 1)

                def scale1(a):
                    b = a.buf()
                    dve.wait_ge(n_dev1, a.t + 1)
                    if not a.early(2):
                        dve.wait_ge(n_x1, a.t - 1)
                    nc.vector.reciprocal(rs[0][b][:, 1:2], rs[0][b][:, 0:1]).then_inc(n_rec1, 1)

                def offset1(a):
                    b = a.buf()
                    dve.wait_ge(n_rec1, a.t + 1)
                    nc.vector.tensor_scalar(rs[0][b][:, 2:3], mv[0][b][:, 0:1], rs[0][b][:, 1:2], -1.0, ALU.mult, ALU.mult)\
                        .then_inc(n_off1, 1)

                def low1(a):
                    b = a.buf()
                    dve.wait_ge(n_hi1, a.t + 1)
                    nc.vector.tensor_tensor(lo1[b][:, :, 0:T], chunks(tp1[b][:, :]), hi1[b][:, :, 0:T].bitcast(F32), ALU.subtract)\
                        .then_inc(n_lo1, 1)

                def hidden(a):
                    b, b4 = a.buf(), a.buf(4)
                    dve.wait_ge(n_mm1, a.t + 1)
                    dve.wait_ge(n_nb[b4], 16 * a.use(4) + 16)
                    if not a.early(2):
                        dve.wait_ge(n_t2, a.t - 1)
                    nc.vector.scalar_tensor_tensor(h1[b][:, :], mm1[b][0:T, :], diag[:, 0, bass.ds(a.t, 1)], nb[b4][:, 0:D],
                                                   ALU.mult, ALU.add).then_inc(n_h1, 1)

                def low2(a):
                    b = a.buf()
                    dve.wait_ge(n_hi2, a.t + 1)
                    nc.vector.scalar_tensor_tensor(lo2[b][:, :, 0:T], chunks(tp2[b][:, :]), 0.0, hi2[b][:, :, 0:T].bitcast(F32),
                                                   ALU.max, ALU.subtract).then_inc(n_lo2, 1)

                def hidden2(a):
                    b, b4 = a.buf(), a.buf(4)
                    dve.wait_ge(n_mm2, a.t + 1)
                    nc.vector.scalar_tensor_tensor(h2[b][:, :], mm2[b][0:T, :], diag[:, 1, bass.ds(a.t, 1)], nb[b4][:, D:2 * D],
                                                   ALU.mult, ALU.add).then_inc(n_h2, 1)

                def sum2(a):
                    b, b8 = a.buf(), a.buf(8)
                    dve.wait_ge(n_h2, a.t + 1)
                    if not a.early(2):
                        dve.wait_ge(n_res, a.t - 1)
                    nc.vector.scalar_tensor_tensor(s2[b][:, :], h2[b][:, :], 0.0, x1[b8][:, :], ALU.max, ALU.add).then_inc(n_s, 1)

                def stats2(a):
                    b = a.buf()
                    dve.wait_ge(n_s, a.t + 1)
                    nc.vector.bn_stats(st[1][b][:, :], s2[b][:, :]).then_inc(n_st2, 1)

                def moments2(a):
                    b = a.buf()
                    dve.wait_ge(n_st2, a.t + 1)
                    alone(dve)
                    nc.vector.bn_aggr(mv[1][b][:, :], st[1][b][:, :]).then_inc(n_ag2, 1)

                def scale2(a):
                    b = a.buf()
                    dve.wait_ge(n_dev2, a.t + 1)
                    if not a.early(2):
                        dve.wait_ge(n_res, a.t - 1)
                    nc.vector.reciprocal(rs[1][b][:, 1:2], rs[1][b][:, 0:1]).then_inc(n_rec2, 1)

                def offset2(a):
                    b = a.buf()
                    dve.wait_ge(n_rec2, a.t + 1)
                    nc.vector.tensor_scalar(rs[1][b][:, 2:3], mv[1][b][:, 0:1], rs[1][b][:, 1:2], -1.0, ALU.mult, ALU.mult)\
                        .then_inc(n_off2, 1)

                def step(a):
                    at(hidden2, a.later(-3))
                    at(stats1, a.later(3))
                    at(sum2, a.later(-3))
                    at(moments1, a.later(3))
                    at(stats2, a.later(-3))
                    at(hidden, a)
                    at(moments2, a.later(-3))
                    at(scale1, a.later(3))
                    at(low1, a.later(2))
                    at(offset1, a.later(3))
                    at(scale2, a.later(-3))
                    at(low2, a.later(-1))
                    at(offset2, a.later(-3))
                tiles(dve, step, NT, UN, before=3, after=3)

            @block.tensor
            def _(pe):
                def turn1(a):
                    b = a.buf()
                    pe.wait_ge(n_x1, a.t + 1)
                    if not a.early(2):
                        pe.wait_ge(n_lo1, a.t - 1)
                    transpose_tile(tp1[b], x1[a.buf(8)], ident).then_inc(n_t1, 1)

                def dense1(a):
                    b = a.buf()
                    pe.wait_ge(n_lo1, a.t + 1)
                    if not a.early(2):
                        pe.wait_ge(n_h1, a.t - 1)
                    product(mm1[b], hi1[b], lo1[b], dense1_w).then_inc(n_mm1, 1)

                def turn2(a):
                    b = a.buf()
                    pe.wait_ge(n_h1, a.t + 1)
                    if not a.early(2):
                        pe.wait_ge(n_lo2, a.t - 1)
                    transpose_tile(tp2[b], h1[b], ident).then_inc(n_t2, 1)

                def dense2(a):
                    b = a.buf()
                    pe.wait_ge(n_lo2, a.t + 1)
                    if not a.early(2):
                        pe.wait_ge(n_h2, a.t - 1)
                    product(mm2[b], hi2[b], lo2[b], dense2_w).then_inc(n_mm2, 1)

                def step(a):
                    at(dense1, a)
                    at(turn1, a.later(2))
                    at(turn2, a.later(-1))
                    at(dense2, a.later(-2))
                tiles(pe, step, NT, UN, before=2, after=2)


_INS = ['x', 'src', 'dst', 'edge_attr_8', 'edge_weight', 'node_vec',
        'L0_gnn_ln_g', 'L0_gnn_ln_b', 'L0_gnn_Wq', 'L0_gnn_bq', 'L0_gnn_Wk', 'L0_gnn_bk', 'L0_gnn_Wv', 'L0_gnn_bv',
        'L0_gnn_W1', 'L0_gnn_b1', 'L0_gnn_W2', 'L0_gnn_b2',
        'L1_gnn_W0_1', 'L1_gnn_W1_1', 'L1_gnn_b1', 'L1_gnn_W0_2', 'L1_gnn_W1_2', 'L1_gnn_b2']


def kernel(**inputs):
    import numpy as _np
    import concourse.bacc as _bacc
    from concourse import mybir as _mybir
    from concourse.bass_utils import run_bass_kernel_spmd as _run

    nc = _bacc.Bacc("TRN2", target_bir_lowering=False, num_devices=1)
    arrays, args = {}, []
    for name in _INS:
        a = _np.ascontiguousarray(inputs[name])
        arrays[f"in_{name}"] = a
        args.append(nc.dram_tensor(f"in_{name}", a.shape, _mybir.dt.from_np(a.dtype), kind="ExternalInput").ap())
    shape = inputs['x'].shape
    args.append(nc.dram_tensor("out_0", shape, _mybir.dt.float32, kind="ExternalOutput").ap())
    build(nc, *args)
    r = _run(nc, [arrays], core_ids=[0])
    return r.results[0]["out_0"]
```

```python
from contextlib import ExitStack

import concourse.bass as bass
from concourse import mybir

ALU = mybir.AluOpType
ACT = mybir.ActivationFunctionType
AX = mybir.AxisListType
F32 = mybir.dt.float32
F32R = mybir.dt.float32r
BF16 = mybir.dt.bfloat16
I32 = mybir.dt.int32

P = 128
D = 512
KC = D // P
H = 8
HD = D // H
T = 125
PARTS = (slice(0, 112), slice(112, T))
MOVED = 16 * len(PARTS)
EPS = 1e-5
FAR = 1000000
GAP = -3.0e38

WS = D
SRC, DST, EW, RANKB, DIAG = WS + H, WS + H + 1, WS + H + 2, WS + H + 3, WS + H + 4
ROW = DIAG + 4
FIELDS = ROW - WS


class Tile:

    def __init__(self, turn, c, unroll, count):
        self.turn, self.c, self.unroll, self.count = turn, c, unroll, count
        self.t = c if turn is None else turn * unroll + c

    def later(self, k):
        return Tile(self.turn, self.c + k, self.unroll, self.count)

    def buf(self, m=2):
        return self.c % m

    def use(self, m=2):
        return self.c // m if self.turn is None else self.turn * (self.unroll // m) + self.c // m

    def early(self, k):
        return self.turn is None and self.c < k

    def exists(self):
        return self.turn is not None or 0 <= self.c < self.count


def tiles(eng, step, count, unroll=2, before=0, after=0, skip=0):
    for c in range(skip - before, unroll):
        step(Tile(None, c, unroll, count))
    with eng.Fori(1, count // unroll - 1) as turn:
        for c in range(unroll):
            step(Tile(turn, c, unroll, count))
    for c in range(count - unroll, count + after):
        step(Tile(None, c, unroll, count))


def steps_ahead(step, first, end, count, unroll):
    for c in range(first, end):
        step(Tile(None, c, unroll, count))


def at(part, a):
    if a.exists():
        part(a)


def alone(eng):
    eng.nop(nofuse=True)


def build(nc, x, src, dst, attr, ew, node_vec, ln_g, ln_b, wq, bq, wk, bk, wv, bv, w1, b1, w2, b2,
          w01, w11, gb1, w02, w12g, gb2, out):
    N = x.shape[0]
    E = src.shape[0]
    NT, ET = N // T, E // T
    SCALE = HD ** -0.5
    CENTRE = N * E // 2

    def dram(name, shape, dt):
        return nc.dram_tensor(name, shape, dt, kind="Internal").ap()

    by_src = dram("by_src", (E, ROW), F32)
    x_by_src = dram("x_by_src", (E, D), F32)
    by_dst = dram("by_dst", (E + 1, 4), F32)
    x_new = dram("x_new", (E, D), F32)
    z_rows = dram("z_rows", (E, D), F32)
    z2_rows = dram("z2_rows", (E, D), F32)
    neigh = dram("neigh", (E, 2 * D), F32)
    neigh1 = dram("neigh1", (E, D), F32)
    slot_src = dram("slot_src", (N, 1), I32)
    slot_dst = dram("slot_dst", (N, 1), I32)
    src_col = src.rearrange("(p t) -> p t", p=T)
    dst_col = dst.rearrange("(p t) -> p t", p=T)
    ew_col = ew.rearrange("(p t) -> p t", p=T)
    vec_rows = node_vec.rearrange("(n o) -> n o", o=1)

    whole = ExitStack()

    def holder(stack):
        def sb(name, shape, dt=F32):
            return stack.enter_context(nc.sbuf_tensor(name, shape, dt))

        def ps(name, shape=(P, D)):
            return stack.enter_context(nc.psum_tensor(name, list(shape), F32))
        return sb, ps

    part_sems = []

    def sem(name):
        part_sems.append(nc.alloc_semaphore(name))
        return part_sems[-1]

    def end_part():
        nc.clear_and_free_semaphores(part_sems)
        nc.all_engine_barrier()
        part_sems.clear()

    def sems(name, n=2):
        return [sem(f"{name}_buf{i}") for i in range(n)]

    def weight_rows(w):
        return w.rearrange("(k p) n -> p k n", p=P)

    def columns(v):
        return v.rearrange("(k p) -> p k", p=P)

    def row_for_all(v, n=T):
        return v.rearrange("(o d) -> o d", o=1).to_broadcast([n, v.shape[0]])

    def chunks(a):
        return a.rearrange("p (k c) -> p k c", k=KC)[:, :, 0:T]

    def transpose_tile(bank, rows, ident):
        for k in range(KC):
            last = nc.tensor.transpose(bank[:, P * k:P * k + T], rows[:, P * k:P * (k + 1)], ident[0:T, 0:T])
        return last

    def product(bank, hi, lo, w):
        w_hi, w_lo = w
        n = 0
        for k in range(KC):
            for a, b in ((hi, w_hi), (hi, w_lo), (lo, w_hi)):
                last = nc.tensor.matmul(bank[0:T, :], a[:, k, 0:T], b[:, k, :], start=(n == 0), stop=(n == 3 * KC - 1))
                n += 1
        return last

    whole.enter_context(nc.allow_non_contiguous_dma(reason="small columns"))
    with whole:
        sb, _ = holder(whole)
        ident = sb("ident", [P, P])
        eps = sb("eps", [P, 3])
        conv2_w = [sb(f"w_slot0_{p}", [P, KC, D], F32R) for p in ("hi", "lo")]
        dense2_w = [sb(f"w_slot1_{p}", [P, KC, D], F32R) for p in ("hi", "lo")]
        q_w, k_w = conv2_w, dense2_w
        attn_w = [sb(f"w_attn_{p}", [P, KC, D], F32R) for p in ("hi", "lo")]
        dense1_w = [sb(f"w_dense1_{p}", [P, KC, D], F32R) for p in ("hi", "lo")]
        conv1_w = [sb(f"w_conv1_{p}", [P, KC, D], F32R) for p in ("hi", "lo")]
        half_c = sb("half_c", [T, D])
        neigh_b = sb("neigh_b", [T, 2 * D])

        with ExitStack() as ph:
            sb, ps = holder(ph)
            v_w = [sb(f"w_v_{p}", [P, KC, D], F32R) for p in ("hi", "lo")]
            q_bias, k_bias, v_bias = (sb(f"{n}_bias", [T, D]) for n in "qkv")
            edge_i = sb("edge_i", [T, 2, ET], I32)
            edge_f = sb("edge_f", [T, 3, ET])
            attr_s = sb("attr_s", [T, ET, H])
            key_row = sb("key_row", [T, 2, E])
            key_col = sb("key_col", [T, 2, ET])
            sums = sb("sums", [T, 2, ET])

            xg = [[sb(f"xg{j}_{b}", [T, D]) for b in range(4)] for j in range(2)]
            dg = [sb(f"dg{b}", [T, 1]) for b in range(4)]
            diag_col = sb("diag_col", [T, ET])
            idx = [sb(f"idx{b}", [T, 2], I32) for b in range(4)]
            rank_i = [sb(f"rank_i{b}", [T, 1], I32) for b in range(4)]
            st = [sb(f"st{b}", [T, 2, 6]) for b in range(2)]
            mv = [sb(f"mv{b}", [T, 2, 2]) for b in range(2)]
            rs = [sb(f"rs{b}", [T, 2, 2]) for b in range(2)]
            xh = [[sb(f"xh{j}_{b}", [T, D]) for b in range(2)] for j in range(2)]
            hi = [[sb(f"p_hi{j}_{b}", [P, KC, P], F32R) for b in range(2)] for j in range(2)]
            lo = [[sb(f"p_lo{j}_{b}", [P, KC, P], F32R) for b in range(2)] for j in range(2)]
            tp = [ps(f"p_tp{j}") for j in range(2)]
            got_x = [sems("got_xs", 4), sems("got_xd", 4)]
            got_diag, sent_x, sent_row = sems("got_diag", 4), sems("sent_x", 4), sems("sent_row", 4)
            p_idx, p_place, p_dg = sem("p_idx"), sem("p_place"), sem("p_dg")
            p_stats, p_aggr, p_dev, p_rec, p_xh = sem("p_stats"), sem("p_aggr"), sem("p_dev"), sem("p_rec"), sem("p_xh")
            p_t, p_hi, p_lo = sem("p_t"), sem("p_hi"), sem("p_lo")
            p_mm = [sem(f"p_mm_{n}") for n in "qkv"]
            p_q, p_k, p_v, p_qk, p_sc, p_row = sem("p_q"), sem("p_k"), sem("p_v"), sem("p_qk"), sem("p_sc"), sem("p_row")
            p_rank = [sem("p_rank_src"), sem("p_rank_dst")]
            project_sems = list(part_sems)
            part_sems.clear()
            UN = 4

            def project_gpsimd(pool, ahead):
                bound = {"N": pool.to_reg(N - 1), "E": pool.to_reg(E - 1)}

                def fetch(a):
                    b4, n = a.buf(4), a.use(4)
                    if not a.early(4):
                        pool.wait_ge(sent_x[b4], 16 * n)
                        pool.wait_ge(p_xh, a.t - 3)
                        pool.wait_ge(p_dg, a.t - 3)
                        pool.wait_ge(got_diag[b4], 16 * n)
                        pool.wait_ge(got_x[0][b4], 16 * n)
                        pool.wait_ge(got_x[1][b4], 16 * n)
                    nc.gpsimd.tensor_copy(idx[b4][:, :], edge_i[:, :, bass.ds(a.t, 1)].rearrange("p j o -> p (j o)"))\
                        .then_inc(p_idx, 1)
                    pool.wait_ge(p_idx, a.t + 1)
                    for j in range(2):
                        alone(pool)
                        pool.indirect_dma_start(xg[j][b4][:, :], None, x,
                                                bass.IndirectOffsetOnAxis(ap=idx[b4][:, j:j + 1], axis=0),
                                                bounds_check=bound["N"], oob_is_err=False).then_inc(got_x[j][b4], 16)
                    alone(pool)
                    pool.indirect_dma_start(dg[b4][:, :], None, vec_rows, bass.IndirectOffsetOnAxis(ap=idx[b4][:, 0:1], axis=0),
                                            bounds_check=bound["N"], oob_is_err=False).then_inc(got_diag[b4], 16)

                def send_x(a):
                    b4 = a.buf(4)
                    pool.wait_ge(p_place, a.t + 1)
                    pool.wait_ge(got_x[0][b4], 16 * a.use(4) + 16)
                    alone(pool)
                    pool.indirect_dma_start(x_by_src, bass.IndirectOffsetOnAxis(ap=rank_i[b4][:, :], axis=0), xg[0][b4][:, :], None,
                                            bounds_check=bound["E"], oob_is_err=False).then_inc(sent_x[b4], 16)

                def multiply(a):
                    b = a.buf()
                    pool.wait_ge(p_k, a.t + 1)
                    if not a.early(2):
                        pool.wait_ge(p_sc, a.t - 1)
                    nc.gpsimd.tensor_tensor(qk[b][:, :], qs[b][:, :], ks[b][:, :], ALU.mult).then_inc(p_qk, 1)

                def send_row(a):
                    b, b4 = a.buf(), a.buf(4)
                    pool.wait_ge(p_row, a.t + 1)
                    alone(pool)
                    pool.indirect_dma_start(by_src, bass.IndirectOffsetOnAxis(ap=rank_i[b4][:, :], axis=0), row[b][:, :], None,
                                            bounds_check=bound["E"], oob_is_err=False).then_inc(sent_row[b4], 16)

                def step(a):
                    at(multiply, a.later(-1))
                    at(fetch, a.later(4))
                    at(send_x, a.later(1))
                    at(send_row, a.later(-1))

                if ahead:
                    for c in range(4):
                        fetch(Tile(None, c, UN, ET))
                    return
                send_x(Tile(None, 0, UN, ET))
                tiles(pool, step, ET, UN, after=1)
                for b4 in range(4):
                    pool.wait_ge(sent_row[b4], 16 * (ET // 4))
                    pool.wait_ge(sent_x[b4], 16 * (ET // 4))

            def project_scalar(act, ahead):
                def high(a):
                    b = a.buf()
                    act.wait_ge(p_t, a.t + 1)
                    if not a.early(2):
                        act.wait_ge(p_mm[2], a.t - 1)
                    nc.scalar.activation(hi[0][b][:, :, 0:T], chunks(tp[0][:, :]), ACT.Copy)
                    nc.scalar.activation(hi[1][b][:, :, 0:T], chunks(tp[1][:, :]), ACT.Copy).then_inc(p_hi, 1)

                def deviation(a):
                    b = a.buf()
                    act.wait_ge(p_aggr, a.t + 1)
                    if not a.early(2):
                        act.wait_ge(p_rec, a.t - 1)
                    nc.scalar.activation(rs[b][:, :, 0:1], mv[b][:, :, 1:2], ACT.Sqrt, bias=eps[0:T, 0:1]).then_inc(p_dev, 1)

                def rank(a, j):
                    if not a.early(1):
                        act.wait_ge(p_rank[j], a.t)
                    nc.scalar.activation(waste[:, j, :], key_row[:, j, :], ACT.Sign, scale=-1.0,
                                         bias=key_col[:, j, bass.ds(a.t, 1)],
                                         accum_out=sums[:, j, bass.ds(a.t, 1)]).then_inc(p_rank[j], 1)

                def rank_src(a):
                    rank(a, 0)

                def rank_dst(a):
                    rank(a, 1)

                def norms(a):
                    at(deviation, a.later(3))
                    at(high, a.later(1))

                def step(a):
                    at(deviation, a.later(3))
                    at(rank_src, a.later(1))
                    at(high, a.later(1))
                    at(rank_dst, a.later(1))

                if ahead:
                    steps_ahead(norms, *ahead, ET, UN)
                    return
                rank_src(Tile(None, 0, UN, ET))
                rank_dst(Tile(None, 0, UN, ET))
                tiles(act, step, ET, UN)

            def project_vector(dve, ahead):
                def stats(a):
                    b, b4, n = a.buf(), a.buf(4), a.use(4)
                    for j in range(2):
                        dve.wait_ge(got_x[j][b4], 16 * n + 16)
                        nc.vector.bn_stats(st[b][:, j, :], xg[j][b4][:, :]).then_inc(p_stats, 1)

                def moments(a):
                    b = a.buf()
                    for j in range(2):
                        dve.wait_ge(p_stats, 2 * a.t + 1 + j)
                        alone(dve)
                        last = nc.vector.bn_aggr(mv[b][:, j, :], st[b][:, j, :])
                    last.then_inc(p_aggr, 1)

                def keep_diag(a):
                    b4, n = a.buf(4), a.use(4)
                    dve.wait_ge(got_diag[b4], 16 * n + 16)
                    nc.vector.tensor_copy(diag_col[:, bass.ds(a.t, 1)], dg[b4][:, :]).then_inc(p_dg, 1)

                def reciprocal(a):
                    b = a.buf()
                    dve.wait_ge(p_dev, a.t + 1)
                    nc.vector.reciprocal(rs[b][:, :, 1:2], rs[b][:, :, 0:1]).then_inc(p_rec, 1)

                def norm(a):
                    b, b4 = a.buf(), a.buf(4)
                    dve.wait_ge(p_rec, a.t + 1)
                    if not a.early(2):
                        dve.wait_ge(p_t, a.t - 1)
                    for j in range(2):
                        last = nc.vector.tensor_scalar(xh[j][b][:, :], xg[j][b4][:, :], mv[b][:, j, 0:1], rs[b][:, j, 1:2],
                                                       ALU.subtract, ALU.mult)
                    last.then_inc(p_xh, 1)

                def low(a):
                    b = a.buf()
                    dve.wait_ge(p_hi, a.t + 1)
                    for j in range(2):
                        last = nc.vector.tensor_tensor(lo[j][b][:, :, 0:T], chunks(tp[j][:, :]), hi[j][b][:, :, 0:T].bitcast(F32),
                                                       ALU.subtract)
                    last.then_inc(p_lo, 1)

                def place(a):
                    b4, n = a.buf(4), a.use(4)
                    dve.wait_ge(p_rank[0], a.t + 1)
                    if not a.early(4):
                        dve.wait_ge(sent_row[b4], 16 * n)
                        dve.wait_ge(sent_x[b4], 16 * n)
                    nc.vector.tensor_scalar(rank_i[b4][:, :], sums[:, 0, bass.ds(a.t, 1)], float(E - 1), 0.5, ALU.add, ALU.mult)\
                        .then_inc(p_place, 1)

                def q_rows(a):
                    b = a.buf()
                    dve.wait_ge(p_mm[0], a.t + 1)
                    if not a.early(2):
                        dve.wait_ge(p_qk, a.t - 1)
                    nc.vector.tensor_tensor(qs[b][:, :], qkv[0][b][0:T, :], q_bias[:, :], ALU.add).then_inc(p_q, 1)

                def k_rows(a):
                    b = a.buf()
                    dve.wait_ge(p_mm[1], a.t + 1)
                    nc.vector.tensor_tensor(ks[b][:, :], qkv[1][b][0:T, :], k_bias[:, :], ALU.add).then_inc(p_k, 1)

                def v_rows(a):
                    b = a.buf()
                    dve.wait_ge(p_mm[2], a.t + 1)
                    if not a.early(2):
                        o = a.later(-2)
                        dve.wait_ge(sent_row[o.buf(4)], 16 * o.use(4) + 16)
                    nc.vector.tensor_tensor(row[b][:, 0:D], qkv[2][b][0:T, :], v_bias[:, :], ALU.add).then_inc(p_v, 1)
                    dve.wait_ge(p_rank[1], a.t + 1)
                    nc.vector.tensor_scalar(row[b][:, RANKB:RANKB + 1], sums[:, 1, bass.ds(a.t, 1)], float(E - 1), 0.5, ALU.add, ALU.mult)
                    nc.vector.tensor_copy(row[b][:, SRC:EW + 1], edge_f[:, :, bass.ds(a.t, 1)].rearrange("p j o -> p (j o)"))
                    nc.vector.tensor_copy(row[b][:, DIAG:DIAG + 1], diag_col[:, bass.ds(a.t, 1)])
                    nc.vector.memset(row[b][:, DIAG + 1:ROW], 0.0)

                def scores(a):
                    b = a.buf()
                    dve.wait_ge(p_qk, a.t + 1)
                    nc.vector.tensor_reduce(score[b][:, :], qk[b][:, :].rearrange("p (h d) -> p h d", h=H), axis=AX.X, op=ALU.add)\
                        .then_inc(p_sc, 1)

                def weigh(a):
                    b = a.buf()
                    dve.wait_ge(p_sc, a.t + 1)
                    nc.vector.scalar_tensor_tensor(row[b][:, WS:WS + H], score[b][:, :], SCALE,
                                                   attr_s[:, bass.ds(a.t, 1), :].rearrange("p o h -> p (o h)"),
                                                   ALU.mult, ALU.mult).then_inc(p_row, 1)

                def step(a):
                    at(v_rows, a.later(-1))
                    at(stats, a.later(3))
                    at(scores, a.later(-1))
                    at(moments, a.later(3))
                    at(norm, a.later(2))
                    at(weigh, a.later(-1))
                    at(q_rows, a)
                    at(keep_diag, a.later(3))
                    at(reciprocal, a.later(3))
                    at(place, a.later(1))
                    at(low, a.later(1))
                    at(k_rows, a)

                def norms(a):
                    at(stats, a.later(3))
                    at(moments, a.later(3))
                    at(norm, a.later(2))
                    at(keep_diag, a.later(3))
                    at(reciprocal, a.later(3))
                    at(low, a.later(1))

                if ahead:
                    steps_ahead(norms, *ahead, ET, UN)
                    return
                place(Tile(None, 0, UN, ET))
                tiles(dve, step, ET, UN, after=1)

            def project_tensor(pe, ahead):
                def turn(a):
                    b = a.buf()
                    pe.wait_ge(p_xh, a.t + 1)
                    if not a.early(1):
                        pe.wait_ge(p_lo, a.t)
                    for j in range(2):
                        last = transpose_tile(tp[j], xh[j][b], ident)
                    last.then_inc(p_t, 1)

                def project(a, n):
                    b = a.buf()
                    side, w, free = ((0, q_w, p_q), (1, k_w, p_k), (1, v_w, p_v))[n]
                    pe.wait_ge(p_lo, a.t + 1)
                    if not a.early(2):
                        pe.wait_ge(free, a.t - 1)
                    product(qkv[n][b], hi[side][b], lo[side][b], w).then_inc(p_mm[n], 1)

                def step(a):
                    if a.exists():
                        project(a, 0)
                    at(turn, a.later(1))
                    if a.exists():
                        project(a, 1)
                        project(a, 2)
                if ahead:
                    turn(Tile(None, 0, UN, ET))
                    return
                tiles(pe, step, ET, UN)

            with ExitStack() as ph0:
                sb0, ps0 = holder(ph0)
                stage = [sb0(f"stage{i}", [P, KC, D]) for i in range(3)]
                gain = sb0("gain", [P, KC])
                shift = sb0("shift", [P, KC])
                node_row = sb0("node_row", [T, E], I32)
                number_c = sb0("number_c", [T, ET], I32)
                far = sb0("far", [T, NT], I32)
                table = sb0("table0", [1, 1])
                sentinel = sb0("sentinel", [1, 4])
                bias_ps = [ps0(f"bias_ps{i}") for i in range(2)]
                w_in, number_made = sems("w_in", 3), sems("number_made")
                small_in, rows_in, edge_in, norm_in = sem("small_in"), sem("rows_in"), sem("edge_in"), sem("norm_in")
                bias_in = sem("bias_in")
                made, ident0, ident1, eps_made = sem("made"), sem("ident0"), sem("ident1"), sem("eps_made")
                w_high, w_done, bias_mm, bias_done = sem("w_high"), sem("w_done"), sem("bias_mm"), sem("bias_done")
                keys_done, far_out = sem("keys_done"), sem("far_out")
                block = nc.Block()
                block = ph0.enter_context(block)

                @block.sync
                def _(sp):
                    sp.dma_start(edge_i[:, 0, :], src_col).then_inc(edge_in, 16)
                    sp.dma_start(edge_i[:, 1, :], dst_col).then_inc(edge_in, 16)
                    for i, w in enumerate((wq, wk, wv)):
                        sp.dma_start(stage[i][:, :, :], weight_rows(w)).then_inc(w_in[i], 16)
                    for b, v in ((q_bias, bq), (k_bias, bk), (v_bias, bv)):
                        sp.dma_start(b[:, :], row_for_all(v)).then_inc(bias_in, 16)
                    sp.dma_start(edge_f[:, 2, :], ew_col).then_inc(small_in, 16)
                    sp.dma_start(attr_s[:, :, :], attr.rearrange("(p t) h -> p t h", p=T)).then_inc(small_in, 16)
                    sp.wait_ge(made, 3)
                    sp.dma_start(slot_src.rearrange("(p t) o -> p (t o)", p=T), far[:, :]).then_inc(far_out, 16)
                    sp.dma_start(slot_dst.rearrange("(p t) o -> p (t o)", p=T), far[:, :]).then_inc(far_out, 16)
                    sp.dma_start(by_dst[E:E + 1, :], sentinel[:, :]).then_inc(far_out, 16)
                    sp.wait_ge(far_out, 48)

                @block.scalar
                def _(act):
                    act.dma_start(gain[:, :], columns(ln_g)).then_inc(norm_in, 16)
                    act.dma_start(shift[:, :], columns(ln_b)).then_inc(norm_in, 16)
                    for rows in PARTS:
                        act.dma_start(node_row[rows, :], row_for_all(src)[rows, :]).then_inc(rows_in, 16)
                    act.wait_ge(eps_made, 3)
                    nc.scalar.activation(table[:, :], eps[0:1, 0:1], ACT.Sqrt)
                    act.wait_ge(norm_in, 32)
                    for i, w in enumerate((q_w, k_w, v_w)):
                        act.wait_ge(w_in[i], 16)
                        for k in range(KC):
                            last = nc.scalar.activation(w[0][:, k, :], stage[i][:, k, :], ACT.Copy, scale=gain[:, k:k + 1])
                        last.then_inc(w_high, 1)
                        if i == 1:
                            act.wait_ge(keys_done, 1)
                            for rows in PARTS:
                                act.dma_start(node_row[rows, :], row_for_all(dst)[rows, :]).then_inc(rows_in, 16)
                    project_scalar(act, (-3, 0))

                @block.gpsimd
                def _(pool):
                    nc.gpsimd.memset(ident[:, :], 0.0).then_inc(ident0, 1)
                    nc.gpsimd.iota(key_row[:, 0, :].bitcast(I32), [[1, E]], base=-CENTRE, channel_multiplier=0).then_inc(number_made[0], 1)
                    nc.gpsimd.iota(number_c[:, :], [[1, ET]], base=-CENTRE, channel_multiplier=ET).then_inc(made, 1)
                    nc.gpsimd.iota(far[:, :], [[0, NT]], base=FAR, channel_multiplier=0).then_inc(made, 1)
                    nc.gpsimd.memset(sentinel[:, :], -1.0).then_inc(made, 1)
                    pool.wait_ge(ident0, 1)
                    nc.gpsimd.affine_select(out=ident[:, :], in_=ident[:, :], compare_op=ALU.not_equal, fill=1.0,
                                            base=0, pattern=[[-1, P]], channel_multiplier=1).then_inc(ident1, 1)
                    pool.wait_ge(edge_in, 32)
                    project_gpsimd(pool, True)
                    nc.gpsimd.iota(key_row[:, 1, :].bitcast(I32), [[1, E]], base=-CENTRE, channel_multiplier=0).then_inc(number_made[1], 1)

                @block.vector
                def _(dve):
                    for i, v in enumerate((EPS, EPS / 4, EPS / 2.25)):
                        nc.vector.memset(eps[:, i:i + 1], v).then_inc(eps_made, 1)
                    def low_part(i):
                        w = (q_w, k_w, v_w)[i]
                        dve.wait_ge(w_high, i + 1)
                        for k in range(KC):
                            last = nc.vector.scalar_tensor_tensor(
                                w[1][:, k, :], stage[i][:, k, :], gain[:, k:k + 1],
                                w[0][:, k, :].bitcast(F32), ALU.mult, ALU.subtract)
                        last.then_inc(w_done, 1)

                    def bias(i):
                        dve.wait_ge(bias_mm, i + 1)
                        dve.wait_ge(bias_in, 48)
                        b = (q_bias, k_bias, v_bias)[i]
                        nc.vector.tensor_tensor(b[:, :], bias_ps[i % 2][0:T, :], b[:, :], ALU.add).then_inc(bias_done, 1)

                    def keys(j):
                        dve.wait_ge(number_made[j], 1)
                        nc.vector.scalar_tensor_tensor(key_row[:, j, :], node_row[:, :], float(E), key_row[:, j, :].bitcast(I32),
                                                       ALU.mult, ALU.add).then_inc(keys_done, 1)

                    low_part(0)
                    dve.wait_ge(made, 2)
                    dve.wait_ge(rows_in, MOVED)
                    keys(0)
                    dve.wait_ge(edge_in, 32)
                    for j in range(2):
                        nc.vector.scalar_tensor_tensor(key_col[:, j, :], edge_i[:, j, :], float(E), number_c[:, :],
                                                       ALU.mult, ALU.add)
                        nc.vector.tensor_copy(edge_f[:, j, :], edge_i[:, j, :])
                    low_part(1)
                    low_part(2)
                    bias(0)
                    bias(1)
                    project_vector(dve, (-3, 0))
                    dve.wait_ge(rows_in, 2 * MOVED)
                    keys(1)
                    bias(2)
                    dve.wait_ge(small_in, 32)

                @block.tensor
                def _(pe):
                    pe.wait_ge(norm_in, 32)
                    for i in range(3):
                        pe.wait_ge(w_in[i], 16)
                        if i >= 2:
                            pe.wait_ge(bias_done, i - 1)
                        for k in range(KC):
                            last = nc.tensor.matmul(bias_ps[i % 2][0:T, :], shift[:, k:k + 1].to_broadcast([P, T]),
                                                    stage[i][:, k, :], start=(k == 0), stop=(k == KC - 1))
                        last.then_inc(bias_mm, 1)
                    pe.wait_ge(ident1, 1)
                    project_tensor(pe, True)

            end_part()
            part_sems.extend(project_sems)
            with ExitStack() as ph1:
                sb1, ps1 = holder(ph1)
                row = [sb1(f"row{b}", [T, ROW]) for b in range(2)]
                qs, ks, qk = ([sb1(f"{n}{b}", [T, D]) for b in range(2)] for n in ("qs", "ks", "qk"))
                score = [sb1(f"score{b}", [T, H]) for b in range(2)]
                waste = sb1("waste", [T, 2, E], BF16)
                qkv = [[ps1(f"p_{n}{b}") for b in range(2)] for n in "qkv"]
                block = ph1.enter_context(nc.Block())

                @block.gpsimd
                def _(pool):
                    project_gpsimd(pool, False)

                @block.scalar
                def _(act):
                    project_scalar(act, None)

                @block.vector
                def _(dve):
                    project_vector(dve, None)

                @block.tensor
                def _(pe):
                    project_tensor(pe, False)

        end_part()
        by_dst_s = whole.enter_context(nc.sbuf_tensor("by_dst_s", [T, ET, 4], F32))
        near = whole.enter_context(nc.sbuf_tensor("src_fields", [T, ET, FIELDS], F32))
        place_i = whole.enter_context(nc.sbuf_tensor("place_i", [T, 4, ET], I32))
        PLACE, SLOT, RB, SRCI = range(4)
        rec_den = whole.enter_context(nc.sbuf_tensor("rec_den", [T, ET, H], F32))
        e_col = whole.enter_context(nc.sbuf_tensor("e_col", [T, ET, H], F32))
        prev_key = whole.enter_context(nc.sbuf_tensor("prev_key", [T, ET + 1], F32))
        last_row = whole.enter_context(nc.sbuf_tensor("last_row", [T, 1], F32))
        with ExitStack() as ph:
            sb, ps = holder(ph)
            R = H + 1
            QT = 4
            NB = ET // QT
            key9 = sb("key9", [R, E])
            val9 = sb("val9", [R, E])
            table = sb("table", [1, 1])
            run = sb("run", [R, E])
            top = sb("top", [R, E])
            same = sb("same", [R, E + 1])
            gap = sb("gap", [R, E + 1])
            place_f = sb("place_f", [T, ET])
            ends = sb("ends", [T, ET])
            stage = [sb(f"stage_b{i}", [P, KC, D]) for i in range(3)]
            w1_rows = sb("w1_rows", [P, KC, D])
            w2_parts = [sb(f"w2_{p}", [P, KC, D], F32R) for p in ("hi", "lo")]
            w1t = [sb(f"w1t_{p}", [P, KC, P], F32R) for p in ("hi", "lo")]
            b1_col = sb("b1_col", [P, KC])
            field9 = sb("field9", [T, ET, R])
            banks = ps("wide", (P, NB, D))
            one = ps("one_bank")
            two = ps("two_bank")
            three = ps("three_bank")
            wide = banks[0:R, :, 0:QT * T]
            s_in, s_small, s_bias = sem("s_in"), sem("s_small"), sem("s_bias")
            s_w_in, s_w1_in = sems("s_w_in", 3), sem("s_w1_in")
            s_pos, s_f9, s_t = sem("s_pos"), sem("s_f9"), sem("s_t")
            s_ev, s_same, s_gap, s_run, s_top, s_d, s_e, s_sum = (sem(f"s_{n}") for n in ("ev", "same", "gap", "run", "top", "d", "e", "sum"))
            s_ev2 = sem("s_ev2")
            s_back, s_got, s_end, s_c = sem("s_back"), sem("s_got"), sem("s_end"), sem("s_c")
            s_hi, s_lo, s_w1t, s_w1h, s_w1l, s_w12, s_w12h, s_w12l, s_cmm, s_cev = (
                sem(f"s_{n}") for n in ("hi", "lo", "w1t", "w1h", "w1l", "w12", "w12h", "w12l", "cmm", "cev"))
            block = ph.enter_context(nc.Block())
            loads = ((w2, w2_parts), (w01, dense1_w), (w11, conv1_w))

            @block.sync
            def _(sp):
                for rows in PARTS:
                    sp.dma_start(near[rows, :, :], by_src[:, WS:ROW].rearrange("(t p) f -> p t f", p=T)[rows, :, :]).then_inc(s_in, 16)
                sp.dma_start(b1_col[:, :], columns(b1)).then_inc(s_small, 16)
                sp.dma_start(stage[0][:, :, :], weight_rows(w2)).then_inc(s_w_in[0], 16)
                sp.dma_start(half_c[:, :], row_for_all(b2)).then_inc(s_bias, 16)
                sp.dma_start(neigh_b[:, 0:D], row_for_all(gb1)).then_inc(s_bias, 16)
                sp.dma_start(neigh_b[:, D:2 * D], row_for_all(gb2)).then_inc(s_bias, 16)
                sp.dma_start(w1_rows[:, :, :], weight_rows(w1)).then_inc(s_w1_in, 16)
                for i in range(1, len(loads)):
                    sp.dma_start(stage[i][:, :, :], weight_rows(loads[i][0])).then_inc(s_w_in[i], 16)

            @block.gpsimd
            def _(pool):
                nc.gpsimd.iota(place_i[:, PLACE, :], [[T, ET]], base=0, channel_multiplier=1).then_inc(s_pos, 1)
                nc.gpsimd.memset(last_row[:, :], 0.0).then_inc(s_pos, 1)
                pool.wait_ge(s_pos, 2)
                nc.gpsimd.affine_select(out=last_row[:, :], in_=last_row[:, :], compare_op=ALU.not_equal, fill=1.0,
                                        base=-(T - 1), pattern=[[0, 1]], channel_multiplier=1).then_inc(s_pos, 1)
                for i, (_, w) in enumerate(loads):
                    pool.wait_ge(s_hi, i + 1)
                    for k in range(KC):
                        last = nc.gpsimd.tensor_tensor(w[1][:, k, :], stage[i][:, k, :], w[0][:, k, :].bitcast(F32), ALU.subtract)
                    last.then_inc(s_lo, 1)

            @block.scalar
            def _(act):
                def high(i):
                    act.wait_ge(s_w_in[i], 16)
                    for k in range(KC):
                        last = nc.scalar.activation(loads[i][1][0][:, k, :], stage[i][:, k, :], ACT.Copy)
                    last.then_inc(s_hi, 1)

                def high_w1(m):
                    act.wait_ge(s_w1t, m + 1)
                    if m:
                        act.wait_ge(s_w12, m)
                    nc.scalar.activation(w1t[0][:, :, :], one[:, :].rearrange("p (k c) -> p k c", k=KC), ACT.Copy).then_inc(s_w1h, 1)

                def high_w12(m):
                    act.wait_ge(s_w12, m + 1)
                    nc.scalar.activation(attn_w[0][:, m, :], two[:, :], ACT.Copy).then_inc(s_w12h, 1)

                nc.scalar.activation(table[:, :], eps[0:1, 0:1], ACT.Exp)
                high(0)
                act.wait_ge(s_t, 2)
                nc.scalar.activation(val9[:, :].rearrange("r (b c) -> r b c", b=NB), wide, ACT.Copy).then_inc(s_ev2, 1)
                high(1)
                high_w1(0)
                high(2)
                high_w12(0)
                high_w1(1)
                high_w12(1)
                high_w1(2)
                act.wait_ge(s_d, 1)
                nc.scalar.activation(run[0:H, :], top[0:H, :], ACT.Exp).then_inc(s_e, 1)
                high_w12(2)
                high_w1(3)
                high_w12(3)

            @block.vector
            def _(dve):
                def low_w1(m):
                    dve.wait_ge(s_w1h, m + 1)
                    nc.vector.tensor_tensor(w1t[1][:, :, :], one[:, :].rearrange("p (k c) -> p k c", k=KC),
                                            w1t[0][:, :, :].bitcast(F32), ALU.subtract).then_inc(s_w1l, 1)

                def low_w12(m):
                    dve.wait_ge(s_w12h, m + 1)
                    nc.vector.tensor_tensor(attn_w[1][:, m, :], two[:, :], attn_w[0][:, m, :].bitcast(F32), ALU.subtract).then_inc(s_w12l, 1)

                dve.wait_ge(s_pos, 3)
                dve.wait_ge(s_in, MOVED)
                nc.vector.tensor_copy(place_f[:, :], place_i[:, PLACE, :]).then_inc(s_f9, 1)
                nc.vector.tensor_copy(field9[:, :, 0:H], near[:, :, 0:H]).then_inc(s_f9, 1)
                dve.wait_ge(s_f9, 1)
                nc.vector.tensor_copy(field9[:, :, H], place_f[:, :]).then_inc(s_f9, 1)
                dve.wait_ge(s_t, 1)
                nc.vector.tensor_copy(key9[:, :].rearrange("r (b c) -> r b c", b=NB), wide).then_inc(s_ev, 1)
                nc.vector.memset(same[:, 0:1], 0.0)
                nc.vector.memset(same[:, E:E + 1], 0.0)
                dve.wait_ge(s_ev, 1)
                nc.vector.tensor_tensor(same[:, 1:E], key9[:, 1:E], key9[:, 0:E - 1], ALU.is_equal).then_inc(s_same, 1)
                dve.wait_ge(s_same, 1)
                nc.vector.tensor_scalar(gap[:, :], same[:, :], 1.0, -GAP, ALU.subtract, ALU.mult).then_inc(s_gap, 1)
                dve.wait_ge(s_ev2, 1)
                dve.wait_ge(s_gap, 1)
                nc.vector.tensor_tensor_scan(run[:, :], gap[:, 0:E], val9[:, :], 0.0, ALU.add, ALU.max).then_inc(s_run, 1)
                dve.wait_ge(s_bias, 48)
                dve.wait_ge(s_cmm, 1)
                nc.vector.tensor_tensor(half_c[:, :], two[0:T, :], half_c[:, :], ALU.add).then_inc(s_cev, 1)
                dve.wait_ge(s_cev, 1)
                nc.vector.tensor_scalar(half_c[:, :], half_c[:, :], 0.5, None, ALU.mult)
                nc.vector.tensor_scalar(neigh_b[:, D:2 * D], neigh_b[:, D:2 * D], 1.0 / 3.0, None, ALU.mult)
                low_w1(0)
                dve.wait_ge(s_run, 1)
                nc.vector.tensor_tensor_scan(top[:, ::-1], gap[:, E:0:-1], run[:, ::-1], 0.0, ALU.add, ALU.max).then_inc(s_top, 1)
                low_w12(0)
                low_w1(1)
                dve.wait_ge(s_back, 1)
                nc.vector.tensor_copy(ends[:, :], three[0:T, 0:ET * R].rearrange("p (t r) -> p t r", r=R)[:, :, H]).then_inc(s_end, 1)
                nc.vector.tensor_tensor(top[0:H, :], val9[0:H, :], top[0:H, :], ALU.subtract).then_inc(s_d, 1)
                low_w12(1)
                low_w1(2)
                dve.wait_ge(s_e, 1)
                nc.vector.tensor_tensor_scan(key9[0:H, :], same[0:H, 0:E], run[0:H, :], 0.0, ALU.mult, ALU.add).then_inc(s_sum, 1)
                low_w12(2)
                low_w1(3)
                dve.wait_ge(s_end, 1)
                nc.vector.tensor_tensor(place_f[:, :], place_f[:, :], ends[:, :], ALU.not_equal).then_inc(s_end, 1)
                dve.wait_ge(s_end, 2)
                nc.vector.scalar_tensor_tensor(place_i[:, SLOT, :], place_f[:, :], float(FAR), near[:, :, SRC - WS], ALU.mult, ALU.add)
                nc.vector.tensor_copy(place_i[:, RB, :], near[:, :, RANKB - WS])
                nc.vector.tensor_copy(place_i[:, SRCI, :], near[:, :, SRC - WS])
                nc.vector.tensor_copy(by_dst_s[:, :, 0:2], near[:, :, DST - WS:EW - WS + 1])
                nc.vector.tensor_copy(by_dst_s[:, :, 2], ends[:, :])
                nc.vector.tensor_copy(by_dst_s[:, :, 3], ends[:, :])
                nc.vector.tensor_scalar(prev_key[:, 1:ET + 1], near[:, :, SRC - WS], 1.0, last_row[:, 0:1], ALU.add, ALU.mult).then_inc(s_c, 1)
                nc.vector.memset(prev_key[:, 0:1], 0.0).then_inc(s_c, 1)
                dve.wait_ge(s_c, 2)
                nc.vector.tensor_scalar(prev_key[:, :], prev_key[:, :], 1.0, None, ALU.subtract)
                dve.wait_ge(s_back, 2)
                nc.vector.tensor_copy(e_col[:, :, :], three[0:T, 0:ET * H].rearrange("p (t h) -> p t h", h=H)).then_inc(s_got, 1)
                nc.vector.tensor_scalar(rec_den[:, :, :], three[0:T, ET * H:2 * ET * H].rearrange("p (t h) -> p t h", h=H),
                                        1e-16, None, ALU.add).then_inc(s_got, 1)
                dve.wait_ge(s_got, 2)
                nc.vector.reciprocal(rec_den[:, :, :], rec_den[:, :, :])
                low_w12(3)

            @block.tensor
            def _(pe):
                def wide_at(t):
                    return banks[0:R, t // QT, (t % QT) * T:(t % QT + 1) * T]

                pe.wait_ge(s_in, MOVED)
                for t in range(ET):
                    last = nc.tensor.transpose(wide_at(t), near[:, t, SRC - WS:SRC - WS + 1].to_broadcast([T, R]), ident[0:T, 0:T])
                last.then_inc(s_t, 1)
                pe.wait_ge(s_f9, 3)
                pe.wait_ge(s_ev, 1)
                for t in range(ET):
                    last = nc.tensor.transpose(wide_at(t), field9[:, t, :], ident[0:T, 0:T])
                last.then_inc(s_t, 1)
                pe.wait_ge(s_small, 16)
                pe.wait_ge(s_w_in[0], 16)
                for k in range(KC):
                    last = nc.tensor.matmul(two[0:T, :], b1_col[:, k:k + 1].to_broadcast([P, T]), stage[0][:, k, :],
                                            start=(k == 0), stop=(k == KC - 1))
                last.then_inc(s_cmm, 1)
                def turn_w1(m):
                    if m:
                        pe.wait_ge(s_w1l, m)
                    else:
                        pe.wait_ge(s_w1_in, 16)
                    for k in range(KC):
                        last = nc.tensor.transpose(one[:, P * k:P * (k + 1)], w1_rows[:, m, P * k:P * (k + 1)], ident[:, :])
                    last.then_inc(s_w1t, 1)

                def product_w12(m):
                    pe.wait_ge(s_w1l, m + 1)
                    if m:
                        pe.wait_ge(s_w12l, m)
                    else:
                        pe.wait_ge(s_cev, 1)
                        pe.wait_ge(s_lo, 1)
                    n = 0
                    for k in range(KC):
                        for a, b in ((0, 0), (0, 1), (1, 0)):
                            last = nc.tensor.matmul(two[:, :], w1t[a][:, k, :], w2_parts[b][:, k, :], start=(n == 0), stop=(n == 3 * KC - 1))
                            n += 1
                    last.then_inc(s_w12, 1)

                turn_w1(0)
                product_w12(0)
                turn_w1(1)
                pe.wait_ge(s_top, 1)
                for t in range(ET):
                    last = nc.tensor.transpose(three[0:T, t * R:(t + 1) * R], top[:, t * T:(t + 1) * T], ident[0:R, 0:R])
                last.then_inc(s_back, 1)
                product_w12(1)
                turn_w1(2)
                product_w12(2)
                turn_w1(3)
                pe.wait_ge(s_end, 1)
                pe.wait_ge(s_sum, 1)
                for t in range(ET):
                    nc.tensor.transpose(three[0:T, t * H:(t + 1) * H], run[0:H, t * T:(t + 1) * T], ident[0:H, 0:H])
                    last = nc.tensor.transpose(three[0:T, (ET + t) * H:(ET + t + 1) * H], key9[0:H, t * T:(t + 1) * T], ident[0:H, 0:H])
                last.then_inc(s_back, 1)
                product_w12(3)

        end_part()
        dfield = whole.enter_context(nc.sbuf_tensor("dfield", [T, ET, 4], F32))
        dprev = whole.enter_context(nc.sbuf_tensor("dprev", [T, ET + 1], F32))
        dnext = whole.enter_context(nc.sbuf_tensor("dnext", [T, ET], F32))
        dplace = whole.enter_context(nc.sbuf_tensor("dplace", [T, 3, ET], I32))
        in_place = whole.enter_context(nc.sbuf_tensor("in_place", [T, ET], I32))
        hidden_parts = ExitStack()
        m_all = hidden_parts.enter_context(nc.sbuf_tensor("m_all", [T, ET, D], F32))
        with ExitStack() as ph:
            sb, ps = holder(ph)
            vrow = [sb(f"vrow{b}", [T, D]) for b in range(2)]
            xrow = [sb(f"xrow{b}", [T, D]) for b in range(2)]
            wvs = [sb(f"wvs{b}", [T, D]) for b in range(2)]
            wv_hi, wv_lo, total_hi, total_lo = ([sb(f"{n}{b}", [T, D], F32R) for b in range(2)]
                                                for n in ("wv_hi", "wv_lo", "total_hi", "total_lo"))
            match = [sb(f"match{b}", [T, 2, T], F32R) for b in range(2)]
            key_now = [sb(f"key_now{b}", [T, 1]) for b in range(2)]
            vals = [sb(f"vals{b}", [T, D]) for b in range(2)]
            hi_v, lo_v, hi_x, lo_x = ([sb(f"a_{n}{b}", [P, KC, P], F32R) for b in range(2)] for n in ("hi_v", "lo_v", "hi_x", "lo_x"))
            u = [sb(f"u{b}", [T, D]) for b in range(2)]
            y = [sb(f"y{b}", [T, D]) for b in range(2)]
            x1 = [sb(f"x1_{b}", [T, D]) for b in range(2)]
            z = [sb(f"z{b}", [T, D]) for b in range(2)]
            st, mv, rs = ([sb(f"a_{n}{b}", [T, s]) for b in range(2)] for n, s in (("st", 6), ("mv", 2), ("rs", 3)))
            pidx = [sb(f"pidx{b}", [T, 4], I32) for b in range(2)]
            brow = [sb(f"brow{b}", [T, 4]) for b in range(2)]
            didx = [sb(f"didx{b}", [T, 2], I32) for b in range(4)]
            later_w = sb("later_w", [P, KC, D])
            sidx = [sb(f"sidx{b}", [T, 2], I32) for b in range(4)]
            keys_ps = ps("a_keys")
            sum_ps = [ps(f"a_sum{b}") for b in range(2)]
            tp_v, tp_x, attn_ps, m_ps, z_ps = (ps(f"a_{n}") for n in ("tp_v", "tp_x", "attn_ps", "m_ps", "z_ps"))
            a_v, a_x, a_u_out, a_z_out = sems("a_v"), sems("a_x"), sems("a_u_out"), sems("a_z_out")
            a_slot, a_brow = sems("a_slot"), sems("a_brow")
            a_dslot, a_look = sems("a_dslot", 4), sems("a_look", 4)
            a_w, a_w_hi, a_w_lo, a_wh, a_wl, a_tot_lo = sem("a_w"), sem("a_w_hi"), sem("a_w_lo"), sem("a_wh"), sem("a_wl"), sem("a_tot_lo")
            a_field, a_prep, a_didx, a_sidx, a_got = sem("a_field"), sem("a_prep"), sem("a_didx"), sem("a_sidx"), sem("a_got")
            (a_now, a_key, a_m, a_wv, a_sum, a_tot, a_val, a_tv, a_hv, a_lv, a_attn, a_u, a_y, a_st, a_ag, a_dev, a_rec, a_off,
             a_x1, a_tx, a_hx, a_lx, a_mmm, a_mcp, a_zmm, a_zcp, a_idx, a_zero) = (
                sem(f"a_{n}") for n in ("now", "key", "m", "wv", "sum", "tot", "val", "tv", "hv", "lv", "attn", "u", "y", "st", "ag",
                                        "dev", "rec", "off", "x1", "tx", "hx", "lx", "mmm", "mcp", "zmm", "zcp", "idx", "zero"))
            UN = 4
            block = ph.enter_context(nc.Block())

            @block.sync
            def _(sp):
                def load_v(a):
                    b = a.buf()
                    if not a.early(2):
                        sp.wait_ge(a_wv, a.t - 1)
                    for rows in PARTS:
                        sp.dma_start(vrow[b][rows, :], by_src[bass.ds(a.t * T, T), 0:D][rows, :]).then_inc(a_v[b], 16)

                def load_x(a):
                    b = a.buf()
                    if not a.early(2):
                        sp.wait_ge(a_u, a.t - 1)
                    for rows in PARTS:
                        sp.dma_start(xrow[b][rows, :], x_by_src[bass.ds(a.t * T, T), :][rows, :]).then_inc(a_x[b], 16)

                def store_u(a):
                    b = a.buf()
                    sp.wait_ge(a_u, a.t + 1)
                    for rows in PARTS:
                        sp.dma_start(x_new[bass.ds(a.t * T, T), :][rows, :], u[b][rows, :]).then_inc(a_u_out[b], 16)

                def store_z(a):
                    b = a.buf()
                    sp.wait_ge(a_zcp, a.t + 1)
                    for rows in PARTS:
                        sp.dma_start(z_rows[bass.ds(a.t * T, T), :][rows, :], z[b][rows, :]).then_inc(a_z_out[b], 16)

                def step(a):
                    at(load_v, a.later(4))
                    at(store_z, a.later(-3))
                    at(load_x, a.later(1))
                    at(store_u, a.later(-1))
                tiles(sp, step, ET, UN, before=4, after=3)
                for b in range(2):
                    sp.wait_ge(a_u_out[b], MOVED * (ET // 2))
                    sp.wait_ge(a_z_out[b], MOVED * (ET // 2))

            @block.gpsimd
            def _(pool):
                bound = {"N": pool.to_reg(N - 1), "E": pool.to_reg(E - 1)}
                def step(a):
                    b, n = a.buf(), a.use()
                    if not a.early(2):
                        pool.wait_ge(a_slot[b], 16 * n)
                        pool.wait_ge(a_brow[b], 16 * n)
                    nc.gpsimd.tensor_copy(pidx[b][:, 0:3], place_i[:, 0:3, bass.ds(a.t, 1)].rearrange("p j o -> p (j o)"))
                    nc.gpsimd.tensor_copy(brow[b][:, :], by_dst_s[:, bass.ds(a.t, 1), :].rearrange("p o f -> p (o f)")).then_inc(a_idx, 1)
                    pool.wait_ge(a_idx, a.t + 1)
                    alone(pool)
                    pool.indirect_dma_start(by_dst, bass.IndirectOffsetOnAxis(ap=pidx[b][:, RB:RB + 1], axis=0), brow[b][:, :], None,
                                            bounds_check=bound["E"], oob_is_err=False).then_inc(a_brow[b], 16)
                    alone(pool)
                    pool.indirect_dma_start(slot_src, bass.IndirectOffsetOnAxis(ap=pidx[b][:, SLOT:SLOT + 1], axis=0),
                                            pidx[b][:, PLACE:PLACE + 1], None,
                                            bounds_check=bound["N"], oob_is_err=False).then_inc(a_slot[b], 16)
                tiles(pool, step, ET)
                for b in range(2):
                    pool.wait_ge(a_slot[b], 16 * (ET // 2))
                    pool.wait_ge(a_brow[b], 16 * (ET // 2))

                pool.dma_start(dfield[:, :, :], by_dst[0:E, :].rearrange("(t p) f -> p t f", p=T)).then_inc(a_field, 16)
                pool.dma_start(dnext[:, :], by_dst[1:E + 1, 0:1].rearrange("(t p) f -> p (t f)", p=T)).then_inc(a_field, 16)
                nc.gpsimd.memset(dprev[:, 0:1], 0.0)
                pool.wait_ge(a_field, 32)
                nc.gpsimd.tensor_tensor(dnext[:, :], dnext[:, :], dfield[:, :, 0], ALU.subtract).then_inc(a_prep, 1)
                nc.gpsimd.tensor_scalar(dprev[:, 1:ET + 1], dfield[:, :, 0], 1.0, last_row[:, 0:1], ALU.add, ALU.mult).then_inc(a_prep, 1)
                pool.wait_ge(a_prep, 2)
                nc.gpsimd.tensor_scalar(dnext[:, :], dnext[:, :], 0.0, float(FAR), ALU.is_equal, ALU.mult).then_inc(a_prep, 1)
                nc.gpsimd.tensor_scalar(dprev[:, :], dprev[:, :], 1.0, None, ALU.subtract)
                pool.wait_ge(a_prep, 3)
                nc.gpsimd.tensor_tensor(dnext[:, :], dnext[:, :], dfield[:, :, 0], ALU.add).then_inc(a_prep, 1)
                pool.wait_ge(a_prep, 4)
                nc.gpsimd.tensor_copy(dplace[:, 0, :], dnext[:, :])
                nc.gpsimd.tensor_copy(dplace[:, 1, :], place_i[:, PLACE, :])
                nc.gpsimd.tensor_copy(dplace[:, 2, :], dfield[:, :, 2]).then_inc(a_prep, 1)
                pool.wait_ge(a_prep, 5)

                def send_slot(a):
                    b4, n = a.buf(4), a.use(4)
                    if not a.early(4):
                        pool.wait_ge(a_dslot[b4], 16 * n)
                    nc.gpsimd.tensor_copy(didx[b4][:, :], dplace[:, 0:2, bass.ds(a.t, 1)].rearrange("p j o -> p (j o)")).then_inc(a_didx, 1)
                    pool.wait_ge(a_didx, a.t + 1)
                    alone(pool)
                    pool.indirect_dma_start(slot_dst, bass.IndirectOffsetOnAxis(ap=didx[b4][:, 0:1], axis=0), didx[b4][:, 1:2], None,
                                            bounds_check=bound["N"], oob_is_err=False).then_inc(a_dslot[b4], 16)
                tiles(pool, send_slot, ET, UN)
                for b4 in range(4):
                    pool.wait_ge(a_dslot[b4], 16 * (ET // 4))

                def look(a):
                    b4 = a.buf(4)
                    if not a.early(4):
                        pool.wait_ge(a_got, a.t - 3)
                    nc.gpsimd.tensor_copy(sidx[b4][:, 0:1], place_i[:, SRCI, bass.ds(a.t, 1)]).then_inc(a_sidx, 1)
                    pool.wait_ge(a_sidx, a.t + 1)
                    alone(pool)
                    pool.indirect_dma_start(sidx[b4][:, 1:2], None, slot_dst, bass.IndirectOffsetOnAxis(ap=sidx[b4][:, 0:1], axis=0),
                                            bounds_check=bound["N"], oob_is_err=False).then_inc(a_look[b4], 16)

                def keep(a):
                    b4, n = a.buf(4), a.use(4)
                    pool.wait_ge(a_look[b4], 16 * n + 16)
                    nc.gpsimd.tensor_copy(in_place[:, bass.ds(a.t, 1)], sidx[b4][:, 1:2]).then_inc(a_got, 1)

                def look_and_keep(a):
                    at(look, a)
                    at(keep, a.later(-3))
                tiles(pool, look_and_keep, ET, UN, after=3)

                for i, (rows, w) in enumerate(((w12g, conv2_w), (w02, dense2_w))):
                    if i:
                        pool.wait_ge(a_w_lo, i)
                    pool.dma_start(later_w[:, :, :], weight_rows(rows)).then_inc(a_w, 16)
                    pool.wait_ge(a_w, 16 * i + 16)
                    nc.gpsimd.tensor_copy(w[0][:, :, :], later_w[:, :, :]).then_inc(a_w_hi, 1)
                    pool.wait_ge(a_w_hi, i + 1)
                    nc.gpsimd.tensor_tensor(w[1][:, :, :], later_w[:, :, :], w[0][:, :, :].bitcast(F32), ALU.subtract).then_inc(a_w_lo, 1)

            @block.scalar
            def _(act):
                def now(a):
                    if not a.early(2):
                        act.wait_ge(a_key, a.t - 1)
                    nc.scalar.copy(key_now[a.buf()][:, :], near[:, bass.ds(a.t, 1), SRC - WS:SRC - WS + 1].rearrange("p o f -> p (o f)"))\
                        .then_inc(a_now, 1)

                def keep_total(a):
                    b = a.buf()
                    act.wait_ge(a_sum, a.t + 1)
                    nc.scalar.activation(total_hi[b][:, :], sum_ps[b][0:T, :], ACT.Copy).then_inc(a_tot, 1)

                def high_wv(a):
                    b = a.buf()
                    act.wait_ge(a_wv, a.t + 1)
                    nc.scalar.activation(wv_hi[b][:, :], wvs[b][:, :], ACT.Copy).then_inc(a_wh, 1)

                def high_v(a):
                    b = a.buf()
                    act.wait_ge(a_tv, a.t + 1)
                    if not a.early(2):
                        act.wait_ge(a_attn, a.t - 1)
                    nc.scalar.activation(hi_v[b][:, :, 0:T], chunks(tp_v[:, :]), ACT.Copy).then_inc(a_hv, 1)

                def deviation(a):
                    b = a.buf()
                    act.wait_ge(a_ag, a.t + 1)
                    if not a.early(2):
                        act.wait_ge(a_rec, a.t - 1)
                    nc.scalar.activation(rs[b][:, 0:1], mv[b][:, 1:2], ACT.Sqrt, bias=eps[0:T, 1:2]).then_inc(a_dev, 1)

                def norm(a):
                    b = a.buf()
                    act.wait_ge(a_off, a.t + 1)
                    if not a.early(2):
                        act.wait_ge(a_tx, a.t - 1)
                    nc.scalar.activation(x1[b][:, :], y[b][:, :], ACT.Identity, scale=rs[b][:, 1:2], bias=rs[b][:, 2:3]).then_inc(a_x1, 1)

                def high_x(a):
                    b = a.buf()
                    act.wait_ge(a_tx, a.t + 1)
                    if not a.early(2):
                        act.wait_ge(a_zmm, a.t - 1)
                    nc.scalar.activation(hi_x[b][:, :, 0:T], chunks(tp_x[:, :]), ACT.Copy).then_inc(a_hx, 1)

                def keep_m(a):
                    act.wait_ge(a_mmm, a.t + 1)
                    nc.scalar.activation(m_all[:, bass.ds(a.t, 1), :].rearrange("p o d -> p (o d)"), m_ps[0:T, :], ACT.Copy,
                                         scale=near[:, bass.ds(a.t, 1), DIAG - WS:DIAG - WS + 1].rearrange("p o f -> p (o f)"))\
                        .then_inc(a_mcp, 1)

                def keep_z(a):
                    b = a.buf()
                    act.wait_ge(a_zmm, a.t + 1)
                    if not a.early(2):
                        act.wait_ge(a_z_out[b], MOVED * a.use())
                    nc.scalar.activation(z[b][:, :], z_ps[0:T, :], ACT.Copy).then_inc(a_zcp, 1)

                def step(a):
                    at(high_x, a.later(-1))
                    at(keep_z, a.later(-2))
                    at(now, a.later(4))
                    at(keep_total, a.later(2))
                    at(high_wv, a.later(3))
                    at(high_v, a.later(1))
                    at(deviation, a)
                    at(norm, a)
                    at(keep_m, a.later(-1))
                tiles(act, step, ET, UN, before=4, after=2)

            @block.vector
            def _(dve):
                nc.vector.memset(total_hi[1][:, :].bitcast(F32), 0.0)
                nc.vector.memset(total_lo[1][:, :].bitcast(F32), 0.0).then_inc(a_zero, 1)

                def prepare(a):
                    b, n = a.buf(), a.use()
                    dve.wait_ge(a_key, a.t + 1)
                    if not a.early(2):
                        dve.wait_ge(a_sum, a.t - 1)
                    keys = keys_ps[0:T, 0:T]
                    nc.vector.tensor_scalar(match[b][:, 0, :], keys,
                                            near[:, bass.ds(a.t, 1), SRC - WS:SRC - WS + 1].rearrange("p o f -> p (o f)"), None, ALU.is_equal)
                    nc.vector.tensor_scalar(match[b][:, 1, :], keys, prev_key[:, bass.ds(a.t, 1)], None, ALU.is_equal).then_inc(a_m, 1)
                    dve.wait_ge(a_v[b], MOVED * n + MOVED)
                    nc.vector.tensor_tensor(wvs[b][:, :].rearrange("p (h d) -> p h d", h=H), vrow[b][:, :].rearrange("p (h d) -> p h d", h=H),
                                            e_col[:, bass.ds(a.t, 1), :].rearrange("p o h -> p h o").to_broadcast([T, H, HD]),
                                            ALU.mult).then_inc(a_wv, 1)

                def low_wv(a):
                    b = a.buf()
                    dve.wait_ge(a_wh, a.t + 1)
                    nc.vector.tensor_tensor(wv_lo[b][:, :], wvs[b][:, :], wv_hi[b][:, :].bitcast(F32), ALU.subtract).then_inc(a_wl, 1)

                def low_total(a):
                    b = a.buf()
                    dve.wait_ge(a_tot, a.t + 1)
                    nc.vector.tensor_tensor(total_lo[b][:, :], sum_ps[b][0:T, :], total_hi[b][:, :].bitcast(F32), ALU.subtract)\
                        .then_inc(a_tot_lo, 1)

                def values(a):
                    b = a.buf()
                    if not a.early(2):
                        dve.wait_ge(a_tv, a.t - 1)
                    nc.vector.tensor_tensor(vals[b][:, :].rearrange("p (h d) -> p h d", h=H), sum_ps[b][0:T, :].rearrange("p (h d) -> p h d", h=H),
                                            rec_den[:, bass.ds(a.t, 1), :].rearrange("p o h -> p h o").to_broadcast([T, H, HD]),
                                            ALU.mult).then_inc(a_val, 1)

                def low_v(a):
                    b = a.buf()
                    dve.wait_ge(a_hv, a.t + 1)
                    nc.vector.tensor_tensor(lo_v[b][:, :, 0:T], chunks(tp_v[:, :]), hi_v[b][:, :, 0:T].bitcast(F32), ALU.subtract)\
                        .then_inc(a_lv, 1)

                def add(a):
                    b, n = a.buf(), a.use()
                    dve.wait_ge(a_attn, a.t + 1)
                    dve.wait_ge(a_x[b], MOVED * n + MOVED)
                    if not a.early(2):
                        dve.wait_ge(a_u_out[b], MOVED * n)
                        dve.wait_ge(a_x1, a.t - 1)
                    nc.vector.scalar_tensor_tensor(u[b][:, :], attn_ps[0:T, :], 0.5, xrow[b][:, :], ALU.mult, ALU.add).then_inc(a_u, 1)
                    dve.wait_ge(a_u, a.t + 1)
                    nc.vector.tensor_tensor(y[b][:, :], u[b][:, :], half_c[:, :], ALU.add).then_inc(a_y, 1)
                    dve.wait_ge(a_y, a.t + 1)
                    nc.vector.bn_stats(st[b][:, :], y[b][:, :]).then_inc(a_st, 1)
                    dve.wait_ge(a_st, a.t + 1)
                    alone(dve)
                    nc.vector.bn_aggr(mv[b][:, :], st[b][:, :]).then_inc(a_ag, 1)

                def scale(a):
                    b = a.buf()
                    dve.wait_ge(a_dev, a.t + 1)
                    nc.vector.reciprocal(rs[b][:, 1:2], rs[b][:, 0:1]).then_inc(a_rec, 1)
                    dve.wait_ge(a_rec, a.t + 1)
                    nc.vector.tensor_scalar(rs[b][:, 2:3], mv[b][:, 0:1], rs[b][:, 1:2], -1.0, ALU.mult, ALU.mult).then_inc(a_off, 1)

                def low_x(a):
                    b = a.buf()
                    dve.wait_ge(a_hx, a.t + 1)
                    nc.vector.tensor_tensor(lo_x[b][:, :, 0:T], chunks(tp_x[:, :]), hi_x[b][:, :, 0:T].bitcast(F32), ALU.subtract)\
                        .then_inc(a_lx, 1)

                def step(a):
                    at(low_x, a.later(-1))
                    at(values, a.later(1))
                    at(prepare, a.later(3))
                    at(low_total, a.later(2))
                    at(add, a)
                    at(low_v, a.later(1))
                    at(low_wv, a.later(3))
                    at(scale, a)
                tiles(dve, step, ET, UN, before=3, after=1)

            @block.tensor
            def _(pe):
                def keys(a):
                    b = a.buf()
                    if not a.early(1):
                        pe.wait_ge(a_m, a.t)
                    pe.wait_ge(a_now, a.t + 1)
                    nc.tensor.transpose(keys_ps[0:T, 0:T], key_now[b][:, :].to_broadcast([T, T]), ident[0:T, 0:T])\
                        .then_inc(a_key, 1)

                def sums_of(a):
                    b = a.buf()
                    pe.wait_ge(a_m, a.t + 1)
                    pe.wait_ge(a_wl, a.t + 1)
                    if not a.early(2):
                        pe.wait_ge(a_val, a.t - 1)
                    nc.tensor.matmul(sum_ps[b][0:T, :], match[b][:, 0, :], wv_hi[b][:, :], start=True, stop=False)
                    nc.tensor.matmul(sum_ps[b][0:T, :], match[b][:, 0, :], wv_lo[b][:, :], start=False, stop=False)
                    if a.early(1):
                        pe.wait_ge(a_zero, 1)
                    else:
                        pe.wait_ge(a_tot_lo, a.t)
                    nc.tensor.matmul(sum_ps[b][0:T, :], match[b][:, 1, :], total_hi[1 - b][:, :], start=False, stop=False)
                    nc.tensor.matmul(sum_ps[b][0:T, :], match[b][:, 1, :], total_lo[1 - b][:, :], start=False, stop=True).then_inc(a_sum, 1)

                def attend(a):
                    b = a.buf()
                    pe.wait_ge(a_lv, a.t + 1)
                    if not a.early(1):
                        pe.wait_ge(a_u, a.t)
                    product(attn_ps, hi_v[b], lo_v[b], attn_w).then_inc(a_attn, 1)

                def turn_v(a):
                    b = a.buf()
                    pe.wait_ge(a_val, a.t + 1)
                    if not a.early(1):
                        pe.wait_ge(a_lv, a.t)
                    transpose_tile(tp_v, vals[b], ident).then_inc(a_tv, 1)

                def turn_x(a):
                    b = a.buf()
                    pe.wait_ge(a_x1, a.t + 1)
                    if not a.early(1):
                        pe.wait_ge(a_lx, a.t)
                    transpose_tile(tp_x, x1[b], ident).then_inc(a_tx, 1)

                def convolve_rows(a):
                    b = a.buf()
                    pe.wait_ge(a_lx, a.t + 1)
                    if not a.early(1):
                        pe.wait_ge(a_mcp, a.t)
                    product(m_ps, hi_x[b], lo_x[b], dense1_w).then_inc(a_mmm, 1)
                    if not a.early(1):
                        pe.wait_ge(a_zcp, a.t)
                    product(z_ps, hi_x[b], lo_x[b], conv1_w).then_inc(a_zmm, 1)

                def step(a):
                    at(keys, a.later(3))
                    at(sums_of, a.later(2))
                    at(attend, a)
                    at(turn_v, a.later(1))
                    at(convolve_rows, a.later(-1))
                    at(turn_x, a)
                tiles(pe, step, ET, UN, before=3, after=1)

        end_part()
        def sum_by_dst(first, nodes=None):
            c0 = 0 if first else D
            nm = "c1" if first else "c2"
            stores = 32 if first else 16
            with ExitStack() as ph:
                sb, ps = holder(ph)
                g = [sb(f"{nm}_g{b}", [T, D]) for b in range(4)]
                key_now = [sb(f"{nm}_key_now{b}", [T, 1]) for b in range(2)]
                match = [sb(f"{nm}_match{b}", [T, 2, T]) for b in range(4)]
                total = [sb(f"{nm}_total{b}", [T, D]) for b in range(2)]
                res = [sb(f"{nm}_res{b}", [T, D]) for b in range(4)]
                pidx = [sb(f"{nm}_idx{b}", [T, 1], I32) for b in range(4)]
                keys_ps = [ps(f"{nm}_keys{b}") for b in range(2)]
                sum_ps = [ps(f"{nm}_sum{b}") for b in range(4)]
                s_g, s_out = sems(f"{nm}_g", 4), sems(f"{nm}_out", 4)
                s_key, s_m, s_sum, s_tot, s_res, s_idx, s_zero, s_now = (
                    sem(f"{nm}_{n}") for n in ("key", "m", "sum", "tot", "res", "idx", "zero", "now"))
                UN = 4
                block = ph.enter_context(nc.Block())

                @block.sync
                def _(sp):
                    if nodes:
                        nodes[0](sp, 1)

                    def step(a):
                        b4 = a.buf(4)
                        sp.wait_ge(s_res, a.t + 1)
                        sp.dma_start(neigh[bass.ds(a.t * T, T), c0:c0 + D], res[b4][:, :]).then_inc(s_out[b4], 16)
                        if first:
                            sp.dma_start(neigh1[bass.ds(a.t * T, T), :], res[b4][:, :]).then_inc(s_out[b4], 16)
                    tiles(sp, step, ET, UN)
                    if nodes:
                        nodes[0](sp, 2)
                    for b4 in range(4):
                        sp.wait_ge(s_out[b4], stores * (ET // 4))

                @block.gpsimd
                def _(pool):
                    bound = {"N": pool.to_reg(N - 1), "E": pool.to_reg(E - 1)}
                    def step(a):
                        b4, n = a.buf(4), a.use(4)
                        if not a.early(4):
                            pool.wait_ge(s_sum, a.t - 3)
                            pool.wait_ge(s_g[b4], 16 * n)
                        nc.gpsimd.tensor_copy(pidx[b4][:, :], dplace[:, 2, bass.ds(a.t, 1)]).then_inc(s_idx, 1)
                        pool.wait_ge(s_idx, a.t + 1)
                        alone(pool)
                        pool.indirect_dma_start(g[b4][:, :], None, z_rows if first else z2_rows,
                                                bass.IndirectOffsetOnAxis(ap=pidx[b4][:, 0:1], axis=0),
                                                bounds_check=bound["E"], oob_is_err=False).then_inc(s_g[b4], 16)
                    steps_ahead(step, 0, 4, ET, UN)
                    if nodes:
                        nodes[1](pool, 1)
                    tiles(pool, step, ET, UN, skip=4)
                    if nodes:
                        nodes[1](pool, 2)

                @block.scalar
                def _(act):
                    def now(a):
                        if not a.early(2):
                            act.wait_ge(s_key, a.t - 1)
                        nc.scalar.copy(key_now[a.buf()][:, :], dfield[:, bass.ds(a.t, 1), 0:1].rearrange("p o f -> p (o f)")).then_inc(s_now, 1)

                    def keep_total(a):
                        b, b4 = a.buf(), a.buf(4)
                        act.wait_ge(s_sum, a.t + 1)
                        nc.scalar.activation(total[b][:, :], sum_ps[b4][0:T, :], ACT.Copy).then_inc(s_tot, 1)

                    def step(a):
                        at(keep_total, a)
                        at(now, a.later(4))
                    tiles(act, step, ET, UN, before=4)
                    if nodes:
                        nodes[2](act, 1)

                @block.vector
                def _(dve):
                    nc.vector.memset(total[1][:, :], 0.0).then_inc(s_zero, 1)

                    def prepare(a):
                        b, b4 = a.buf(), a.buf(4)
                        dve.wait_ge(s_key, a.t + 1)
                        if not a.early(4):
                            dve.wait_ge(s_sum, a.t - 3)
                        nc.vector.tensor_scalar(match[b4][:, 0, :], keys_ps[b][0:T, 0:T],
                                                dfield[:, bass.ds(a.t, 1), 0:1].rearrange("p o f -> p (o f)"),
                                                dfield[:, bass.ds(a.t, 1), 1:2].rearrange("p o f -> p (o f)"), ALU.is_equal, ALU.mult)
                        nc.vector.tensor_scalar(match[b4][:, 1, :], keys_ps[b][0:T, 0:T],
                                                dprev[:, bass.ds(a.t, 1)], None, ALU.is_equal).then_inc(s_m, 1)

                    def add_bias(a):
                        b4, n = a.buf(4), a.use(4)
                        dve.wait_ge(s_tot, a.t + 1)
                        if not a.early(4):
                            dve.wait_ge(s_out[b4], stores * n)
                        nc.vector.scalar_tensor_tensor(res[b4][:, :], sum_ps[b4][0:T, :], 1.0 if first else 1.0 / 3.0, neigh_b[:, c0:c0 + D],
                                                       ALU.mult, ALU.add).then_inc(s_res, 1)

                    def step(a):
                        at(prepare, a.later(3))
                        at(add_bias, a)
                    tiles(dve, step, ET, UN, before=3)
                    if nodes:
                        nodes[3](dve, 1)

                @block.tensor
                def _(pe):
                    def keys(a):
                        b = a.buf()
                        if not a.early(2):
                            pe.wait_ge(s_m, a.t - 1)
                        pe.wait_ge(s_now, a.t + 1)
                        nc.tensor.transpose(keys_ps[b][0:T, 0:T], key_now[b][:, :].to_broadcast([T, T]), ident[0:T, 0:T]).then_inc(s_key, 1)

                    def own_sums(a):
                        b4, n = a.buf(4), a.use(4)
                        pe.wait_ge(s_m, a.t + 1)
                        pe.wait_ge(s_g[b4], 16 * n + 16)
                        if not a.early(4):
                            pe.wait_ge(s_res, a.t - 3)
                        nc.tensor.matmul(sum_ps[b4][0:T, :], match[b4][:, 0, :], g[b4][:, :], start=True, stop=False)

                    def carried(a):
                        b, b4 = a.buf(), a.buf(4)
                        if a.early(1):
                            pe.wait_ge(s_zero, 1)
                        else:
                            pe.wait_ge(s_tot, a.t)
                        nc.tensor.matmul(sum_ps[b4][0:T, :], match[b4][:, 1, :], total[1 - b][:, :],
                                         start=False, stop=True).then_inc(s_sum, 1)

                    def step(a):
                        at(carried, a)
                        at(own_sums, a.later(2))
                        at(keys, a.later(4))
                    tiles(pe, step, ET, UN, before=4)
                    if nodes:
                        nodes[4](pe, 1)

        sum_by_dst(True)
        end_part()

        with ExitStack() as ph:
            sb, ps = holder(ph)
            hi = [sb(f"h_hi{b}", [P, KC, P], F32R) for b in range(2)]
            lo = [sb(f"h_lo{b}", [P, KC, P], F32R) for b in range(2)]
            nb = [sb(f"h_nb{b}", [T, D]) for b in range(4)]
            pre = [sb(f"h_pre{b}", [T, D]) for b in range(2)]
            z = [sb(f"h_z{b}", [T, D]) for b in range(2)]
            pidx = [sb(f"h_idx{b}", [T, 1], I32) for b in range(4)]
            tp = [ps(f"h_tp{b}") for b in range(2)]
            out_ps = [ps(f"h_out{b}") for b in range(2)]
            h_nb, h_store = sems("h_nb", 4), sems("h_store")
            h_idx, h_fill, h_t, h_hi, h_lo, h_mm, h_pre, h_z = (sem(f"h_{n}") for n in ("idx", "fill", "t", "hi", "lo", "mm", "pre", "z"))
            UN = 4
            block = ph.enter_context(nc.Block())

            @block.sync
            def _(sp):
                def step(a):
                    b = a.buf()
                    sp.wait_ge(h_z, a.t + 1)
                    for rows in PARTS:
                        sp.dma_start(z2_rows[bass.ds(a.t * T, T), :][rows, :], z[b][rows, :]).then_inc(h_store[b], 16)
                tiles(sp, step, ET)
                for b in range(2):
                    sp.wait_ge(h_store[b], MOVED * (ET // 2))

            @block.gpsimd
            def _(pool):
                bound = {"N": pool.to_reg(N - 1), "E": pool.to_reg(E - 1)}

                def fetch(a):
                    b4, n = a.buf(4), a.use(4)
                    if not a.early(4):
                        pool.wait_ge(h_nb[b4], 16 * n)
                    nc.gpsimd.tensor_copy(pidx[b4][:, :], in_place[:, bass.ds(a.t, 1)]).then_inc(h_idx, 1)
                    pool.wait_ge(h_idx, a.t + 1)
                    pool.wait_ge(h_fill, a.t + 1)
                    alone(pool)
                    pool.indirect_dma_start(nb[b4][:, :], None, neigh1, bass.IndirectOffsetOnAxis(ap=pidx[b4][:, 0:1], axis=0),
                                            bounds_check=bound["E"], oob_is_err=False).then_inc(h_nb[b4], 16)
                tiles(pool, fetch, ET, UN)

            @block.scalar
            def _(act):
                def fill(a):
                    b4 = a.buf(4)
                    if not a.early(4):
                        act.wait_ge(h_pre, a.t - 3)
                    nc.scalar.activation(nb[b4][:, :], neigh_b[:, 0:D], ACT.Copy).then_inc(h_fill, 1)

                def high(a):
                    b = a.buf()
                    act.wait_ge(h_t, a.t + 1)
                    if not a.early(2):
                        act.wait_ge(h_mm, a.t - 1)
                    nc.scalar.activation(hi[b][:, :, 0:T], chunks(tp[b][:, :]), ACT.Relu).then_inc(h_hi, 1)

                def keep(a):
                    b, n = a.buf(), a.use()
                    act.wait_ge(h_mm, a.t + 1)
                    if not a.early(2):
                        act.wait_ge(h_store[b], MOVED * n)
                    nc.scalar.activation(z[b][:, :], out_ps[b][0:T, :], ACT.Copy).then_inc(h_z, 1)

                def step(a):
                    at(fill, a.later(3))
                    at(high, a)
                    at(keep, a.later(-1))
                tiles(act, step, ET, UN, before=3, after=1)

            @block.vector
            def _(dve):
                def add(a):
                    b, b4, n = a.buf(), a.buf(4), a.use(4)
                    dve.wait_ge(h_nb[b4], 16 * n + 16)
                    if not a.early(2):
                        dve.wait_ge(h_t, a.t - 1)
                    nc.vector.tensor_tensor(pre[b][:, :], m_all[:, bass.ds(a.t, 1), :].rearrange("p o d -> p (o d)"), nb[b4][:, :], ALU.add)\
                        .then_inc(h_pre, 1)

                def low(a):
                    b = a.buf()
                    dve.wait_ge(h_hi, a.t + 1)
                    nc.vector.scalar_tensor_tensor(lo[b][:, :, 0:T], chunks(tp[b][:, :]), 0.0, hi[b][:, :, 0:T].bitcast(F32),
                                                   ALU.max, ALU.subtract).then_inc(h_lo, 1)

                def step(a):
                    at(add, a.later(1))
                    at(low, a)
                tiles(dve, step, ET, UN, before=1)

            @block.tensor
            def _(pe):
                def turn(a):
                    b = a.buf()
                    pe.wait_ge(h_pre, a.t + 1)
                    if not a.early(2):
                        pe.wait_ge(h_lo, a.t - 1)
                    transpose_tile(tp[b], pre[b], ident).then_inc(h_t, 1)

                def project(a):
                    b = a.buf()
                    pe.wait_ge(h_lo, a.t + 1)
                    if not a.early(2):
                        pe.wait_ge(h_z, a.t - 1)
                    product(out_ps[b], hi[b], lo[b], conv2_w).then_inc(h_mm, 1)

                def step(a):
                    at(turn, a)
                    at(project, a.later(-1))
                tiles(pe, step, ET, UN, after=1)

        end_part()
        hidden_parts.close()
        with ExitStack() as ph:
            sb, ps = holder(ph)
            slots = sb("slots", [T, 2, NT], I32)
            diag = sb("diag", [T, 2, NT])
            xb = [sb(f"xb{b}", [T, D]) for b in range(4)]
            nb = [sb(f"nb{b}", [T, 2 * D]) for b in range(4)]
            pidx = [sb(f"n_idx{b}", [T, 2], I32) for b in range(8)]
            y = [sb(f"n_y{b}", [T, D]) for b in range(2)]
            x1 = [sb(f"n_x1_{b}", [T, D]) for b in range(8)]
            st, mv, rs = ([[sb(f"n_{n}{j}_{b}", [T, s]) for b in range(2)] for j in range(2)]
                          for n, s in (("st", 6), ("mv", 2), ("rs", 3)))
            hi1, lo1, hi2, lo2 = ([sb(f"n_{n}_{b}", [P, KC, P], F32R) for b in range(2)] for n in ("hi1", "lo1", "hi2", "lo2"))
            h1 = [sb(f"n_h1_{b}", [T, D]) for b in range(2)]
            h2 = [sb(f"n_h2_{b}", [T, D]) for b in range(2)]
            s2 = [sb(f"n_s{b}", [T, D]) for b in range(2)]
            res = [sb(f"n_res{b}", [T, D]) for b in range(2)]
            tp1 = [ps(f"n_tp1_{b}") for b in range(2)]
            n_in, n_u, n_nb = sems("n_in", 4), sems("n_u", 4), sems("n_nb", 4)
            n_store = sems("n_store")
            n_small, n_third, n_fill, n_idx = sem("n_small"), sem("n_third"), sem("n_fill"), sem("n_idx")
            (n_y, n_st1, n_ag1, n_dev1, n_rec1, n_off1, n_x1, n_t1, n_hi1, n_lo1, n_mm1, n_h1, n_t2, n_hi2, n_lo2, n_mm2,
             n_h2, n_s, n_st2, n_ag2, n_dev2, n_rec2, n_off2, n_res) = (
                sem(f"n_{n}") for n in ("y", "st1", "ag1", "dev1", "rec1", "off1", "x1", "t1", "hi1", "lo1", "mm1", "h1", "t2", "hi2",
                                        "lo2", "mm2", "h2", "s", "st2", "ag2", "dev2", "rec2", "off2", "res"))
            part_sems.clear()
            UN = 8

            def tile_rows(table, a):
                return table.rearrange("(p t) d -> p t d", p=T)[:, bass.ds(a.t, 1), :].rearrange("p o d -> p (o d)")

            def nodes_sync(sp, ahead):
                def load(a):
                    b4 = a.buf(4)
                    if not a.early(4):
                        sp.wait_ge(n_y, a.t - 3)
                    for rows in PARTS:
                        sp.dma_start(xb[b4][rows, :], tile_rows(x, a)[rows, :]).then_inc(n_in[b4], 16)

                def store(a):
                    b = a.buf()
                    sp.wait_ge(n_res, a.t + 1)
                    for rows in PARTS:
                        sp.dma_start(tile_rows(out, a)[rows, :], res[b][rows, :]).then_inc(n_store[b], 16)

                def step(a):
                    at(load, a.later(6))
                    at(store, a.later(-3))
                if ahead == 1:
                    sp.dma_start(slots[:, 0, :], slot_src.rearrange("(p t) o -> p (t o)", p=T)).then_inc(n_small, 16)
                    sp.dma_start(slots[:, 1, :], slot_dst.rearrange("(p t) o -> p (t o)", p=T)).then_inc(n_small, 16)
                    sp.dma_start(diag[:, 0, :], node_vec.rearrange("(p t) -> p t", p=T)).then_inc(n_small, 16)
                    steps_ahead(step, -6, -2, NT, UN)
                    return
                if ahead == 2:
                    steps_ahead(step, -2, 0, NT, UN)
                    return
                tiles(sp, step, NT, UN, after=3)
                for b in range(2):
                    sp.wait_ge(n_store[b], MOVED * (NT // 2))

            def nodes_gpsimd(pool, ahead):
                bound = {"N": pool.to_reg(N - 1), "E": pool.to_reg(E - 1)}
                if ahead == 1:
                    pool.wait_ge(n_small, 48)

                def fetch_x(a):
                    n, b4, b8 = a.use(4), a.buf(4), a.buf(8)
                    if not a.early(8):
                        pool.wait_ge(n_u[b4], 16 * n - 16)
                        pool.wait_ge(n_nb[b4], 16 * n - 16)
                    nc.gpsimd.tensor_copy(pidx[b8][:, :], slots[:, :, bass.ds(a.t, 1)].rearrange("p j o -> p (j o)")).then_inc(n_idx, 1)
                    pool.wait_ge(n_idx, a.t + 1)
                    pool.wait_ge(n_in[b4], MOVED * n + MOVED)
                    alone(pool)
                    pool.indirect_dma_start(xb[b4][:, :], None, x_new, bass.IndirectOffsetOnAxis(ap=pidx[b8][:, 0:1], axis=0),
                                            bounds_check=bound["E"], oob_is_err=False).then_inc(n_u[b4], 16)

                def fetch_nb(a):
                    b4, b8 = a.buf(4), a.buf(8)
                    pool.wait_ge(n_fill, a.t + 1)
                    alone(pool)
                    pool.indirect_dma_start(nb[b4][:, :], None, neigh, bass.IndirectOffsetOnAxis(ap=pidx[b8][:, 1:2], axis=0),
                                            bounds_check=bound["E"], oob_is_err=False).then_inc(n_nb[b4], 16)

                def add(a):
                    b, n, b4 = a.buf(), a.use(4), a.buf(4)
                    pool.wait_ge(n_u[b4], 16 * n + 16)
                    if not a.early(2):
                        pool.wait_ge(n_x1, a.t - 1)
                    nc.gpsimd.tensor_tensor(y[b][:, :], xb[b4][:, :], half_c[:, :], ALU.add).then_inc(n_y, 1)

                def step(a):
                    at(fetch_x, a.later(5))
                    at(add, a.later(4))
                    at(fetch_nb, a.later(1))
                if ahead == 1:
                    steps_ahead(step, -5, -3, NT, UN)
                    return
                if ahead == 2:
                    steps_ahead(step, -3, -1, NT, UN)
                    return
                tiles(pool, step, NT, UN, before=1)

            def nodes_scalar(act, ahead):
                def dev1(a):
                    b = a.buf()
                    act.wait_ge(n_ag1, a.t + 1)
                    if not a.early(2):
                        act.wait_ge(n_rec1, a.t - 1)
                    nc.scalar.activation(rs[0][b][:, 0:1], mv[0][b][:, 1:2], ACT.Sqrt, bias=eps[0:T, 1:2]).then_inc(n_dev1, 1)

                def norm1(a):
                    b, b8 = a.buf(), a.buf(8)
                    act.wait_ge(n_off1, a.t + 1)
                    if not a.early(8):
                        act.wait_ge(n_s, a.t - 7)
                    nc.scalar.activation(x1[b8][:, :], y[b][:, :], ACT.Identity, scale=rs[0][b][:, 1:2], bias=rs[0][b][:, 2:3])\
                        .then_inc(n_x1, 1)

                def fill(a):
                    b4 = a.buf(4)
                    if not a.early(4):
                        act.wait_ge(n_h2, a.t - 3)
                    nc.scalar.activation(nb[b4][:, :], neigh_b[:, :], ACT.Copy).then_inc(n_fill, 1)

                def high1(a):
                    b = a.buf()
                    act.wait_ge(n_t1, a.t + 1)
                    if not a.early(2):
                        act.wait_ge(n_mm1, a.t - 1)
                    nc.scalar.activation(hi1[b][:, :, 0:T], chunks(tp1[b][:, :]), ACT.Copy).then_inc(n_hi1, 1)

                def high2(a):
                    b = a.buf()
                    act.wait_ge(n_t2, a.t + 1)
                    if not a.early(2):
                        act.wait_ge(n_mm2, a.t - 1)
                    nc.scalar.activation(hi2[b][:, :, 0:T], chunks(tp2[b][:, :]), ACT.Relu).then_inc(n_hi2, 1)

                def dev2(a):
                    b = a.buf()
                    act.wait_ge(n_ag2, a.t + 1)
                    if not a.early(2):
                        act.wait_ge(n_rec2, a.t - 1)
                    nc.scalar.activation(rs[1][b][:, 0:1], mv[1][b][:, 1:2], ACT.Sqrt, bias=eps[0:T, 2:3]).then_inc(n_dev2, 1)

                def finish(a):
                    b, n = a.buf(), a.use()
                    act.wait_ge(n_off2, a.t + 1)
                    if not a.early(2):
                        act.wait_ge(n_store[b], MOVED * n)
                    nc.scalar.activation(res[b][:, :], s2[b][:, :], ACT.Identity, scale=rs[1][b][:, 1:2], bias=rs[1][b][:, 2:3])\
                        .then_inc(n_res, 1)

                def step(a):
                    at(fill, a.later(1))
                    at(dev1, a.later(3))
                    at(dev2, a.later(-3))
                    at(high1, a.later(2))
                    at(high2, a.later(-1))
                    at(norm1, a.later(3))
                    at(finish, a.later(-3))
                if ahead:
                    steps_ahead(step, -3, 0, NT, UN)
                    return
                tiles(act, step, NT, UN, after=3)

            def nodes_vector(dve, ahead):
                def stats1(a):
                    b = a.buf()
                    dve.wait_ge(n_y, a.t + 1)
                    nc.vector.bn_stats(st[0][b][:, :], y[b][:, :]).then_inc(n_st1, 1)

                def moments1(a):
                    b = a.buf()
                    dve.wait_ge(n_st1, a.t + 1)
                    alone(dve)
                    nc.vector.bn_aggr(mv[0][b][:, :], st[0][b][:, :]).then_inc(n_ag1, 1)

                def scale1(a):
                    b = a.buf()
                    dve.wait_ge(n_dev1, a.t + 1)
                    if not a.early(2):
                        dve.wait_ge(n_x1, a.t - 1)
                    nc.vector.reciprocal(rs[0][b][:, 1:2], rs[0][b][:, 0:1]).then_inc(n_rec1, 1)

                def offset1(a):
                    b = a.buf()
                    dve.wait_ge(n_rec1, a.t + 1)
                    nc.vector.tensor_scalar(rs[0][b][:, 2:3], mv[0][b][:, 0:1], rs[0][b][:, 1:2], -1.0, ALU.mult, ALU.mult)\
                        .then_inc(n_off1, 1)

                def low1(a):
                    b = a.buf()
                    dve.wait_ge(n_hi1, a.t + 1)
                    nc.vector.tensor_tensor(lo1[b][:, :, 0:T], chunks(tp1[b][:, :]), hi1[b][:, :, 0:T].bitcast(F32), ALU.subtract)\
                        .then_inc(n_lo1, 1)

                def hidden(a):
                    b, b4 = a.buf(), a.buf(4)
                    dve.wait_ge(n_mm1, a.t + 1)
                    dve.wait_ge(n_nb[b4], 16 * a.use(4) + 16)
                    if not a.early(2):
                        dve.wait_ge(n_t2, a.t - 1)
                    nc.vector.scalar_tensor_tensor(h1[b][:, :], mm1[b][0:T, :], diag[:, 0, bass.ds(a.t, 1)], nb[b4][:, 0:D],
                                                   ALU.mult, ALU.add).then_inc(n_h1, 1)

                def low2(a):
                    b = a.buf()
                    dve.wait_ge(n_hi2, a.t + 1)
                    nc.vector.scalar_tensor_tensor(lo2[b][:, :, 0:T], chunks(tp2[b][:, :]), 0.0, hi2[b][:, :, 0:T].bitcast(F32),
                                                   ALU.max, ALU.subtract).then_inc(n_lo2, 1)

                def hidden2(a):
                    b, b4 = a.buf(), a.buf(4)
                    dve.wait_ge(n_mm2, a.t + 1)
                    nc.vector.scalar_tensor_tensor(h2[b][:, :], mm2[b][0:T, :], diag[:, 1, bass.ds(a.t, 1)], nb[b4][:, D:2 * D],
                                                   ALU.mult, ALU.add).then_inc(n_h2, 1)

                def sum2(a):
                    b, b8 = a.buf(), a.buf(8)
                    dve.wait_ge(n_h2, a.t + 1)
                    if not a.early(2):
                        dve.wait_ge(n_res, a.t - 1)
                    nc.vector.scalar_tensor_tensor(s2[b][:, :], h2[b][:, :], 0.0, x1[b8][:, :], ALU.max, ALU.add).then_inc(n_s, 1)

                def stats2(a):
                    b = a.buf()
                    dve.wait_ge(n_s, a.t + 1)
                    nc.vector.bn_stats(st[1][b][:, :], s2[b][:, :]).then_inc(n_st2, 1)

                def moments2(a):
                    b = a.buf()
                    dve.wait_ge(n_st2, a.t + 1)
                    alone(dve)
                    nc.vector.bn_aggr(mv[1][b][:, :], st[1][b][:, :]).then_inc(n_ag2, 1)

                def scale2(a):
                    b = a.buf()
                    dve.wait_ge(n_dev2, a.t + 1)
                    if not a.early(2):
                        dve.wait_ge(n_res, a.t - 1)
                    nc.vector.reciprocal(rs[1][b][:, 1:2], rs[1][b][:, 0:1]).then_inc(n_rec2, 1)

                def offset2(a):
                    b = a.buf()
                    dve.wait_ge(n_rec2, a.t + 1)
                    nc.vector.tensor_scalar(rs[1][b][:, 2:3], mv[1][b][:, 0:1], rs[1][b][:, 1:2], -1.0, ALU.mult, ALU.mult)\
                        .then_inc(n_off2, 1)

                def step(a):
                    at(hidden2, a.later(-3))
                    at(stats1, a.later(3))
                    at(sum2, a.later(-3))
                    at(moments1, a.later(3))
                    at(stats2, a.later(-3))
                    at(hidden, a)
                    at(moments2, a.later(-3))
                    at(scale1, a.later(3))
                    at(low1, a.later(2))
                    at(offset1, a.later(3))
                    at(scale2, a.later(-3))
                    at(low2, a.later(-1))
                    at(offset2, a.later(-3))
                if ahead:
                    dve.wait_ge(n_small, 48)
                    nc.vector.tensor_scalar(diag[:, 1, :], diag[:, 0, :], 1.0 / 3.0, None, ALU.mult).then_inc(n_third, 1)
                    dve.wait_ge(n_third, 1)
                    steps_ahead(step, -3, 0, NT, UN)
                    return
                tiles(dve, step, NT, UN, after=3)

            def nodes_tensor(pe, ahead):
                def turn1(a):
                    b = a.buf()
                    pe.wait_ge(n_x1, a.t + 1)
                    if not a.early(2):
                        pe.wait_ge(n_lo1, a.t - 1)
                    transpose_tile(tp1[b], x1[a.buf(8)], ident).then_inc(n_t1, 1)

                def dense1(a):
                    b = a.buf()
                    pe.wait_ge(n_lo1, a.t + 1)
                    if not a.early(2):
                        pe.wait_ge(n_h1, a.t - 1)
                    product(mm1[b], hi1[b], lo1[b], dense1_w).then_inc(n_mm1, 1)

                def turn2(a):
                    b = a.buf()
                    pe.wait_ge(n_h1, a.t + 1)
                    if not a.early(2):
                        pe.wait_ge(n_lo2, a.t - 1)
                    transpose_tile(tp2[b], h1[b], ident).then_inc(n_t2, 1)

                def dense2(a):
                    b = a.buf()
                    pe.wait_ge(n_lo2, a.t + 1)
                    if not a.early(2):
                        pe.wait_ge(n_h2, a.t - 1)
                    product(mm2[b], hi2[b], lo2[b], dense2_w).then_inc(n_mm2, 1)

                def step(a):
                    at(dense1, a)
                    at(turn1, a.later(2))
                    at(turn2, a.later(-1))
                    at(dense2, a.later(-2))
                if ahead:
                    steps_ahead(step, -2, 0, NT, UN)
                    return
                tiles(pe, step, NT, UN, after=2)

            sum_by_dst(False, (nodes_sync, nodes_gpsimd, nodes_scalar, nodes_vector, nodes_tensor))
            end_part()
            tp2, mm1, mm2 = ([ps(f"n_{n}_{b}") for b in range(2)] for n in ("tp2", "mm1", "mm2"))
            block = ph.enter_context(nc.Block())

            @block.sync
            def _(sp):
                nodes_sync(sp, 0)

            @block.gpsimd
            def _(pool):
                nodes_gpsimd(pool, 0)

            @block.scalar
            def _(act):
                nodes_scalar(act, 0)

            @block.vector
            def _(dve):
                nodes_vector(dve, 0)

            @block.tensor
            def _(pe):
                nodes_tensor(pe, 0)


_INS = ['x', 'src', 'dst', 'edge_attr_8', 'edge_weight', 'node_vec',
        'L0_gnn_ln_g', 'L0_gnn_ln_b', 'L0_gnn_Wq', 'L0_gnn_bq', 'L0_gnn_Wk', 'L0_gnn_bk', 'L0_gnn_Wv', 'L0_gnn_bv',
        'L0_gnn_W1', 'L0_gnn_b1', 'L0_gnn_W2', 'L0_gnn_b2',
        'L1_gnn_W0_1', 'L1_gnn_W1_1', 'L1_gnn_b1', 'L1_gnn_W0_2', 'L1_gnn_W1_2', 'L1_gnn_b2']


def kernel(**inputs):
    import numpy as _np
    import concourse.bacc as _bacc
    from concourse import mybir as _mybir
    from concourse.bass_utils import run_bass_kernel_spmd as _run

    nc = _bacc.Bacc("TRN2", target_bir_lowering=False, num_devices=1)
    arrays, args = {}, []
    for name in _INS:
        a = _np.ascontiguousarray(inputs[name])
        arrays[f"in_{name}"] = a
        args.append(nc.dram_tensor(f"in_{name}", a.shape, _mybir.dt.from_np(a.dtype), kind="ExternalInput").ap())
    shape = inputs['x'].shape
    args.append(nc.dram_tensor("out_0", shape, _mybir.dt.float32, kind="ExternalOutput").ap())
    build(nc, *args)
    r = _run(nc, [arrays], core_ids=[0])
    return r.results[0]["out_0"]
```
